# Optimizing a Trainium2 kernel written in Bass

```python
import numpy as np
import jax
import jax.numpy as jnp

def _softmax(x, axis=-1):
    return jax.nn.softmax(x, axis=axis)

def _gelu(x):
    return jax.nn.gelu(x, approximate=True)

def _silu(x):
    return jax.nn.silu(x)

def _sigmoid(x):
    return jax.nn.sigmoid(x)

def _layernorm(x, axis=-1, eps=1e-05):
    m = jnp.mean(x, axis=axis, keepdims=True)
    v = jnp.var(x, axis=axis, keepdims=True)
    return (x - m) / jnp.sqrt(v + eps)

def _scatter_add(tgt, idx, src, axis=0):
    return tgt.at[idx].add(src)

def _segment_sum(src, seg, n):
    return jax.ops.segment_sum(src, seg, n)
kernel_name = 'mk_conv_preact_d4_conv_nchw256_r2_c52a7f'

def setup_inputs(seed: int=0):
    np.random.seed(seed)
    _w = jnp.asarray

    def _rec_inputs():
        import jax
        import jax.numpy as jnp
        _gk = jax.random.key(seed)
        x = -0.0003929 + 0.9999 * jax.random.normal(jax.random.fold_in(_gk, 1), (16, 128, 32, 32), jnp.float32)
        return x
    x = _rec_inputs()

    def _L0_conv_setup():
        import jax, jax.numpy as jnp
        import numpy as np

        def conv2d(x, w, padding, groups=1):
            return jax.lax.conv_general_dilated(x, w, window_strides=(1, 1), padding=[(padding, padding), (padding, padding)], feature_group_count=groups)

        def grid_sample_bilinear(img, gx, gy):
            B, C, H, W = img.shape
            ix = (gx + 1.0) * 0.5 * (W - 1)
            iy = (gy + 1.0) * 0.5 * (H - 1)
            x0 = jnp.floor(ix)
            y0 = jnp.floor(iy)
            x1 = x0 + 1.0
            y1 = y0 + 1.0
            wx1 = ix - x0
            wx0 = 1.0 - wx1
            wy1 = iy - y0
            wy0 = 1.0 - wy1
            flat = img.reshape(B, C, H * W)

            def corner(yy, xx, w):
                valid = ((xx >= 0) & (xx <= W - 1) & (yy >= 0) & (yy <= H - 1)).astype(img.dtype)
                xi = jnp.clip(xx, 0, W - 1).astype(jnp.int32)
                yi = jnp.clip(yy, 0, H - 1).astype(jnp.int32)
                idx = (yi * W + xi).reshape(B, 1, H * W)
                v = jnp.take_along_axis(flat, jnp.broadcast_to(idx, (B, C, H * W)), axis=-1)
                return v.reshape(B, C, H, W) * (w * valid)[:, None, :, :]
            return corner(y0, x0, wy0 * wx0) + corner(y0, x1, wy0 * wx1) + corner(y1, x0, wy1 * wx0) + corner(y1, x1, wy1 * wx1)
        key = jax.random.key(seed)
        k = jax.random.split(key, 5)
        B, C, H, W, Cout = (16, 128, 32, 32, 128)
        x = jax.random.normal(k[0], (B, C, H, W), jnp.float32)
        w_off = jax.random.normal(k[1], (3, C, 3, 3), jnp.float32) * 0.01
        b_off = jax.random.normal(k[2], (3,), jnp.float32) * 0.01
        w_dw = jax.random.normal(k[3], (C, 1, 3, 3), jnp.float32) / 3.0
        w_pw = jax.random.normal(k[4], (Cout, C, 1, 1), jnp.float32) / np.sqrt(C)
        return {'x': x, 'w_off': w_off, 'b_off': b_off, 'w_dw': w_dw, 'w_pw': w_pw}
    _L0_conv_all = _L0_conv_setup()
    _L0_conv_in = {k: v for k, v in _L0_conv_all.items() if k in ('w_off', 'b_off', 'w_dw', 'w_pw')}
    del _L0_conv_all

    def _L1_conv_setup():
        import jax, jax.numpy as jnp
        import numpy as np
        from jax import lax
        K = 3
        PAD = 1
        STRIDE = 1

        def conv2d(x, w, b, stride, pad):
            y = lax.conv_general_dilated(x, w, (stride, stride), [(pad, pad), (pad, pad)], dimension_numbers=('NCHW', 'OIHW', 'NCHW'))
            return y + b[None, :, None, None]

        def avg_pool3(x):
            s = lax.reduce_window(x, 0.0, lax.add, (1, 1, 3, 3), (1, 1, 1, 1), [(0, 0), (0, 0), (1, 1), (1, 1)])
            return s / 9.0

        def deform_conv2d(x, offset, mask, w, b):
            B, C, H, W = x.shape
            KK = K * K
            Ho, Wo = (offset.shape[2], offset.shape[3])
            off = offset.reshape(B, KK, 2, Ho, Wo)
            dy, dx = (off[:, :, 0], off[:, :, 1])
            ki = (jnp.arange(KK) // K).astype(jnp.float32)
            kj = (jnp.arange(KK) % K).astype(jnp.float32)
            base_y = (jnp.arange(Ho) * STRIDE - PAD).astype(jnp.float32)
            base_x = (jnp.arange(Wo) * STRIDE - PAD).astype(jnp.float32)
            py = base_y[None, :, None] + ki[:, None, None] + dy
            px = base_x[None, None, :] + kj[:, None, None] + dx
            y0 = jnp.floor(py).astype(jnp.int32)
            x0 = jnp.floor(px).astype(jnp.int32)
            wy = py - y0.astype(py.dtype)
            wx = px - x0.astype(px.dtype)
            xT = jnp.transpose(x, (0, 2, 3, 1))
            bidx = jnp.arange(B)[:, None, None, None]

            def gather(yi, xi):
                valid = ((yi >= 0) & (yi < H) & (xi >= 0) & (xi < W)).astype(x.dtype)
                yc = jnp.clip(yi, 0, H - 1)
                xc = jnp.clip(xi, 0, W - 1)
                v = xT[bidx, yc, xc]
                return v * valid[..., None]
            sampled = ((1 - wy) * (1 - wx))[..., None] * gather(y0, x0) + ((1 - wy) * wx)[..., None] * gather(y0, x0 + 1) + (wy * (1 - wx))[..., None] * gather(y0 + 1, x0) + (wy * wx)[..., None] * gather(y0 + 1, x0 + 1)
            sampled = sampled * mask[..., None]
            wk = w.reshape(w.shape[0], w.shape[1], KK)
            out = jnp.einsum('bkhwc,ock->bohw', sampled, wk)
            return out + b[None, :, None, None]
        key = jax.random.key(seed)
        ks = jax.random.split(key, 7)
        B, C, H, W = (4, 128, 40, 40)
        KK = K * K
        x = jax.random.normal(ks[0], (B, C, H, W), jnp.float32)
        off_w = jax.random.normal(ks[1], (2 * KK, C, K, K), jnp.float32) * 0.01
        off_b = jnp.zeros((2 * KK,), jnp.float32)
        mod_w = jax.random.normal(ks[2], (KK, C, K, K), jnp.float32) * 0.01
        mod_b = jnp.zeros((KK,), jnp.float32)
        fan_in = C * K * K
        w = jax.random.normal(ks[3], (C, C, K, K), jnp.float32) / np.sqrt(fan_in)
        b = jax.random.normal(ks[4], (C,), jnp.float32) * 0.01
        return {'x': x, 'off_w': off_w, 'off_b': off_b, 'mod_w': mod_w, 'mod_b': mod_b, 'w': w, 'b': b}
    _L1_conv_all = _L1_conv_setup()
    _L1_conv_in = {k: v for k, v in _L1_conv_all.items() if k in ('off_w', 'off_b', 'mod_w', 'mod_b', 'w', 'b')}
    del _L1_conv_all

    def _L2_conv_setup():
        import jax, jax.numpy as jnp
        import numpy as np
        TAU = 0.5
        C = 0.7
        ITAU = 1.0 - TAU
        key = jax.random.key(seed)
        k1, k2, k3, k4 = jax.random.split(key, 4)
        x = jax.random.normal(k1, (32, 128, 56, 56), dtype=jnp.float32)
        weight = jax.random.normal(k2, (128, 128, 3, 3), dtype=jnp.float32) * 0.02
        bias = jax.random.normal(k3, (128,), dtype=jnp.float32) * 0.02
        r_matrix = jax.random.uniform(k4, (128, 128, 3, 3), dtype=jnp.float32)
        return {'x': x, 'weight': weight, 'bias': bias, 'r_matrix': r_matrix}
    _L2_conv_all = _L2_conv_setup()
    _L2_conv_in = {k: v for k, v in _L2_conv_all.items() if k in ('weight', 'bias', 'r_matrix')}
    del _L2_conv_all

    def _L3_conv_setup():
        import jax, jax.numpy as jnp
        import numpy as np
        from jax import lax
        B, DIM, H, W = (4, 128, 64, 64)
        KS, LOC, STRIDES_CFG, HEADS = (5, [2, 3], [1, 2], 8)
        C2 = DIM // 2
        GK = HEADS * KS

        def _kernel_map(ks, kstride, kloc):
            axes, strides, start = ([0], [1], 1)
            for loc, s in zip(kloc, kstride):
                for num in range(0, loc - start):
                    axes.append(num * s + axes[-1] + strides[-1])
                    strides.append(s)
                start = loc
            patch = (axes[-1] + strides[-1]) * 2 - 1
            full_axes = [-a for a in axes[:0:-1]] + axes
            full_strides = strides[:0:-1] + strides
            return (full_axes, full_strides, patch)
        OFFS, STRDS, PATCH = _kernel_map(KS, STRIDES_CFG, LOC)
        PAD = PATCH // 2

        def _pw(x, w, b):
            return jnp.einsum('bchw,oc->bohw', x, w) + b[None, :, None, None]

        def _dw(x, w, b, ph, pw):
            y = lax.conv_general_dilated(x, w, (1, 1), [(ph, ph), (pw, pw)], feature_group_count=x.shape[1], dimension_numbers=('NCHW', 'OIHW', 'NCHW'))
            return y + b[None, :, None, None]

        def _fsa(x, kern, groups, axis):
            Bx, Cx, Hx, Wx = x.shape
            gd = Cx // groups
            K = len(OFFS)
            L = x.shape[axis]
            padcfg = [(0, 0)] * 4
            padcfg[axis] = (PAD, PAD)
            xp = jnp.pad(x, padcfg)
            taps = []
            for a, s in zip(OFFS, STRDS):
                start = a if a >= 0 else a - s + 1
                acc = lax.slice_in_dim(xp, PAD + start, PAD + start + L, axis=axis)
                for d in range(1, s):
                    acc = acc + lax.slice_in_dim(xp, PAD + start + d, PAD + start + d + L, axis=axis)
                taps.append(acc / s)
            t = jnp.stack(taps, 0).reshape(K, Bx, groups, gd, Hx, Wx)
            k = kern.reshape(Bx, groups, K, Hx, Wx)
            return jnp.einsum('kbgdhw,bgkhw->bgdhw', t, k).reshape(Bx, Cx, Hx, Wx)
        key = jax.random.key(seed)
        ks = jax.random.split(key, 12)
        sc = 0.02
        f32 = jnp.float32
        return {'x': jax.random.normal(ks[0], (B, DIM, H, W), f32), 'proj_in_w': jax.random.normal(ks[1], (DIM, DIM), f32) * sc, 'proj_in_b': jnp.zeros((DIM,), f32), 'hk_dw_w': jax.random.normal(ks[2], (C2, 1, 1, PATCH), f32) * sc, 'hk_dw_b': jnp.zeros((C2,), f32), 'hk_pw_w': jax.random.normal(ks[3], (GK, C2), f32) * sc, 'hk_pw_b': jnp.zeros((GK,), f32), 'vk_dw_w': jax.random.normal(ks[4], (C2, 1, PATCH, 1), f32) * sc, 'vk_dw_b': jnp.zeros((C2,), f32), 'vk_pw_w': jax.random.normal(ks[5], (GK, C2), f32) * sc, 'vk_pw_b': jnp.zeros((GK,), f32), 'cb_w1': jax.random.normal(ks[6], (DIM // 4, C2), f32) * sc, 'cb_b1': jnp.zeros((DIM // 4,), f32), 'cb_w2': jax.random.normal(ks[7], (C2, DIM // 4), f32) * sc, 'cb_b2': jnp.zeros((C2,), f32), 'proj_out_w': jax.random.normal(ks[8], (DIM, DIM), f32) * sc, 'proj_out_b': jnp.zeros((DIM,), f32)}
    _L3_conv_all = _L3_conv_setup()
    _L3_conv_in = {k: v for k, v in _L3_conv_all.items() if k in ('proj_in_w', 'proj_in_b', 'hk_dw_w', 'hk_dw_b', 'hk_pw_w', 'hk_pw_b', 'vk_dw_w', 'vk_dw_b', 'vk_pw_w', 'vk_pw_b', 'cb_w1', 'cb_b1', 'cb_w2', 'cb_b2', 'proj_out_w', 'proj_out_b')}
    del _L3_conv_all
    return {'x': x, 'L0_conv_w_off': _L0_conv_in['w_off'], 'L0_conv_b_off': _L0_conv_in['b_off'], 'L0_conv_w_dw': _L0_conv_in['w_dw'], 'L0_conv_w_pw': _L0_conv_in['w_pw'], 'L1_conv_off_w': _L1_conv_in['off_w'], 'L1_conv_off_b': _L1_conv_in['off_b'], 'L1_conv_mod_w': _L1_conv_in['mod_w'], 'L1_conv_mod_b': _L1_conv_in['mod_b'], 'L1_conv_w': _L1_conv_in['w'], 'L1_conv_b': _L1_conv_in['b'], 'L2_conv_weight': _L2_conv_in['weight'], 'L2_conv_bias': _L2_conv_in['bias'], 'L2_conv_r_matrix': _L2_conv_in['r_matrix'], 'L3_conv_proj_in_w': _L3_conv_in['proj_in_w'], 'L3_conv_proj_in_b': _L3_conv_in['proj_in_b'], 'L3_conv_hk_dw_w': _L3_conv_in['hk_dw_w'], 'L3_conv_hk_dw_b': _L3_conv_in['hk_dw_b'], 'L3_conv_hk_pw_w': _L3_conv_in['hk_pw_w'], 'L3_conv_hk_pw_b': _L3_conv_in['hk_pw_b'], 'L3_conv_vk_dw_w': _L3_conv_in['vk_dw_w'], 'L3_conv_vk_dw_b': _L3_conv_in['vk_dw_b'], 'L3_conv_vk_pw_w': _L3_conv_in['vk_pw_w'], 'L3_conv_vk_pw_b': _L3_conv_in['vk_pw_b'], 'L3_conv_cb_w1': _L3_conv_in['cb_w1'], 'L3_conv_cb_b1': _L3_conv_in['cb_b1'], 'L3_conv_cb_w2': _L3_conv_in['cb_w2'], 'L3_conv_cb_b2': _L3_conv_in['cb_b2'], 'L3_conv_proj_out_w': _L3_conv_in['proj_out_w'], 'L3_conv_proj_out_b': _L3_conv_in['proj_out_b']}

def reference(x, L0_conv_w_off, L0_conv_b_off, L0_conv_w_dw, L0_conv_w_pw, L1_conv_off_w, L1_conv_off_b, L1_conv_mod_w, L1_conv_mod_b, L1_conv_w, L1_conv_b, L2_conv_weight, L2_conv_bias, L2_conv_r_matrix, L3_conv_proj_in_w, L3_conv_proj_in_b, L3_conv_hk_dw_w, L3_conv_hk_dw_b, L3_conv_hk_pw_w, L3_conv_hk_pw_b, L3_conv_vk_dw_w, L3_conv_vk_dw_b, L3_conv_vk_pw_w, L3_conv_vk_pw_b, L3_conv_cb_w1, L3_conv_cb_b1, L3_conv_cb_w2, L3_conv_cb_b2, L3_conv_proj_out_w, L3_conv_proj_out_b):
    import jax
    import jax.numpy as jnp

    def _L0_conv_ref(x, w_off, b_off, w_dw, w_pw):
        import jax, jax.numpy as jnp
        import numpy as np

        def conv2d(x, w, padding, groups=1):
            return jax.lax.conv_general_dilated(x, w, window_strides=(1, 1), padding=[(padding, padding), (padding, padding)], feature_group_count=groups)

        def grid_sample_bilinear(img, gx, gy):
            B, C, H, W = img.shape
            ix = (gx + 1.0) * 0.5 * (W - 1)
            iy = (gy + 1.0) * 0.5 * (H - 1)
            x0 = jnp.floor(ix)
            y0 = jnp.floor(iy)
            x1 = x0 + 1.0
            y1 = y0 + 1.0
            wx1 = ix - x0
            wx0 = 1.0 - wx1
            wy1 = iy - y0
            wy0 = 1.0 - wy1
            flat = img.reshape(B, C, H * W)

            def corner(yy, xx, w):
                valid = ((xx >= 0) & (xx <= W - 1) & (yy >= 0) & (yy <= H - 1)).astype(img.dtype)
                xi = jnp.clip(xx, 0, W - 1).astype(jnp.int32)
                yi = jnp.clip(yy, 0, H - 1).astype(jnp.int32)
                idx = (yi * W + xi).reshape(B, 1, H * W)
                v = jnp.take_along_axis(flat, jnp.broadcast_to(idx, (B, C, H * W)), axis=-1)
                return v.reshape(B, C, H, W) * (w * valid)[:, None, :, :]
            return corner(y0, x0, wy0 * wx0) + corner(y0, x1, wy0 * wx1) + corner(y1, x0, wy1 * wx0) + corner(y1, x1, wy1 * wx1)
        B, C, H, W = x.shape
        om = conv2d(x, w_off, 1) + b_off[None, :, None, None]
        off_y = om[:, 0]
        off_x = om[:, 1]
        mask = jax.nn.sigmoid(om[:, 2:3])
        gy_base, gx_base = jnp.meshgrid(jnp.linspace(-1.0, 1.0, H, dtype=x.dtype), jnp.linspace(-1.0, 1.0, W, dtype=x.dtype), indexing='ij')
        gx = gx_base[None] + off_x * (2.0 / W)
        gy = gy_base[None] + off_y * (2.0 / H)
        x_def = grid_sample_bilinear(x, gx, gy) * mask
        out = conv2d(x_def, w_dw, 1, groups=C)
        out = conv2d(out, w_pw, 0)
        return out

    def _L1_conv_ref(x, off_w, off_b, mod_w, mod_b, w, b):
        import jax, jax.numpy as jnp
        import numpy as np
        from jax import lax
        K = 3
        PAD = 1
        STRIDE = 1

        def conv2d(x, w, b, stride, pad):
            y = lax.conv_general_dilated(x, w, (stride, stride), [(pad, pad), (pad, pad)], dimension_numbers=('NCHW', 'OIHW', 'NCHW'))
            return y + b[None, :, None, None]

        def avg_pool3(x):
            s = lax.reduce_window(x, 0.0, lax.add, (1, 1, 3, 3), (1, 1, 1, 1), [(0, 0), (0, 0), (1, 1), (1, 1)])
            return s / 9.0

        def deform_conv2d(x, offset, mask, w, b):
            B, C, H, W = x.shape
            KK = K * K
            Ho, Wo = (offset.shape[2], offset.shape[3])
            off = offset.reshape(B, KK, 2, Ho, Wo)
            dy, dx = (off[:, :, 0], off[:, :, 1])
            ki = (jnp.arange(KK) // K).astype(jnp.float32)
            kj = (jnp.arange(KK) % K).astype(jnp.float32)
            base_y = (jnp.arange(Ho) * STRIDE - PAD).astype(jnp.float32)
            base_x = (jnp.arange(Wo) * STRIDE - PAD).astype(jnp.float32)
            py = base_y[None, :, None] + ki[:, None, None] + dy
            px = base_x[None, None, :] + kj[:, None, None] + dx
            y0 = jnp.floor(py).astype(jnp.int32)
            x0 = jnp.floor(px).astype(jnp.int32)
            wy = py - y0.astype(py.dtype)
            wx = px - x0.astype(px.dtype)
            xT = jnp.transpose(x, (0, 2, 3, 1))
            bidx = jnp.arange(B)[:, None, None, None]

            def gather(yi, xi):
                valid = ((yi >= 0) & (yi < H) & (xi >= 0) & (xi < W)).astype(x.dtype)
                yc = jnp.clip(yi, 0, H - 1)
                xc = jnp.clip(xi, 0, W - 1)
                v = xT[bidx, yc, xc]
                return v * valid[..., None]
            sampled = ((1 - wy) * (1 - wx))[..., None] * gather(y0, x0) + ((1 - wy) * wx)[..., None] * gather(y0, x0 + 1) + (wy * (1 - wx))[..., None] * gather(y0 + 1, x0) + (wy * wx)[..., None] * gather(y0 + 1, x0 + 1)
            sampled = sampled * mask[..., None]
            wk = w.reshape(w.shape[0], w.shape[1], KK)
            out = jnp.einsum('bkhwc,ock->bohw', sampled, wk)
            return out + b[None, :, None, None]
        xp = avg_pool3(x)
        offset = conv2d(xp, off_w, off_b, STRIDE, PAD)
        mask = 2.0 * jax.nn.sigmoid(conv2d(xp, mod_w, mod_b, STRIDE, PAD))
        return deform_conv2d(xp, offset, mask, w, b)

    def _L2_conv_ref(x, weight, bias, r_matrix):
        import jax, jax.numpy as jnp
        import numpy as np
        TAU = 0.5
        C = 0.7
        ITAU = 1.0 - TAU
        mask = (TAU > r_matrix).astype(weight.dtype)
        imask = (r_matrix > TAU).astype(weight.dtype)
        w = C * jnp.sign(weight * imask) + ITAU * (weight + C * TAU * jnp.sign(weight * mask))
        y = jax.lax.conv_general_dilated(x, w, window_strides=(1, 1), padding=((1, 1), (1, 1)), dimension_numbers=('NCHW', 'OIHW', 'NCHW'))
        return y + bias[None, :, None, None]

    def _L3_conv_ref(x, proj_in_w, proj_in_b, hk_dw_w, hk_dw_b, hk_pw_w, hk_pw_b, vk_dw_w, vk_dw_b, vk_pw_w, vk_pw_b, cb_w1, cb_b1, cb_w2, cb_b2, proj_out_w, proj_out_b):
        import jax, jax.numpy as jnp
        import numpy as np
        from jax import lax
        B, DIM, H, W = (4, 128, 64, 64)
        KS, LOC, STRIDES_CFG, HEADS = (5, [2, 3], [1, 2], 8)
        C2 = DIM // 2
        GK = HEADS * KS

        def _kernel_map(ks, kstride, kloc):
            axes, strides, start = ([0], [1], 1)
            for loc, s in zip(kloc, kstride):
                for num in range(0, loc - start):
                    axes.append(num * s + axes[-1] + strides[-1])
                    strides.append(s)
                start = loc
            patch = (axes[-1] + strides[-1]) * 2 - 1
            full_axes = [-a for a in axes[:0:-1]] + axes
            full_strides = strides[:0:-1] + strides
            return (full_axes, full_strides, patch)
        OFFS, STRDS, PATCH = _kernel_map(KS, STRIDES_CFG, LOC)
        PAD = PATCH // 2

        def _pw(x, w, b):
            return jnp.einsum('bchw,oc->bohw', x, w) + b[None, :, None, None]

        def _dw(x, w, b, ph, pw):
            y = lax.conv_general_dilated(x, w, (1, 1), [(ph, ph), (pw, pw)], feature_group_count=x.shape[1], dimension_numbers=('NCHW', 'OIHW', 'NCHW'))
            return y + b[None, :, None, None]

        def _fsa(x, kern, groups, axis):
            Bx, Cx, Hx, Wx = x.shape
            gd = Cx // groups
            K = len(OFFS)
            L = x.shape[axis]
            padcfg = [(0, 0)] * 4
            padcfg[axis] = (PAD, PAD)
            xp = jnp.pad(x, padcfg)
            taps = []
            for a, s in zip(OFFS, STRDS):
                start = a if a >= 0 else a - s + 1
                acc = lax.slice_in_dim(xp, PAD + start, PAD + start + L, axis=axis)
                for d in range(1, s):
                    acc = acc + lax.slice_in_dim(xp, PAD + start + d, PAD + start + d + L, axis=axis)
                taps.append(acc / s)
            t = jnp.stack(taps, 0).reshape(K, Bx, groups, gd, Hx, Wx)
            k = kern.reshape(Bx, groups, K, Hx, Wx)
            return jnp.einsum('kbgdhw,bgkhw->bgdhw', t, k).reshape(Bx, Cx, Hx, Wx)
        Bv, _, Hv, Wv = x.shape
        h = _pw(x, proj_in_w, proj_in_b)
        x1, x2 = (h[:, :C2], h[:, C2:])
        x_conv = _pw(jax.nn.relu(_pw(x1, cb_w1, cb_b1)), cb_w2, cb_b2)
        kh = jnp.tanh(_pw(_dw(x2, hk_dw_w, hk_dw_b, 0, PAD), hk_pw_w, hk_pw_b))
        attn_h = _fsa(x2, kh, HEADS, axis=3)
        kv = jnp.tanh(_pw(_dw(attn_h, vk_dw_w, vk_dw_b, PAD, 0), vk_pw_w, vk_pw_b))
        attn = _fsa(attn_h, kv, HEADS, axis=2)
        N = Hv * Wv
        xc = x_conv.reshape(Bv, C2, N)
        at = attn.reshape(Bv, C2, N)
        s_sig = jax.nn.sigmoid(jnp.einsum('bc,bcn->bn', at.mean(-1), xc) / C2)[:, None, :]
        spatial_map = (s_sig * xc).reshape(Bv, C2, Hv, Wv)
        c_sig = jax.nn.sigmoid(jnp.einsum('bcn,bn->bc', at, xc.mean(1)) / N)[:, :, None]
        channel_map = (c_sig * at).reshape(Bv, C2, Hv, Wv)
        out = jnp.concatenate([spatial_map, channel_map], axis=1)
        return _pw(out, proj_out_w, proj_out_b)

    def _gn(v, G=32, eps=1e-05):
        B_, C_, H_, W_ = v.shape
        g = v.reshape(B_, G, C_ // G, H_, W_)
        m = jnp.mean(g, axis=(2, 3, 4), keepdims=True)
        s = jnp.var(g, axis=(2, 3, 4), keepdims=True)
        return ((g - m) / jnp.sqrt(s + eps)).reshape(v.shape)

    def _ln_c(v, eps=1e-06):
        m = jnp.mean(v, axis=1, keepdims=True)
        s = jnp.var(v, axis=1, keepdims=True)
        return (v - m) / jnp.sqrt(s + eps)

    def _ln_t(v, eps=1e-05):
        m = jnp.mean(v, axis=-1, keepdims=True)
        s = jnp.var(v, axis=-1, keepdims=True)
        return (v - m) / jnp.sqrt(s + eps)

    def _to_tokens(v):
        B_, C_, H_, W_ = v.shape
        return v.reshape(B_, C_, H_ * W_).transpose(0, 2, 1)

    def _from_tokens(t, like):
        B_, C_, H_, W_ = like.shape
        return t.transpose(0, 2, 1).reshape(B_, C_, H_, W_)
    x = x + _L0_conv_ref(_gn(x), L0_conv_w_off, L0_conv_b_off, L0_conv_w_dw, L0_conv_w_pw)
    x = x + _L1_conv_ref(_gn(x), L1_conv_off_w, L1_conv_off_b, L1_conv_mod_w, L1_conv_mod_b, L1_conv_w, L1_conv_b)
    x = x + _L2_conv_ref(_gn(x), L2_conv_weight, L2_conv_bias, L2_conv_r_matrix)
    x = x + _L3_conv_ref(_gn(x), L3_conv_proj_in_w, L3_conv_proj_in_b, L3_conv_hk_dw_w, L3_conv_hk_dw_b, L3_conv_hk_pw_w, L3_conv_hk_pw_b, L3_conv_vk_dw_w, L3_conv_vk_dw_b, L3_conv_vk_pw_w, L3_conv_vk_pw_b, L3_conv_cb_w1, L3_conv_cb_b1, L3_conv_cb_w2, L3_conv_cb_b2, L3_conv_proj_out_w, L3_conv_proj_out_b)
    return x

_drawn_inputs = setup_inputs


def setup_inputs(seed=0):
    import zlib

    import numpy as np

    out = dict(_drawn_inputs(seed))
    spreads = {'L1_conv_off_b': (0.0, 0.3),
     'L1_conv_mod_b': (0.0, 2.0),
     'L3_conv_proj_in_b': (0.0, 0.8),
     'L3_conv_hk_dw_b': (0.0, 0.8),
     'L3_conv_hk_pw_b': (0.0, 0.8),
     'L3_conv_vk_dw_b': (0.0, 0.8),
     'L3_conv_vk_pw_b': (0.0, 0.8),
     'L3_conv_cb_b1': (0.0, 2.0),
     'L3_conv_cb_b2': (0.0, 0.8),
     'L3_conv_proj_out_b': (0.0, 0.8)}
    factors = {'L0_conv_b_off': 8.0,
     'L1_conv_mod_w': 3.514,
     'L1_conv_b': 6.365,
     'L2_conv_bias': 47.616,
     'L3_conv_proj_in_w': 8.0,
     'L3_conv_hk_dw_w': 8.0,
     'L3_conv_hk_pw_w': 8.0,
     'L3_conv_vk_dw_w': 8.0,
     'L3_conv_vk_pw_w': 8.0,
     'L3_conv_cb_w1': 8.0,
     'L3_conv_cb_w2': 8.0,
     'L3_conv_proj_out_w': 8.0}
    for name, (base, spread) in spreads.items():
        noise = np.random.default_rng([zlib.crc32(name.encode()), seed]).standard_normal(out[name].shape)
        drawn = base * np.exp(spread * noise) if base else spread * noise
        out[name] = jnp.asarray(drawn.astype(out[name].dtype))
    for name, factor in factors.items():
        out[name] = (out[name] * factor).astype(out[name].dtype)
    return out
```

```python
from contextlib import ExitStack

import concourse.bass as bass
from concourse import mybir

F32 = mybir.dt.float32
I32 = mybir.dt.int32
ALU = mybir.AluOpType
ACT = mybir.ActivationFunctionType
AX = mybir.AxisListType

C = 128
H = W = 32
N = H * W
HALF = 512
PAD = 2
PW = W + 2 * PAD
TILES = 8
STRIPS = 4
SW = W // STRIPS
K9 = 9
GROUP = 4
EPS = 1e-5
BR, BC = 10, 12
BLK = BR * BC
C2 = 64
TAPS = 5
LPAD = 3
LW = W + 2 * LPAD

V_B1, V_B2, V_BIN1, V_BIN2, V_BCB1, V_BCB2, V_BOUT, V_DWHB, V_DWVB = range(9)
V_DWH, V_DWV = 9, 16
V_KHB, V_KVB = 23, 28
V_DW0 = 33
V_N = 42

T_IOTA = 0
T_GAVG = T_IOTA + 32
T_ONES = T_GAVG + C
T_BLK = T_ONES + C
T_LIN = T_BLK + C
T_POS = T_LIN + 2 * TILES
T_EY = T_POS + 2 * TILES * K9
T_EX = T_EY + BR
T_SEL = T_EX + K9 * BC
TAB_N = T_SEL + 32
NEAR = 1.0
CONSTS = 15
DVE_STEPS = 100


class Signal:

    def __init__(self, sem, per_pass, start=1):
        self.sem, self.per_pass, self.start = sem, per_pass, start

    def at(self, i, n):
        assert self.start or n
        return i * self.per_pass + n + self.start


class Own:

    def __init__(self, eng, steps, i):
        self.eng, self.steps, self.i, self.n = eng, steps, i, 0

    def step(self, ins):
        ins.then_inc(self.steps.sem, 1)
        self.n += 1

    def settle(self):
        self.eng.wait_ge(self.steps.sem, self.steps.at(self.i, self.n))


def conv_preact_kernel(nc, x_d, ident_d, tab_d, vec_d, offb_d, w0off_d, w0dw_pw_d, w1off_d, w1_d, w2_d, r2_d,
                       win_d, win2T_d, cb1T_d, cb2T_d, kh_d, kv_d, woT_d, out_d):
    PASSES = x_d.shape[0] // 2
    with ExitStack() as ctx:
        def sb(name, shape, dt=F32):
            return ctx.enter_context(nc.sbuf_tensor(name, shape, dt))

        def sem(name):
            return ctx.enter_context(nc.semaphore(name))

        signals = []

        def signal(name, per_pass):
            signals.append(Signal(sem(name), per_pass))
            return signals[-1]

        ident = sb("ident", [C, C])
        tab = sb("tab", [C, TAB_N])
        vec = sb("vec", [C, V_N])
        offb = sb("offb", [C, 30])
        w0off = sb("w0off", [C, K9, 32])
        pwT = sb("pwT", [C, C])
        w0 = sb("w0", [C, K9, C])
        w1off = sb("w1off", [C, K9, 32])
        w1 = sb("w1", [C, K9, C])
        w2 = sb("w2", [C, K9, C])
        win = sb("win", [C2, C])
        win2T = sb("win2T", [C, C2])
        cb1T = sb("cb1T", [C2, C2])
        cb2T = sb("cb2T", [C, C])
        kh_w = sb("kh_w", [C, TAPS, C])
        kv_w = sb("kv_w", [C, TAPS, C])
        woT = sb("woT", [C, 2, 2, C])
        wu = sb("wu", [C, C2])
        bu = sb("bu", [C2, 1])

        xin = [sb(f"xin{s}", [C, N]) for s in range(2)]
        x = [sb(f"x{s}", [C, N]) for s in range(2)]
        yout = [sb(f"yout{s}", [C, N]) for s in range(2)]
        xn = [sb(f"xn{s}", [C, PW, PW]) for s in range(2)]
        img = [sb(f"img{s}", [C, PW, PW]) for s in range(2)]
        gst = [sb(f"gst{s}", [C, 24]) for s in range(2)]
        om = [sb(f"om{s}", [C, 3, TILES, K9]) for s in range(2)]
        om0 = [sb(f"om0{s}", [C, 3, TILES]) for s in range(2)]
        mk = [sb(f"mk{s}", [C, TILES * K9]) for s in range(2)]
        xT = [sb(f"xT{s}", [C, TILES, C]) for s in range(2)]
        hat = [sb(f"hat{s}", [C, 2 * TILES, 32]) for s in range(2)]
        hfy = [sb(f"hfy{s}", [C, TILES * K9, BR]) for s in range(2)]
        hfx = [sb(f"hfx{s}", [C, TILES * K9, BC]) for s in range(2)]
        pool_v = sb("pool_v", [C, H, W + 2])
        neg_half = sb("neg_half", [C, 1])
        GT = [sb(f"GT{b}", [C, N]) for b in range(2)]
        Gd = [sb(f"Gd{b}", [C, TILES, C]) for b in range(2)]
        GT1 = [sb(f"GT1{b}", [C, 3, BLK]) for b in range(2)]
        G1 = [sb(f"G1{b}", [BLK, 3, C]) for b in range(2)]
        xblk = [sb(f"xblk{b}", [BLK, 2, C]) for b in range(2)]
        samp = sb("samp", [C, K9, N])
        q_strips = [sb(f"q_strips{s}", [C, N]) for s in range(2)]
        strip12 = [sb(f"strip12{s}", [C, STRIPS, PW, BC]) for s in range(2)]
        flag = [sb(f"flag{s}", [C, 1], I32) for s in range(2)]
        flagf = [sb(f"flagf{s}", [C, 2]) for s in range(2)]
        x2p = sb("x2p", [C, H, LW])
        ahp = sb("ahp", [C, H + 2 * LPAD, W])
        kern, dwo, tmp3, sg, sm = samp[:, 0:TAPS, :], *(samp[:, TAPS + n, :] for n in range(4))
        psum2 = strip12[0][:].rearrange("p j r c -> p (j r c)")
        u3 = sb("u3", [C, N])
        xc = sb("xc", [C, N])
        at = sb("at", [C, N])
        off_parts = [xc, at]
        wss = sb("wss", [C, C])
        wo2 = xT[0][:, 0:2, :]
        st3 = sb("st3", [C, 4])

        ps = [ctx.enter_context(nc.psum_tensor(f"ps{b}", [C, HALF], F32)) for b in range(2)]
        psO = [ctx.enter_context(nc.psum_tensor(f"psO{b}", [C, 2, HALF], F32)) for b in range(2)]
        psT = ctx.enter_context(nc.psum_tensor("psT", [C, 2, HALF], F32))

        iota32 = tab[:, T_IOTA:T_IOTA + 32]
        gavg = tab[:, T_GAVG:T_GAVG + C]
        ones = tab[:, T_ONES:T_ONES + C]
        blk64 = tab[:, T_BLK:T_BLK + C]

        passed = {eng: sem(f"passed_{name}") for eng, name in ((nc.tensor, "pe"), (nc.scalar, "act"), (nc.vector, "dve"))}
        consts_landed = sem("consts_landed")
        borders_zero = sem("borders_zero")
        prep = sem("prep")
        prep_dve = sem("prep_dve")
        weights_ready = sem("weights_ready")
        w2_landed = sem("w2_landed")
        x_landed = [Signal(sem(f"x_landed{s}"), 16, 0) for s in range(2)]
        y_ready = signal("y_ready", 2)
        yout_free = signal("yout_free", 2)
        y_stored = [Signal(sem(f"y_stored{s}"), 16, 0) for s in range(2)]
        stats_ready = signal("stats_ready", 8)
        group_ready = signal("group_ready", 8)
        var_ready = signal("var_ready", 8)
        rstd_ready = signal("rstd_ready", 8)
        affine_ready = signal("affine_ready", 8)
        xn_ready = signal("xn_ready", 8)
        pooled_ready = signal("pooled_ready", 2)
        strips_ready = signal("strips_ready", 2)
        parts_product = signal("parts_product", 4)
        parts_ready = signal("parts_ready", 4)
        wide_ready = signal("wide_ready", 2)
        xT_product = signal("xT_product", 2)
        xT_ready = signal("xT_ready", 2)
        offs_ready = signal("offs_ready", 4)
        om_ready = signal("om_ready", 4)
        mask_ready = signal("mask_ready", 4)
        GT_ready = signal("GT_ready", 2 * TILES)
        GTt_ready = signal("GTt_ready", 2 * TILES)
        Gd_ready = signal("Gd_ready", 2 * TILES)
        sampled = signal("sampled", 2 * TILES)
        img_ready = signal("img_ready", 2)
        conv_ready = signal("conv_ready", 6)
        added = signal("added", 6)
        far_count = signal("far_count", 2)
        far_input = signal("far_input", 2)
        far_ready = signal("far_ready", 2)
        G_OWN = 1 + K9 * 4
        g_strips = signal("g_strips", 2)
        g_xTp = signal("g_xTp", 2)
        g_xT = signal("g_xT", 2)
        g_own = signal("g_own", 2 * G_OWN)
        g_GT = signal("g_GT", 2 * K9 * TILES)
        g_GTt = signal("g_GTt", 2 * K9 * TILES)
        g_Gd = signal("g_Gd", 2 * K9 * TILES)
        g_smp = signal("g_smp", 2 * K9 * TILES)
        g_smp_sb = signal("g_smp_sb", 2 * K9)
        STEPS = TILES * 3
        N_OWN = 7
        n_own = signal("n_own", 2 * N_OWN)
        n_GT = signal("n_GT", 2 * STEPS)
        n_blkp = signal("n_blkp", 2 * STEPS)
        n_Gp = signal("n_Gp", 2 * STEPS)
        n_blk = signal("n_blk", 2 * STEPS)
        n_G = signal("n_G", 2 * STEPS)
        n_smp = signal("n_smp", 2 * STEPS)
        n_smp_sb = signal("n_smp_sb", 2 * STEPS)
        PRODUCTS = 17
        l3_product = signal("l3_product", PRODUCTS)
        l3_act = signal("l3_act", 14)
        l3_dw = signal("l3_dw", 2)
        l3_at = signal("l3_at", 1)
        l3_wss = signal("l3_wss", 1)
        l3_csum = signal("l3_csum", 1)
        l3_csig = signal("l3_csig", 1)
        l3_maps = signal("l3_maps", 2)
        dve_own = signal("dve_own", DVE_STEPS)

        def inner(t):
            return t[:, PAD:PAD + H, PAD:PAD + W]

        def tiled(t, b):
            return t[:, :, 16 * b:16 * b + 16].rearrange("p r (j c) -> p j r c", c=SW)

        def wait_apart(eng, *waits):
            for signal, value in waits:
                eng.wait_ge(signal.sem, value)
            eng.sem_inc(passed[eng], 1)

        block = ctx.enter_context(nc.Block())

        @block.sync
        def _(sp):
            for dst, src in ((tab, tab_d), (vec, vec_d), (offb, offb_d), (w0off, w0off_d), (w1off, w1off_d),
                             (ident, ident_d), (win, win_d), (win2T, win2T_d),
                             (cb1T, cb1T_d), (cb2T, cb2T_d)):
                sp.dma_start(dst[:], src).then_inc(consts_landed, 16)
            for s in range(2):
                sp.dma_start(xin[s][:], x_d[s, :, :]).then_inc(x_landed[s].sem, 16)
            for dst, src in ((pwT, w0dw_pw_d), (w1, w1_d), (kh_w, kh_d), (kv_w, kv_d), (woT, woT_d)):
                sp.dma_start(dst[:], src).then_inc(consts_landed, 16)
            sp.dma_start(w2[:], w2_d).then_inc(w2_landed, 16)
            sp.dma_start(samp[:, 0:2, :].rearrange("p a b -> p (a b)")[:, 0:K9 * C], r2_d).then_inc(w2_landed, 16)

            def store(i, s):
                sp.wait_ge(y_ready.sem, y_ready.at(i, s + 1))
                sp.dma_start(out_d[2 * i + s, :, :], yout[s][:]).then_inc(y_stored[s].sem, 16)

            if PASSES > 1:
                with sp.Fori(0, PASSES - 1) as i:
                    for s in range(2):
                        sp.wait_ge(added.sem, added.at(i, s + 1))
                        sp.dma_start(xin[s][:], x_d[2 * i + 2 + s, :, :]).then_inc(x_landed[s].sem, 16)
                    for s in range(2):
                        store(i, s)
                    for s in range(2):
                        sp.wait_ge(y_stored[s].sem, y_stored[s].at(i, 16))
                        sp.sem_inc(yout_free.sem, 1)
            for s in range(2):
                store(PASSES - 1, s)
            for s in range(2):
                sp.wait_ge(y_stored[s].sem, y_stored[s].at(PASSES - 1, 16))

        @block.gpsimd
        def _(pool):
            for each in signals:
                pool.sem_inc(each.sem, each.start)
            for t in (xn[0], xn[1], img[0], img[1], x2p, ahp, u3):
                nc.gpsimd.memset(t[:], 0.0).then_inc(borders_zero, 1)
            nc.gpsimd.memset(neg_half[:], -0.5).then_inc(borders_zero, 1)
            pool.wait_ge(borders_zero, 8)
            with pool.Fori(0, PASSES) as i:
                for n in range(8):
                    g = gst[n % 2]
                    pool.wait_ge(var_ready.sem, var_ready.at(i, n + 1))
                    nc.gpsimd.tensor_tensor(out=g[:, 18:19], in0=g[:, 17:18], in1=neg_half[:],
                                            op=ALU.pow).then_inc(rstd_ready.sem, 1)

        @block.tensor
        def _(pe):
            mm = nc.tensor.matmul
            pe.wait_ge(consts_landed, CONSTS * 16)
            mm(ps[0][:, 0:C2], win[:], cb1T[:], start=True, stop=True).then_inc(prep, 1)
            mm(ps[1][0:C2, 0:1], cb1T[:], vec[0:C2, V_BIN1:V_BIN1 + 1], start=True, stop=True).then_inc(prep, 1)
            pe.wait_ge(weights_ready, 1)
            pe.wait_ge(borders_zero, 8)

            def group_mean(i, n):
                pe.wait_ge(stats_ready.sem, stats_ready.at(i, n + 1))
                mm(ps[n % 2][:, 0:2], gavg, gst[n % 2][:, 12:14], start=True, stop=True).then_inc(group_ready.sem, 1)

            def offset_parts(n, src, w):
                s = n % 2
                for h in range(2):
                    for k in range(K9):
                        g = k % 4
                        last = mm(psO[s][32 * g:32 * g + 32, h, :], w[:, k, :], window(src)(h, k),
                                  start=(k < 4), stop=(k >= K9 - 4), skip_group_check=True)
                last.then_inc(parts_product.sem, 1)

            def offsets(i, n, m):
                s = n % 2
                pe.wait_ge(parts_ready.sem, parts_ready.at(i, n + 1))
                for t in range(TILES):
                    last = mm(ps[s][:, 4 + m * t:4 + m * t + m], off_parts[s][:, C * t:C * t + C],
                              tab[:, T_SEL:T_SEL + m], start=True, stop=True)
                last.then_inc(offs_ready.sem, 1)

            def image_T(s, finished):
                for q in range(TILES):
                    last = nc.tensor.transpose(psT[:, q // 4, C * (q % 4):C * (q % 4) + C],
                                               q_strips[s][:, C * q:C * q + C], ident[:])
                last.then_inc(finished.sem, 1)

            def conv(dst, wgt, rhs, mid=None):
                for h in range(2):
                    if mid and h:
                        mid()
                    for k in range(K9):
                        last = mm(dst[:, h, :], wgt[:, k, :], rhs(h, k), start=(k == 0), stop=(k == K9 - 1))
                last.then_inc(conv_ready.sem, 1)

            def window(src):
                return lambda h, k: src[:, PAD + 16 * h + k // 3 - 1:PAD + 16 * h + k // 3 + 15,
                                        PAD + k % 3 - 1:PAD + k % 3 - 1 + W]

            def dense(i, base, dst, xTs, GTr, GTt, Gdr, smp):
                for t in range(TILES + 1):
                    if t < TILES:
                        pe.wait_ge(GTr.sem, GTr.at(i, base + t + 1))
                        pe.wait_ge(Gdr.sem, Gdr.at(i, base + t))
                        for q in range(TILES):
                            last = nc.tensor.transpose(psT[:, q // 4, C * (q % 4):C * (q % 4) + C],
                                                       GT[t % 2][:, C * q:C * q + C], ident[:])
                        last.then_inc(GTt.sem, 1)
                    if t:
                        p = t - 1
                        pe.wait_ge(Gdr.sem, Gdr.at(i, base + p + 1))
                        for q in range(TILES):
                            last = mm(dst[:, p // 4, C * (p % 4):C * (p % 4) + C], xTs[:, q, :], Gd[p % 2][:, q, :],
                                      start=(q == 0), stop=(q == TILES - 1))
                        last.then_inc(smp.sem, 1)

            def near(i, s):
                for n in range(STEPS + 1):
                    if n < STEPS:
                        t, ki = n // 3, n % 3
                        o = STEPS * s + n
                        pe.wait_ge(n_blk.sem, n_blk.at(i, o))
                        for h in range(2):
                            r0 = 16 * (t % 2) + 8 * h + ki
                            b = strip12[s][:, t // 2, r0:r0 + BR, :].rearrange("p r c -> p (r c)")
                            last = nc.tensor.transpose(psT[0:BLK, 1, C * h:C * h + C], b, ident[:])
                        last.then_inc(n_blkp.sem, 1)
                        pe.wait_ge(n_GT.sem, n_GT.at(i, o + 1))
                        pe.wait_ge(n_G.sem, n_G.at(i, o))
                        for kj in range(3):
                            last = nc.tensor.transpose(psT[0:BLK, 0, C * kj:C * kj + C], GT1[n % 2][:, kj, :], ident[:])
                        last.then_inc(n_Gp.sem, 1)
                    if n:
                        p = n - 1
                        o = STEPS * s + p
                        pe.wait_ge(n_blk.sem, n_blk.at(i, o + 1))
                        pe.wait_ge(n_G.sem, n_G.at(i, o + 1))
                        if o >= 2:
                            pe.wait_ge(n_smp_sb.sem, n_smp_sb.at(i, o - 1))
                        dst = psO[1][:, p % 2, 0:3 * C].rearrange("p (k c) -> p k c", k=3)
                        for h in range(2):
                            half = slice(64 * h, 64 * h + 64)
                            last = mm(dst[:, :, half], xblk[p % 2][:, h, :], G1[p % 2][:, :, half],
                                      start=True, stop=True)
                        last.then_inc(n_smp.sem, 1)

            with pe.Fori(0, PASSES) as i:
                for s in range(2):
                    group_mean(i, s)
                for s in range(2):
                    pe.wait_ge(xn_ready.sem, xn_ready.at(i, s + 1))
                    pe.wait_ge(y_ready.sem, y_ready.at(i, 0))
                    offset_parts(s, xn[s], w0off)
                    pe.wait_ge(strips_ready.sem, strips_ready.at(i, s + 1))
                    pe.wait_ge(xT_ready.sem, xT_ready.at(i, s))
                    image_T(s, xT_product)
                for s in range(2):
                    offsets(i, s, 3)
                pe.wait_ge(xT_ready.sem, xT_ready.at(i, 2))
                for s in range(2):
                    dense(i, TILES * s, psO[s], xT[s], GT_ready, GTt_ready, Gd_ready, sampled)
                for s in range(2):
                    pe.wait_ge(img_ready.sem, img_ready.at(i, s + 1))
                    conv(psO[s], w0, window(img[s]), mid=(lambda: group_mean(i, 2)) if s else None)
                def far(s):
                    pe.wait_ge(far_input.sem, far_input.at(i, s + 1))
                    mm(ps[s][:, 2:3], ones, flagf[s][:, 0:1], start=True, stop=True).then_inc(far_count.sem, 1)

                pe.wait_ge(pooled_ready.sem, pooled_ready.at(i, 1))
                offset_parts(2, img[0], w1off)
                group_mean(i, 3)
                offsets(i, 2, 27)
                pe.wait_ge(pooled_ready.sem, pooled_ready.at(i, 2))
                offset_parts(3, img[1], w1off)
                far(0)
                offsets(i, 3, 27)
                far(1)
                for s in range(2):
                    wait_apart(pe, (added, added.at(i, 2)), (far_ready, far_ready.at(i, s + 1)))
                    is_far = pe.value_load(flag[s][0:1, 0:1])
                    with pe.If(is_far > 0):
                        pe.wait_ge(g_strips.sem, g_strips.at(i, s + 1))
                        image_T(s, g_xTp)
                        wait_apart(pe, (g_xT, g_xT.at(i, s + 1)))
                        with pe.Fori(0, K9) as k:
                            pe.wait_ge(g_smp_sb.sem, g_smp_sb.at(i, K9 * s) + k)
                            dense(i, K9 * TILES * s + k * TILES, psO[1], xT[s], g_GT, g_GTt, g_Gd, g_smp)
                        pe.wait_ge(g_smp_sb.sem, g_smp_sb.at(i, K9 * (s + 1)))
                        for each in (n_blkp, n_Gp, n_smp):
                            pe.sem_inc(each.sem, STEPS)
                    with pe.Else():
                        pe.wait_ge(wide_ready.sem, wide_ready.at(i, s + 1))
                        near(i, s)
                        pe.wait_ge(n_smp_sb.sem, n_smp_sb.at(i, STEPS * (s + 1)))
                        pe.sem_inc(g_xTp.sem, 1)
                        pe.sem_inc(g_GTt.sem, K9 * TILES)
                        pe.sem_inc(g_smp.sem, K9 * TILES)
                    if s:
                        pe.wait_ge(added.sem, added.at(i, 3))
                    conv(psO[0], w1, lambda h, k: samp[:, k, HALF * h:HALF * h + HALF],
                         mid=(lambda: group_mean(i, 4)) if s else None)
                pe.wait_ge(xn_ready.sem, xn_ready.at(i, 5))
                conv(psO[1], w2, window(xn[0]), mid=lambda: group_mean(i, 5))
                pe.wait_ge(xn_ready.sem, xn_ready.at(i, 6))
                conv(psO[0], w2, window(xn[1]), mid=lambda: group_mean(i, 6))
                group_mean(i, 7)
                pe.wait_ge(xn_ready.sem, xn_ready.at(i, 8))
                pe.wait_ge(added.sem, added.at(i, 6))

                def img_rows(s, h):
                    return xn[s][:, PAD + 16 * h:PAD + 16 * h + 16, PAD:PAD + W]

                def product(n):
                    if n >= 3:
                        pe.wait_ge(l3_act.sem, l3_act.at(i, n - 2))
                    return psO[n % 2]

                d = product(1)
                for s in range(2):
                    for h in range(2):
                        last = mm(d[C2 * s:C2 * s + C2, h, :], win2T[:], img_rows(s, h), start=True, stop=True)
                last.then_inc(l3_product.sem, 1)
                d = product(2)
                for s in range(2):
                    for h in range(2):
                        last = mm(d[32 * s:32 * s + 32, h, :], wu[:, 32 * s:32 * s + 32], img_rows(s, h), start=True, stop=True)
                last.then_inc(l3_product.sem, 1)

                def whole(n, lhsT, rhs):
                    d = product(n)
                    for h in range(2):
                        last = mm(d[:, h, :], lhsT, rhs[:, HALF * h:HALF * h + HALF], start=True, stop=True)
                    last.then_inc(l3_product.sem, 1)

                pe.wait_ge(l3_act.sem, l3_act.at(i, 2))
                whole(3, cb2T[:], u3)
                for v in range(2):
                    pe.wait_ge(l3_dw.sem, l3_dw.at(i, v + 1))
                    for t in range(TAPS):
                        whole(4 + TAPS * v + t, (kh_w, kv_w)[v][:, t, :], dwo)
                pe.wait_ge(l3_wss.sem, l3_wss.at(i, 1))
                whole(14, wss[:], xc)
                whole(15, blk64, xc)
                pe.wait_ge(l3_maps.sem, l3_maps.at(i, 2))
                pe.wait_ge(l3_act.sem, l3_act.at(i, 14))
                pe.wait_ge(l3_csum.sem, l3_csum.at(i, 1))
                for s in range(2):
                    for h in range(2):
                        hh = slice(HALF * h, HALF * h + HALF)
                        mm(psO[s][:, h, :], woT[:, s, 0, :], sm[:, hh], start=True, stop=False)
                        last = mm(psO[s][:, h, :], wo2[:, s, :], at[:, hh], start=False, stop=True)
                    last.then_inc(l3_product.sem, 1)

        @block.scalar
        def _(act):
            def copy(out, in_):
                return nc.scalar.activation(out, in_, ACT.Copy)

            def dense(i, base, GTt, Gdr, smp):
                for t in range(TILES):
                    act.wait_ge(GTt.sem, GTt.at(i, base + t + 1))
                    if t >= 2:
                        act.wait_ge(smp.sem, smp.at(i, base + t - 1))
                    else:
                        act.wait_ge(smp.sem, smp.at(i, base))
                    copy(Gd[t % 2][:].rearrange("p q c -> p (q c)"),
                         psT[:].rearrange("p b c -> p (b c)")).then_inc(Gdr.sem, 1)

            def wide_windows(s):
                whole = img[s][:]
                return bass.AP(whole.tensor, whole.offset, [whole.ap[0], [SW, STRIPS], [PW, PW], [1, BC]])

            def normalise(i, n):
                s = n % 2
                act.wait_ge(affine_ready.sem, affine_ready.at(i, n + 1))
                src = (xin if n < 2 else x)[s]
                nc.scalar.activation(inner(xn[s]), src[:].rearrange("p (r c) -> p r c", c=W), ACT.Identity,
                                     bias=gst[s][:, 20:21], scale=gst[s][:, 19:20]).then_inc(xn_ready.sem, 1)

            def parts(i, n):
                s = n % 2
                act.wait_ge(parts_product.sem, parts_product.at(i, n + 1))
                for b in range(2):
                    last = copy(off_parts[s][:].rearrange("p (j b r c) -> p j b r c", b=2, j=STRIPS, c=SW)[:, :, b],
                                psO[s][:, b, :].rearrange("p (r j c) -> p j r c", j=STRIPS, c=SW))
                last.then_inc(parts_ready.sem, 1)

            act.wait_ge(borders_zero, 8)
            with act.Fori(0, PASSES) as i:
                for s in range(2):
                    normalise(i, s)
                for s in range(2):
                    parts(i, s)
                    act.wait_ge(xT_product.sem, xT_product.at(i, s + 1))
                    copy(xT[s][:].rearrange("p q c -> p (q c)"), psT[:].rearrange("p b c -> p (b c)"))\
                        .then_inc(xT_ready.sem, 1)
                for s in range(2):
                    act.wait_ge(om_ready.sem, om_ready.at(i, s + 1))
                    nc.scalar.activation(mk[s][:, 0:TILES], om0[s][:, 2, :], ACT.Sigmoid).then_inc(mask_ready.sem, 1)
                for s in range(2):
                    dense(i, TILES * s, GTt_ready, Gd_ready, sampled)
                    act.wait_ge(sampled.sem, sampled.at(i, TILES * (s + 1)))
                    for b in range(2):
                        last = copy(tiled(inner(img[s]), b), psO[s][:, b, :].rearrange("p (j r c) -> p j r c", j=2, c=SW))
                    last.then_inc(img_ready.sem, 1)
                for s in range(2):
                    normalise(i, 2 + s)
                for s in range(2):
                    parts(i, 2 + s)
                    act.wait_ge(pooled_ready.sem, pooled_ready.at(i, s + 1))
                    copy(strip12[s][:], wide_windows(s)).then_inc(wide_ready.sem, 1)
                for s in range(2):
                    act.wait_ge(om_ready.sem, om_ready.at(i, 3 + s))
                    nc.scalar.activation(mk[s][:], om[s][:, 2, :, :].rearrange("p t k -> p (t k)"), ACT.Sigmoid)\
                        .then_inc(mask_ready.sem, 1)
                for s in range(2):
                    wait_apart(act, (far_ready, far_ready.at(i, s + 1)))
                    far = act.value_load(flag[s][0:1, 0:1])
                    with act.If(far > 0):
                        act.wait_ge(g_xTp.sem, g_xTp.at(i, s + 1))
                        copy(xT[s][:].rearrange("p q c -> p (q c)"), psT[:].rearrange("p b c -> p (b c)"))\
                            .then_inc(g_xT.sem, 1)
                        with act.Fori(0, K9) as k:
                            dense(i, K9 * TILES * s + k * TILES, g_GTt, g_Gd, g_smp)
                            act.wait_ge(g_smp.sem, g_smp.at(i, K9 * TILES * s + k * TILES + TILES))
                            tap = samp[:, bass.ds(k, 1), :].rearrange("p k (r c) -> p (k r) c", c=W)
                            for b in range(2):
                                last = copy(tiled(tap, b), psO[1][:, b, :].rearrange("p (j r c) -> p j r c", j=2, c=SW))
                            last.then_inc(g_smp_sb.sem, 1)
                        act.wait_ge(g_smp_sb.sem, g_smp_sb.at(i, K9 * (s + 1)))
                        act.sem_inc(n_G.sem, STEPS)
                        act.sem_inc(n_smp_sb.sem, STEPS)
                    with act.Else():
                        for n in range(STEPS + 1):
                            if n < STEPS:
                                o = STEPS * s + n
                                act.wait_ge(n_Gp.sem, n_Gp.at(i, o + 1))
                                if o >= 2:
                                    act.wait_ge(n_smp.sem, n_smp.at(i, o - 1))
                                copy(G1[n % 2][:].rearrange("p k c -> p (k c)"), psT[0:BLK, 0, 0:3 * C])\
                                    .then_inc(n_G.sem, 1)
                            if n:
                                p = n - 1
                                t, ki = p // 3, p % 3
                                act.wait_ge(n_smp.sem, n_smp.at(i, STEPS * s + p + 1))
                                r0, c0 = 16 * (t % 2), SW * (t // 2)
                                copy(samp[:, 3 * ki:3 * ki + 3, :].rearrange("p k (r c) -> p k r c", c=W)
                                     [:, :, r0:r0 + 16, c0:c0 + SW],
                                     psO[1][:, p % 2, 0:3 * C].rearrange("p (k r c) -> p k r c", k=3, c=SW))\
                                    .then_inc(n_smp_sb.sem, 1)
                        act.wait_ge(n_smp_sb.sem, n_smp_sb.at(i, STEPS * (s + 1)))
                        act.sem_inc(g_xT.sem, 1)
                        act.sem_inc(g_Gd.sem, K9 * TILES)
                        act.sem_inc(g_smp_sb.sem, K9)
                for n in range(4, 8):
                    normalise(i, n)
                act.wait_ge(l3_product.sem, l3_product.at(i, 1))
                nc.scalar.activation(x2p[:, :, LPAD:LPAD + W], psO[1][:].rearrange("p b (r c) -> p (b r) c", c=W),
                                     ACT.Identity, bias=vec[:, V_BIN2:V_BIN2 + 1]).then_inc(l3_act.sem, 1)
                act.wait_ge(l3_product.sem, l3_product.at(i, 2))
                nc.scalar.activation(u3[0:C2], psO[0][0:C2].rearrange("p b c -> p (b c)"), ACT.Relu,
                                     bias=bu[:]).then_inc(l3_act.sem, 1)
                act.wait_ge(l3_product.sem, l3_product.at(i, 3))
                nc.scalar.activation(xc[:], psO[1][:].rearrange("p b c -> p (b c)"), ACT.Identity,
                                     bias=vec[:, V_BCB2:V_BCB2 + 1]).then_inc(l3_act.sem, 1)
                for v in range(2):
                    for t in range(TAPS):
                        n = 4 + TAPS * v + t
                        act.wait_ge(l3_product.sem, l3_product.at(i, n))
                        b = (V_KHB, V_KVB)[v] + t
                        nc.scalar.activation(kern[:, t, :], psO[n % 2][:].rearrange("p b c -> p (b c)"), ACT.Tanh,
                                             bias=vec[:, b:b + 1]).then_inc(l3_act.sem, 1)
                act.wait_ge(l3_product.sem, l3_product.at(i, 14))
                nc.scalar.activation(sg, psO[0][:].rearrange("p b c -> p (b c)"), ACT.Sigmoid)\
                    .then_inc(l3_act.sem, 1)
                act.wait_ge(l3_csum.sem, l3_csum.at(i, 1))
                nc.scalar.activation(st3[:, 2:3], st3[:, 1:2], ACT.Sigmoid, scale=1.0 / N).then_inc(l3_csig.sem, 1)

        @block.vector
        def _(dve):
            v_ = nc.vector
            dve.wait_ge(consts_landed, CONSTS * 16)
            for k in range(K9):
                v_.tensor_scalar(w0[:, k, :], pwT[:], vec[:, V_DW0 + k:V_DW0 + k + 1], None, ALU.mult)
            dve.wait_ge(prep, 2)
            v_.tensor_copy(wu[:], ps[0][:, 0:C2])
            v_.tensor_tensor(bu[:], ps[1][0:C2, 0:1], vec[0:C2, V_BCB1:V_BCB1 + 1], ALU.add)
            dve.wait_ge(w2_landed, 32)
            n2 = K9 * C
            f2 = w2[:].rearrange("p k o -> p (k o)")
            flat = samp[:].rearrange("p a b -> p (a b)")
            r2, sgn, t2, neg = (flat[:, n * n2:(n + 1) * n2] for n in range(4))
            v_.tensor_scalar(sgn, f2, 0.0, None, ALU.is_gt)
            v_.tensor_scalar(neg, f2, 0.0, None, ALU.is_lt)
            v_.tensor_scalar(t2, r2, 0.5, 0.7, ALU.is_gt, ALU.mult).then_inc(prep_dve, 1)
            dve.wait_ge(prep_dve, 1)
            v_.tensor_tensor(sgn, sgn, neg, ALU.subtract)
            v_.tensor_scalar(r2, r2, 0.5, 0.175, ALU.is_lt, ALU.mult).then_inc(prep_dve, 1)
            dve.wait_ge(prep_dve, 2)
            v_.tensor_tensor(t2, t2, r2, ALU.add).then_inc(prep_dve, 1)
            dve.wait_ge(prep_dve, 3)
            v_.tensor_tensor(t2, t2, sgn, ALU.mult).then_inc(prep_dve, 1)
            dve.wait_ge(prep_dve, 4)
            v_.scalar_tensor_tensor(f2, f2, 0.5, t2, ALU.mult, ALU.add).then_inc(weights_ready, 1)
            dve.wait_ge(weights_ready, 1)
            dve.wait_ge(borders_zero, 8)

            with dve.Fori(0, PASSES) as i:
                own = Own(dve, dve_own, i)

                def stats(n, src):
                    g = gst[n % 2]
                    for h in range(2):
                        own.step(v_.bn_stats(g[:, 6 * h:6 * h + 6], src[:, HALF * h:HALF * h + HALF]))
                    wait_apart(dve, (dve_own, dve_own.at(i, own.n)))
                    own.step(v_.bn_aggr(g[:, 12:14], g[:, 0:12]))
                    own.settle()
                    v_.scalar_tensor_tensor(g[:, 13:14], g[:, 12:13], g[:, 12:13], g[:, 13:14], ALU.mult, ALU.add)\
                        .then_inc(stats_ready.sem, 1)

                def affine(n):
                    g = gst[n % 2]
                    dve.wait_ge(group_ready.sem, group_ready.at(i, n + 1))
                    own.step(v_.tensor_copy(g[:, 14:16], ps[n % 2][:, 0:2]))
                    own.settle()
                    own.step(v_.scalar_tensor_tensor(g[:, 16:17], g[:, 14:15], g[:, 14:15], g[:, 15:16],
                                                     ALU.mult, ALU.subtract))
                    own.settle()
                    v_.tensor_scalar(g[:, 17:18], g[:, 16:17], -1.0, EPS, ALU.mult, ALU.add)\
                        .then_inc(var_ready.sem, 1)
                    dve.wait_ge(rstd_ready.sem, rstd_ready.at(i, n + 1))
                    own.step(v_.tensor_scalar(g[:, 19:20], g[:, 18:19], 1.0 / 9 if n // 2 == 1 else 1.0, None, ALU.mult))
                    own.settle()
                    v_.tensor_scalar(g[:, 20:21], g[:, 14:15], g[:, 19:20], -1.0, ALU.mult, ALU.mult)\
                        .then_inc(affine_ready.sem, 1)

                def hats_dense(s, settle, step, uv, mask, gain):
                    h = hat[s]
                    step(v_.tensor_tensor(h[:], iota32.unsqueeze(1).broadcast_to((C, 2 * TILES, 32)),
                                          uv.broadcast_to((C, 2 * TILES, 32)), ALU.subtract))
                    settle()
                    step(v_.scalar_tensor_tensor(h[:], h[:], -1.0, h[:], ALU.mult, ALU.max))
                    settle()
                    step(v_.tensor_scalar(h[:], h[:], 1.0, 0.0, ALU.subtract, ALU.min))
                    settle()
                    step(v_.scalar_tensor_tensor(h[:, TILES:], h[:, TILES:], gain, mask.broadcast_to((C, TILES, 32)),
                                                 ALU.mult, ALU.mult))
                    settle()

                def dense(i_, base, s, GTr, GTt):
                    for t in range(TILES):
                        dve.wait_ge(GTt.sem, GTt.at(i_, base + (t - 1 if t >= 2 else 0)))
                        v_.tensor_tensor(GT[t % 2][:].rearrange("p (j a b) -> p j a b", j=STRIPS, b=SW),
                                         hat[s][:, t, :].unsqueeze(1).unsqueeze(3).broadcast_to((C, STRIPS, H, SW)),
                                         hat[s][:, TILES + t, :].rearrange("p (j b) -> p j b", b=SW).unsqueeze(2)
                                         .broadcast_to((C, STRIPS, H, SW)), ALU.mult).then_inc(GTr.sem, 1)

                for s in range(2):
                    dve.wait_ge(x_landed[s].sem, x_landed[s].at(i, 16))
                    stats(s, xin[s])
                for s in range(2):
                    affine(s)

                def tile_order(s, src):
                    return v_.tensor_copy(q_strips[s][:].rearrange("p (j r c) -> p j r c", j=STRIPS, c=SW),
                                          inner(src).rearrange("p r (j c) -> p j r c", c=SW))

                for s in range(2):
                    dve.wait_ge(xn_ready.sem, xn_ready.at(i, s + 1))
                    tile_order(s, xn[s]).then_inc(strips_ready.sem, 1)
                for s in range(2):
                    dve.wait_ge(offs_ready.sem, offs_ready.at(i, s + 1))
                    v_.tensor_tensor(om0[s][:].rearrange("p g t -> p t g"),
                                     ps[s][:, 4:4 + 3 * TILES].rearrange("p (t g) -> p t g", g=3),
                                     offb[:, 27:30].unsqueeze(1).broadcast_to((C, TILES, 3)), ALU.add)\
                        .then_inc(om_ready.sem, 1)
                for s in range(2):
                    dve.wait_ge(om_ready.sem, om_ready.at(i, s + 1))
                    o2 = om0[s][:, 0:2, :].rearrange("p g t -> p (g t)")
                    own.step(v_.scalar_tensor_tensor(o2, o2, 2.0 / W, tab[:, T_LIN:T_LIN + 2 * TILES], ALU.mult, ALU.add))
                    own.settle()
                    own.step(v_.tensor_scalar(o2, o2, 1.0, 0.5 * (W - 1), ALU.add, ALU.mult))
                    own.settle()
                    dve.wait_ge(mask_ready.sem, mask_ready.at(i, s + 1))
                    hats_dense(s, own.settle, own.step, o2.unsqueeze(2), mk[s][:, 0:TILES].unsqueeze(2), 1.0)
                for s in range(2):
                    dense(i, TILES * s, s, GT_ready, GTt_ready)
                for s in range(2):
                    dve.wait_ge(conv_ready.sem, conv_ready.at(i, s + 1))
                    v_.tensor_tensor(x[s][:], psO[s][:].rearrange("p b c -> p (b c)"), xin[s][:], ALU.add)\
                        .then_inc(added.sem, 1)
                    dve.wait_ge(added.sem, added.at(i, s + 1))
                    stats(2 + s, x[s])
                    affine(2 + s)
                    dve.wait_ge(xn_ready.sem, xn_ready.at(i, 3 + s))
                    a, b, o = xn[s], pool_v, inner(img[s])
                    cols = slice(PAD - 1, PAD + W + 1)
                    own.step(v_.tensor_tensor(b[:], a[:, PAD - 1:PAD - 1 + H, cols], a[:, PAD:PAD + H, cols], ALU.add))
                    own.settle()
                    own.step(v_.tensor_tensor(b[:], b[:], a[:, PAD + 1:PAD + 1 + H, cols], ALU.add))
                    own.settle()
                    own.step(v_.tensor_tensor(o, b[:, :, 0:W], b[:, :, 1:W + 1], ALU.add))
                    own.settle()
                    v_.tensor_tensor(o, o, b[:, :, 2:W + 2], ALU.add).then_inc(pooled_ready.sem, 1)
                for s in range(2):
                    dve.wait_ge(offs_ready.sem, offs_ready.at(i, 3 + s))
                    v_.tensor_tensor(om[s][:].rearrange("p g t k -> p t g k"),
                                     ps[s][:, 4:4 + 27 * TILES].rearrange("p (t g k) -> p t g k", g=3, k=K9),
                                     offb[:, 0:27].rearrange("p (g k) -> p g k", k=K9).unsqueeze(1)
                                     .broadcast_to((C, TILES, 3, K9)), ALU.add).then_inc(om_ready.sem, 1)
                    dve.wait_ge(om_ready.sem, om_ready.at(i, 3 + s))
                    own.step(v_.tensor_reduce(out=flagf[s][:, 1:2], in_=om[s][:, 0:2].rearrange("p g t k -> p (g t k)"),
                                              op=ALU.max, axis=AX.X, apply_absolute_value=True))
                    own.settle()
                    v_.tensor_scalar(flagf[s][:, 0:1], flagf[s][:, 1:2], NEAR, None, ALU.is_gt)\
                        .then_inc(far_input.sem, 1)
                    dve.wait_ge(far_count.sem, far_count.at(i, s + 1))
                    v_.tensor_copy(flag[s][:], ps[s][:, 2:3]).then_inc(far_ready.sem, 1)
                for s in range(2):
                    wait_apart(dve, (far_ready, far_ready.at(i, s + 1)), (mask_ready, mask_ready.at(i, 3 + s)))
                    far = dve.value_load(flag[s][0:1, 0:1])
                    with dve.If(far > 0):
                        count = [0]
                        tap = [None]

                        def gstep(ins):
                            ins.then_inc(g_own.sem, 1)
                            count[0] += 1

                        def gsettle():
                            v = g_own.at(i, G_OWN * s + count[0])
                            dve.wait_ge(g_own.sem, v if tap[0] is None else v + tap[0] * 4)

                        tile_order(s, img[s]).then_inc(g_strips.sem, 1)
                        o2 = om[s][:, 0:2].rearrange("p g t k -> p (g t k)")
                        gstep(v_.tensor_tensor(o2, o2, tab[:, T_POS:T_POS + 2 * TILES * K9], ALU.add))
                        wait_apart(dve, (g_own, g_own.at(i, G_OWN * s + count[0])))
                        with dve.Fori(0, K9) as k:
                            tap[0] = k
                            dve.wait_ge(g_GTt.sem, g_GTt.at(i, K9 * TILES * s + k * TILES))
                            uv = om[s][:, 0:2].rearrange("p g t k -> p (g t) k")[:, :, bass.ds(k, 1)]
                            m = mk[s][:].rearrange("p (t k) -> p t k", k=K9)[:, :, bass.ds(k, 1)]
                            hats_dense(s, gsettle, gstep, uv, m, 2.0)
                            dense(i, K9 * TILES * s + k * TILES, s, g_GT, g_GTt)
                        assert count[0] == 5
                        dve.wait_ge(g_GTt.sem, g_GTt.at(i, K9 * TILES * (s + 1)))
                        dve.sem_inc(n_own.sem, N_OWN)
                        dve.sem_inc(n_GT.sem, STEPS)
                        dve.sem_inc(n_blk.sem, STEPS)
                    with dve.Else():
                        cnt = [0]

                        def nstep(ins):
                            ins.then_inc(n_own.sem, 1)
                            cnt[0] += 1

                        def nsettle():
                            dve.wait_ge(n_own.sem, n_own.at(i, N_OWN * s + cnt[0]))

                        TK = TILES * K9
                        dyx = om[s][:].rearrange("p g t k -> p g (t k)")
                        nstep(v_.tensor_tensor(hfy[s][:], tab[:, T_EY:T_EY + BR].unsqueeze(1).broadcast_to((C, TK, BR)),
                                               dyx[:, 0, :].unsqueeze(2).broadcast_to((C, TK, BR)), ALU.subtract))
                        nstep(v_.tensor_tensor(
                            hfx[s][:].rearrange("p (t k) b -> p t k b", k=K9),
                            tab[:, T_EX:T_EX + K9 * BC].rearrange("p (k b) -> p k b", b=BC).unsqueeze(1)
                            .broadcast_to((C, TILES, K9, BC)),
                            om[s][:, 1].unsqueeze(3).broadcast_to((C, TILES, K9, BC)), ALU.subtract))
                        nsettle()
                        for hf in (hfy[s], hfx[s]):
                            nstep(v_.scalar_tensor_tensor(hf[:], hf[:], -1.0, hf[:], ALU.mult, ALU.max))
                        nsettle()
                        for hf in (hfy[s], hfx[s]):
                            nstep(v_.tensor_scalar(hf[:], hf[:], 1.0, 0.0, ALU.subtract, ALU.min))
                        nsettle()
                        nstep(v_.scalar_tensor_tensor(hfx[s][:], hfx[s][:], 2.0,
                                                      mk[s][:].unsqueeze(2).broadcast_to((C, TK, BC)),
                                                      ALU.mult, ALU.mult))
                        nsettle()
                        assert cnt[0] == N_OWN
                        hy = hfy[s][:].rearrange("p (t k) a -> p t k a", k=K9)
                        hx = hfx[s][:].rearrange("p (t k) b -> p t k b", k=K9)
                        for n in range(STEPS + 1):
                            if n < STEPS:
                                t, ki = n // 3, n % 3
                                o = STEPS * s + n
                                if o >= 2:
                                    dve.wait_ge(n_Gp.sem, n_Gp.at(i, o - 1))
                                three = slice(3 * ki, 3 * ki + 3)
                                v_.tensor_tensor(GT1[n % 2][:].rearrange("p k (a b) -> p k a b", b=BC),
                                                 hy[:, t, three, :].unsqueeze(3).broadcast_to((C, 3, BR, BC)),
                                                 hx[:, t, three, :].unsqueeze(2).broadcast_to((C, 3, BR, BC)),
                                                 ALU.mult).then_inc(n_GT.sem, 1)
                            if n:
                                p = n - 1
                                dve.wait_ge(n_blkp.sem, n_blkp.at(i, STEPS * s + p + 1))
                                if STEPS * s + p >= 2:
                                    dve.wait_ge(n_smp.sem, n_smp.at(i, STEPS * s + p - 1))
                                v_.tensor_copy(xblk[p % 2][:].rearrange("p h c -> p (h c)"),
                                               psT[0:BLK, 1, 0:2 * C]).then_inc(n_blk.sem, 1)
                        dve.wait_ge(n_blk.sem, n_blk.at(i, STEPS * (s + 1)))
                        dve.sem_inc(g_strips.sem, 1)
                        dve.sem_inc(g_own.sem, G_OWN)
                        dve.sem_inc(g_GT.sem, K9 * TILES)
                for s in range(2):
                    dve.wait_ge(conv_ready.sem, conv_ready.at(i, 3 + s))
                    v_.scalar_tensor_tensor(x[s][:], psO[0][:].rearrange("p b c -> p (b c)"),
                                            vec[:, V_B1:V_B1 + 1], x[s][:], ALU.add, ALU.add).then_inc(added.sem, 1)
                    dve.wait_ge(added.sem, added.at(i, 3 + s))
                    stats(4 + s, x[s])
                    affine(4 + s)
                for s in range(2):
                    dve.wait_ge(conv_ready.sem, conv_ready.at(i, 5 + s))
                    v_.scalar_tensor_tensor(x[s][:], psO[1 - s][:].rearrange("p b c -> p (b c)"),
                                            vec[:, V_B2:V_B2 + 1], x[s][:], ALU.add, ALU.add).then_inc(added.sem, 1)
                    dve.wait_ge(added.sem, added.at(i, 5 + s))
                    stats(6 + s, x[s])
                    affine(6 + s)
                img3 = lambda t: t[:, :].rearrange("p (r c) -> p r c", c=W)
                for v in range(2):
                    src, rows, cols = ((x2p, H, LW), (ahp, H + 2 * LPAD, W))[v]

                    def shifted(t, d, v=v):
                        return t[:, :, d:d + W] if v == 0 else t[:, d:d + H, :]

                    if v == 0:
                        dve.wait_ge(l3_act.sem, l3_act.at(i, 1))
                    else:
                        dve.wait_ge(l3_product.sem, l3_product.at(i, 3 + TAPS))
                    w_at = (V_DWH, V_DWV)[v]
                    b_at = (V_DWHB, V_DWVB)[v]
                    own.step(v_.tensor_scalar(img3(dwo), shifted(src, 0), vec[:, w_at:w_at + 1],
                                              vec[:, b_at:b_at + 1], ALU.mult, ALU.add))
                    for d in range(1, 7):
                        own.settle()
                        ins = v_.scalar_tensor_tensor(img3(dwo), shifted(src, d), vec[:, w_at + d:w_at + d + 1],
                                                      img3(dwo), ALU.mult, ALU.add)
                        if d < 6:
                            own.step(ins)
                        else:
                            ins.then_inc(l3_dw.sem, 1)
                    if v == 0:
                        pair = psum2[:, 0:H * (LW - 1)].rearrange("p (r c) -> p r c", c=LW - 1)
                        own.step(v_.tensor_tensor(pair, src[:, :, 0:LW - 1], src[:, :, 1:LW], ALU.add))
                        taps = [pair[:, :, 0:W], shifted(src, 2), shifted(src, 3), shifted(src, 4), pair[:, :, 5:5 + W]]
                    else:
                        pair = psum2[:, 0:(rows - 1) * W].rearrange("p (r c) -> p r c", c=W)
                        own.step(v_.tensor_tensor(pair, src[:, 0:rows - 1, :], src[:, 1:rows, :], ALU.add))
                        taps = [pair[:, 0:H, :], shifted(src, 2), shifted(src, 3), shifted(src, 4), pair[:, 5:5 + H, :]]
                    out = ahp[:, LPAD:LPAD + H, :] if v == 0 else img3(at)
                    own.settle()
                    for t in range(TAPS):
                        dve.wait_ge(l3_act.sem, l3_act.at(i, 4 + TAPS * v + t))
                        kt = kern[:, t, :].rearrange("p (r c) -> p r c", c=W)
                        dst = out if t == 0 else img3(tmp3)
                        own.step(v_.scalar_tensor_tensor(dst, taps[t], 0.5 if t in (0, 4) else 1.0, kt,
                                                         ALU.mult, ALU.mult))
                        own.settle()
                        if t:
                            if t == 4 and v == 1:
                                own.step(v_.scalar_tensor_tensor(out, out, 1.0, img3(tmp3), ALU.mult, ALU.add,
                                                                 accum_out=st3[:, 0:1]))
                            else:
                                own.step(v_.tensor_tensor(out, out, img3(tmp3), ALU.add))
                            own.settle()
                v_.tensor_scalar(wss[:], blk64, st3[:, 0:1], 1.0 / N, ALU.mult, ALU.mult).then_inc(l3_wss.sem, 1)
                dve.wait_ge(l3_product.sem, l3_product.at(i, 15))
                v_.scalar_tensor_tensor(tmp3, at[:], 1.0, psO[1][:].rearrange("p b c -> p (b c)"),
                                        ALU.mult, ALU.mult, accum_out=st3[:, 1:2]).then_inc(l3_csum.sem, 1)
                dve.wait_ge(l3_act.sem, l3_act.at(i, 14))
                v_.tensor_tensor(sm, sg, xc[:], ALU.mult).then_inc(l3_maps.sem, 1)
                dve.wait_ge(l3_csig.sem, l3_csig.at(i, 1))
                v_.tensor_scalar(wo2, woT[:, :, 1, :], st3[:, 2:3], None, ALU.mult).then_inc(l3_maps.sem, 1)
                for s in range(2):
                    dve.wait_ge(l3_product.sem, l3_product.at(i, 16 + s))
                    dve.wait_ge(yout_free.sem, yout_free.at(i, 0))
                    v_.scalar_tensor_tensor(yout[s][:], psO[s][:].rearrange("p b c -> p (b c)"),
                                            vec[:, V_BOUT:V_BOUT + 1], x[s][:], ALU.add, ALU.add)\
                        .then_inc(y_ready.sem, 1)
                assert own.n == DVE_STEPS, own.n


def tables():
    import numpy as np

    tab = np.zeros((C, TAB_N), np.float32)
    p = np.arange(C)
    row, col = p // SW, p % SW
    t = np.arange(TILES)
    y = 16 * (t % 2)[None, :] + row[:, None]
    x = SW * (t // 2)[None, :] + col[:, None]
    k = np.arange(K9)
    tab[:, T_IOTA:T_IOTA + 32] = np.arange(32)
    tab[:, T_GAVG:T_GAVG + C] = (p[:, None] // GROUP == p[None, :] // GROUP) / GROUP
    tab[:, T_ONES:T_ONES + C] = 1
    tab[:, T_BLK:T_BLK + C] = (p[:, None] // C2 == p[None, :] // C2) / C2
    line = np.linspace(-1, 1, W, dtype=np.float32)
    tab[:, T_LIN:T_LIN + 2 * TILES] = np.concatenate([line[y], line[x]], 1)
    pos = np.stack([y[:, :, None] + k // 3 - 1, x[:, :, None] + k % 3 - 1], 1)
    tab[:, T_POS:T_POS + 2 * TILES * K9] = pos.reshape(C, -1)
    tab[:, T_EY:T_EY + BR] = np.arange(BR)[None, :] - (row % 8)[:, None] - 1
    ex = np.arange(BC)[None, None, :] - col[:, None, None] - (k % 3)[None, :, None] - 1
    tab[:, T_EX:T_EX + K9 * BC] = ex.reshape(C, -1)
    tab[:, T_SEL:T_SEL + 32] = p[:, None] % 32 == np.arange(32)
    return tab


def layout(a):
    import numpy as np

    wide = lambda w: np.concatenate([w, np.zeros((32 - len(w),) + w.shape[1:], w.dtype)])
    both = lambda v: np.concatenate([v, v])
    taps = lambda w: np.ascontiguousarray(w.transpose(1, 2, 3, 0).reshape(w.shape[1], K9, w.shape[0]))

    def diagonal(w):
        z = np.zeros((2, w.shape[0], 2, w.shape[1]), np.float32)
        z[0, :, 0] = w
        z[1, :, 1] = w
        return z.reshape(2 * w.shape[0], 2 * w.shape[1])

    def output_weights(w):
        z = np.zeros((2, C2, 2, 2, C), np.float32)
        for s in range(2):
            for m in range(2):
                z[s, :, s, m] = w[C2 * m:C2 * m + C2]
        return z.reshape(C, 2, 2, C)

    def strip(w, b):
        heads = np.arange(C2) // (C2 // 8)
        ws = np.stack([diagonal(w[heads * TAPS + t].T) for t in range(TAPS)], 1)
        return np.ascontiguousarray(ws), np.stack([both(b[heads * TAPS + t]) for t in range(TAPS)], 1)

    kh, khb = strip(a["L3_conv_hk_pw_w"], a["L3_conv_hk_pw_b"])
    kv, kvb = strip(a["L3_conv_vk_pw_w"], a["L3_conv_vk_pw_b"])
    bin_ = a["L3_conv_proj_in_b"]
    cb1 = a["L3_conv_cb_b1"]
    vec = np.zeros((C, V_N), np.float32)
    vec[:, V_B1] = a["L1_conv_b"]
    vec[:, V_B2] = a["L2_conv_bias"]
    vec[:, V_BIN1] = both(bin_[:C2])
    vec[:, V_BIN2] = both(bin_[C2:])
    vec[:, V_BCB1] = both(both(cb1))
    vec[:, V_BCB2] = both(a["L3_conv_cb_b2"])
    vec[:, V_BOUT] = a["L3_conv_proj_out_b"]
    vec[:, V_DWHB] = both(a["L3_conv_hk_dw_b"])
    vec[:, V_DWVB] = both(a["L3_conv_vk_dw_b"])
    vec[:, V_DWH:V_DWH + 7] = both(a["L3_conv_hk_dw_w"].reshape(C2, 7))
    vec[:, V_DWV:V_DWV + 7] = both(a["L3_conv_vk_dw_w"].reshape(C2, 7))
    vec[:, V_KHB:V_KHB + TAPS] = khb
    vec[:, V_KVB:V_KVB + TAPS] = kvb
    vec[:, V_DW0:V_DW0 + K9] = a["L0_conv_w_dw"].reshape(C, K9)

    off = np.arange(2 * K9).reshape(K9, 2).T.reshape(-1)
    w1off = np.concatenate([a["L1_conv_off_w"][off], a["L1_conv_mod_w"]])
    b1off = np.concatenate([a["L1_conv_off_b"][off], a["L1_conv_mod_b"], a["L0_conv_b_off"]])
    x = a["x"]
    wo = a["L3_conv_proj_out_w"].T
    return {
        "x": x.reshape(x.shape[0], C, N),
        "ident": np.eye(C, dtype=np.float32),
        "tab": tables(),
        "vec": vec,
        "offb": np.ascontiguousarray(np.broadcast_to(b1off, (C, 30))),
        "w0off": taps(wide(a["L0_conv_w_off"])),
        "pwT": a["L0_conv_w_pw"].reshape(C, C).T,
        "w1off": taps(wide(w1off)),
        "w1": taps(a["L1_conv_w"]),
        "w2": taps(a["L2_conv_weight"]),
        "r2": taps(a["L2_conv_r_matrix"]).reshape(C, K9 * C),
        "win": a["L3_conv_proj_in_w"][:C2],
        "win2T": a["L3_conv_proj_in_w"][C2:].T,
        "cb1T": both(a["L3_conv_cb_w1"]).T,
        "cb2T": np.concatenate([diagonal(a["L3_conv_cb_w2"].T), np.zeros((C2, C), np.float32)]),
        "kh": kh,
        "kv": kv,
        "woT": output_weights(wo),
    }


def kernel(**inputs):
    import numpy as np
    import concourse.bacc as bacc
    from concourse.bass_utils import run_bass_kernel_spmd

    arrays = {k: np.ascontiguousarray(v) for k, v in layout({k: np.asarray(v) for k, v in inputs.items()}).items()}
    nc = bacc.Bacc("TRN2", target_bir_lowering=False, num_devices=1)
    args = [nc.dram_tensor(f"in_{k}", v.shape, mybir.dt.from_np(v.dtype), kind="ExternalInput").ap()
            for k, v in arrays.items()]
    out = nc.dram_tensor("out", arrays["x"].shape, F32, kind="ExternalOutput").ap()
    conv_preact_kernel(nc, *args, out)
    r = run_bass_kernel_spmd(nc, [{f"in_{k}": v for k, v in arrays.items()}], core_ids=[0])
    return r.results[0]["out"].reshape(inputs["x"].shape)
```

```python
from contextlib import ExitStack

import concourse.bass as bass
from concourse import mybir

F32 = mybir.dt.float32
I32 = mybir.dt.int32
ALU = mybir.AluOpType
ACT = mybir.ActivationFunctionType
AX = mybir.AxisListType

C = 128
H = W = 32
N = H * W
HALF = 512
PAD = 2
PW = W + 2 * PAD
TILES = 8
STRIPS = 4
SW = W // STRIPS
K9 = 9
GROUP = 4
EPS = 1e-5
BR, BC = 10, 12
BLK = BR * BC
C2 = 64
TAPS = 5
LPAD = 3
LW = W + 2 * LPAD

V_B1, V_B2, V_BIN1, V_BIN2, V_BCB1, V_BCB2, V_BOUT, V_DWHB, V_DWVB = range(9)
V_DWH, V_DWV = 9, 16
V_KHB, V_KVB = 23, 28
V_DW0 = 33
V_N = 42

T_IOTA = 0
T_GAVG = T_IOTA + 32
T_ONES = T_GAVG + C
T_BLK = T_ONES + C
T_LIN = T_BLK + C
T_POS = T_LIN + 2 * TILES
T_EY = T_POS + 2 * TILES * K9
T_EX = T_EY + BR
T_SEL = T_EX + K9 * BC
T_ORG = T_SEL + 32
TAB_N = T_ORG + 2 * TILES
NEAR0, NEAR = 2.0, 1.0
CONSTS = 15
DVE_STEPS = 76
START_STEPS = 30


class Signal:

    def __init__(self, sem, per_pass, start=1):
        self.sem, self.per_pass, self.start = sem, per_pass, start

    def at(self, i, n):
        assert self.start or n
        return i * self.per_pass + n + self.start


class Own:

    def __init__(self, eng, steps, i):
        self.eng, self.steps, self.i, self.n = eng, steps, i, 0

    def step(self, ins):
        ins.then_inc(self.steps.sem, 1)
        self.n += 1

    def settle(self):
        self.eng.wait_ge(self.steps.sem, self.steps.at(self.i, self.n))


def conv_preact_kernel(nc, x_d, ident_d, tab_d, vec_d, offb_d, w0off_d, w0dw_pw_d, w1off_d, w1_d, w2_d, r2_d,
                       win_d, win2T_d, cb1T_d, cb2T_d, kh_d, kv_d, woT_d, out_d):
    PASSES = x_d.shape[0] // 2
    with ExitStack() as ctx:
        def sb(name, shape, dt=F32):
            return ctx.enter_context(nc.sbuf_tensor(name, shape, dt))

        def sem(name):
            return ctx.enter_context(nc.semaphore(name))

        signals = []

        def signal(name, per_pass):
            signals.append(Signal(sem(name), per_pass))
            return signals[-1]

        ident = sb("ident", [C, C])
        tab = sb("tab", [C, TAB_N])
        vec = sb("vec", [C, V_N])
        offb = sb("offb", [C, 30])
        w0off = sb("w0off", [C, K9, 32])
        pwT = sb("pwT", [C, C])
        w0 = sb("w0", [C, K9, C])
        w1off = sb("w1off", [C, K9, 32])
        w1 = sb("w1", [C, K9, C])
        w2 = sb("w2", [C, K9, C])
        win = sb("win", [C2, C])
        win2T = sb("win2T", [C, C2])
        cb1T = sb("cb1T", [C2, C2])
        cb2T = sb("cb2T", [C, C])
        kh_w = sb("kh_w", [C, TAPS, C])
        kv_w = sb("kv_w", [C, TAPS, C])
        woT = sb("woT", [C, 2, 2, C])
        wu = sb("wu", [C, C2])
        bu = sb("bu", [C2, 1])

        xin = [sb(f"xin{s}", [C, N]) for s in range(2)]
        x = [sb(f"x{s}", [C, N]) for s in range(2)]
        yout = [sb(f"yout{s}", [C, N]) for s in range(2)]
        xn = [sb(f"xn{s}", [C, PW, PW]) for s in range(2)]
        img = [sb(f"img{s}", [C, PW, PW]) for s in range(2)]
        gst = [sb(f"gst{s}", [C, 24]) for s in range(2)]
        om = [sb(f"om{s}", [C, 3, TILES, K9]) for s in range(2)]
        om0 = [sb(f"om0{s}", [C, 3, TILES]) for s in range(2)]
        mk = [sb(f"mk{s}", [C, TILES * K9]) for s in range(2)]
        xT = [sb(f"xT{s}", [C, TILES, C]) for s in range(2)]
        hat = [sb(f"hat{s}", [C, 2 * TILES, 32]) for s in range(2)]
        hfy = [sb(f"hfy{s}", [C, TILES * K9, BR]) for s in range(2)]
        hfx = [sb(f"hfx{s}", [C, TILES * K9, BC]) for s in range(2)]
        pool_v = sb("pool_v", [C, H, W + 2])
        neg_half = sb("neg_half", [C, 1])
        GTs = sb("GTs", [C, 2, N])
        GT = [GTs[:, b, :] for b in range(2)]
        Gd = [sb(f"Gd{b}", [C, TILES, C]) for b in range(2)]
        GT1 = [sb(f"GT1{b}", [C, 3, BLK]) for b in range(2)]
        G1 = [sb(f"G1{b}", [BLK, 3, C]) for b in range(2)]
        xblk = [sb(f"xblk{b}", [BLK, 2, C]) for b in range(2)]
        samp = sb("samp", [C, K9, N])
        off_parts = [Gd[s][:].rearrange("p q c -> p (q c)") for s in range(2)]
        q_strips = [sb(f"q_strips{s}", [C, N]) for s in range(2)]
        strip12 = [sb(f"strip12{s}", [C, STRIPS, PW, BC]) for s in range(2)]
        flag = [sb(f"flag{s}", [C, 1], I32) for s in range(2)]
        flagf = [sb(f"flagf{s}", [C, 2]) for s in range(2)]
        x2p = sb("x2p", [C, H, LW])
        ahp = sb("ahp", [C, H + 2 * LPAD, W])
        kern, dwo, tmp3, sg, sm = samp[:, 0:TAPS, :], *(samp[:, TAPS + n, :] for n in range(4))
        psum2 = GTs[:].rearrange("p b q -> p (b q)")
        u3 = sb("u3", [C, N])
        xc = sb("xc", [C, N])
        at = sb("at", [C, N])
        wss = sb("wss", [C, C])
        wo2 = xT[0][:, 0:2, :]
        st3 = sb("st3", [C, 4])

        ps = [ctx.enter_context(nc.psum_tensor(f"ps{b}", [C, HALF], F32)) for b in range(2)]
        psO = [ctx.enter_context(nc.psum_tensor(f"psO{b}", [C, 2, HALF], F32)) for b in range(2)]
        psT = ctx.enter_context(nc.psum_tensor("psT", [C, 2, HALF], F32))

        iota32 = tab[:, T_IOTA:T_IOTA + 32]
        gavg = tab[:, T_GAVG:T_GAVG + C]
        ones = tab[:, T_ONES:T_ONES + C]
        blk64 = tab[:, T_BLK:T_BLK + C]

        passed = {eng: sem(f"passed_{name}") for eng, name in ((nc.tensor, "pe"), (nc.scalar, "act"), (nc.vector, "dve"))}
        consts_landed = sem("consts_landed")
        borders_zero = sem("borders_zero")
        prep = sem("prep")
        prep_dve = sem("prep_dve")
        weights_ready = sem("weights_ready")
        w2_landed = sem("w2_landed")
        x_landed = [Signal(sem(f"x_landed{s}"), 16, 0) for s in range(2)]
        y_ready = signal("y_ready", 2)
        yout_free = signal("yout_free", 2)
        y_stored = [Signal(sem(f"y_stored{s}"), 16, 0) for s in range(2)]
        stats_ready = signal("stats_ready", 8)
        group_ready = signal("group_ready", 8)
        var_ready = signal("var_ready", 8)
        rstd_ready = signal("rstd_ready", 8)
        affine_ready = signal("affine_ready", 8)
        xn_ready = signal("xn_ready", 8)
        pooled_ready = signal("pooled_ready", 2)
        strips_ready = signal("strips_ready", 2)
        parts_product = signal("parts_product", 4)
        parts_ready = signal("parts_ready", 4)
        wide_ready = signal("wide_ready", 4)
        xT_product = signal("xT_product", 2)
        xT_ready = signal("xT_ready", 2)
        offs_ready = signal("offs_ready", 4)
        om_ready = signal("om_ready", 4)
        mask_ready = signal("mask_ready", 4)
        GT_ready = signal("GT_ready", 2 * TILES)
        GTt_ready = signal("GTt_ready", 2 * TILES)
        Gd_ready = signal("Gd_ready", 2 * TILES)
        sampled = signal("sampled", 2 * TILES)
        img_ready = signal("img_ready", 2)
        conv_ready = signal("conv_ready", 6)
        added = signal("added", 6)
        far_count = signal("far_count", 4)
        far_input = signal("far_input", 4)
        far_ready = signal("far_ready", 4)
        G_OWN = 1 + K9 * 4
        g_strips = signal("g_strips", 2)
        g_xTp = signal("g_xTp", 2)
        g_xT = signal("g_xT", 2)
        g_own = signal("g_own", 2 * G_OWN)
        g_GT = signal("g_GT", 2 * K9 * TILES)
        g_GTt = signal("g_GTt", 2 * K9 * TILES)
        g_Gd = signal("g_Gd", 2 * K9 * TILES)
        g_smp = signal("g_smp", 2 * K9 * TILES)
        g_smp_sb = signal("g_smp_sb", 2 * K9)
        STEPS = TILES * 3
        N_OWN = 7
        n_own = signal("n_own", 2 * N_OWN)
        n_GT = signal("n_GT", 2 * (TILES + STEPS))
        n_blkp = signal("n_blkp", 2 * (TILES + STEPS))
        n_Gp = signal("n_Gp", 2 * (TILES + STEPS))
        n_blk = signal("n_blk", 2 * (TILES + STEPS))
        n_G = signal("n_G", 2 * (TILES + STEPS))
        n_smp = signal("n_smp", 2 * (TILES + STEPS))
        n_smp_sb = signal("n_smp_sb", 2 * STEPS)

        def first_step(layer, s):
            return (2 * TILES + STEPS * s) if layer else TILES * s

        PRODUCTS = 17
        l3_product = signal("l3_product", PRODUCTS)
        l3_act = signal("l3_act", 14)
        l3_dw = signal("l3_dw", 2)
        l3_at = signal("l3_at", 1)
        l3_wss = signal("l3_wss", 1)
        l3_csum = signal("l3_csum", 1)
        l3_csig = signal("l3_csig", 1)
        l3_maps = signal("l3_maps", 2)
        dve_own = signal("dve_own", DVE_STEPS)
        start_own = signal("start_own", START_STEPS)

        def inner(t):
            return t[:, PAD:PAD + H, PAD:PAD + W]

        def tiled(t, b):
            return t[:, :, 16 * b:16 * b + 16].rearrange("p r (j c) -> p j r c", c=SW)

        def wait_apart(eng, *waits):
            for signal, value in waits:
                eng.wait_ge(signal.sem, value)
            eng.sem_inc(passed[eng], 1)

        block = ctx.enter_context(nc.Block())

        @block.sync
        def _(sp):
            for dst, src in ((tab, tab_d), (vec, vec_d), (offb, offb_d), (w0off, w0off_d), (w1off, w1off_d),
                             (ident, ident_d), (win, win_d), (win2T, win2T_d),
                             (cb1T, cb1T_d), (cb2T, cb2T_d)):
                sp.dma_start(dst[:], src).then_inc(consts_landed, 16)
            for s in range(2):
                sp.dma_start(xin[s][:], x_d[s, :, :]).then_inc(x_landed[s].sem, 16)
            for dst, src in ((pwT, w0dw_pw_d), (w1, w1_d), (kh_w, kh_d), (kv_w, kv_d), (woT, woT_d)):
                sp.dma_start(dst[:], src).then_inc(consts_landed, 16)
            sp.dma_start(w2[:], w2_d).then_inc(w2_landed, 16)
            sp.dma_start(samp[:, 0:2, :].rearrange("p a b -> p (a b)")[:, 0:K9 * C], r2_d).then_inc(w2_landed, 16)

            def store(i, s):
                sp.wait_ge(y_ready.sem, y_ready.at(i, s + 1))
                sp.dma_start(out_d[2 * i + s, :, :], yout[s][:]).then_inc(y_stored[s].sem, 16)

            if PASSES > 1:
                with sp.Fori(0, PASSES - 1) as i:
                    for s in range(2):
                        sp.wait_ge(added.sem, added.at(i, s + 1))
                        sp.dma_start(xin[s][:], x_d[2 * i + 2 + s, :, :]).then_inc(x_landed[s].sem, 16)
                    for s in range(2):
                        store(i, s)
                    for s in range(2):
                        sp.wait_ge(y_stored[s].sem, y_stored[s].at(i, 16))
                        sp.sem_inc(yout_free.sem, 1)
            for s in range(2):
                store(PASSES - 1, s)
            for s in range(2):
                sp.wait_ge(y_stored[s].sem, y_stored[s].at(PASSES - 1, 16))

        @block.gpsimd
        def _(pool):
            for each in signals:
                pool.sem_inc(each.sem, each.start)
            for t in (xn[0], xn[1], img[0], img[1], x2p, ahp, u3):
                nc.gpsimd.memset(t[:], 0.0).then_inc(borders_zero, 1)
            nc.gpsimd.memset(neg_half[:], -0.5).then_inc(borders_zero, 1)
            pool.wait_ge(borders_zero, 8)
            with pool.Fori(0, PASSES) as i:
                for n in range(8):
                    g = gst[n % 2]
                    pool.wait_ge(var_ready.sem, var_ready.at(i, n + 1))
                    nc.gpsimd.tensor_tensor(out=g[:, 18:19], in0=g[:, 17:18], in1=neg_half[:],
                                            op=ALU.pow).then_inc(rstd_ready.sem, 1)

        @block.tensor
        def _(pe):
            mm = nc.tensor.matmul
            pe.wait_ge(consts_landed, CONSTS * 16)
            mm(ps[0][:, 0:C2], win[:], cb1T[:], start=True, stop=True).then_inc(prep, 1)
            mm(ps[1][0:C2, 0:1], cb1T[:], vec[0:C2, V_BIN1:V_BIN1 + 1], start=True, stop=True).then_inc(prep, 1)
            pe.wait_ge(weights_ready, 1)
            pe.wait_ge(borders_zero, 8)

            def group_mean(i, n):
                pe.wait_ge(stats_ready.sem, stats_ready.at(i, n + 1))
                mm(ps[n % 2][:, 0:2], gavg, gst[n % 2][:, 12:14], start=True, stop=True).then_inc(group_ready.sem, 1)

            def offset_parts(n, src, w):
                dst = psO[n % 2] if n >= 2 else psT
                for h in range(2):
                    for k in range(K9):
                        g = k % 4
                        last = mm(dst[32 * g:32 * g + 32, h, :], w[:, k, :], window(src)(h, k),
                                  start=(k < 4), stop=(k >= K9 - 4), skip_group_check=True)
                last.then_inc(parts_product.sem, 1)

            def offsets(i, n, m):
                s = n % 2
                pe.wait_ge(parts_ready.sem, parts_ready.at(i, n + 1))
                for t in range(TILES):
                    last = mm(ps[s][:, 4 + m * t:4 + m * t + m], off_parts[s][:, C * t:C * t + C],
                              tab[:, T_SEL:T_SEL + m], start=True, stop=True)
                last.then_inc(offs_ready.sem, 1)

            def image_T(s, finished):
                for q in range(TILES):
                    last = nc.tensor.transpose(psT[:, q // 4, C * (q % 4):C * (q % 4) + C],
                                               q_strips[s][:, C * q:C * q + C], ident[:])
                last.then_inc(finished.sem, 1)

            def conv(dst, wgt, rhs, mid=None):
                for h in range(2):
                    if mid and h:
                        mid()
                    for k in range(K9):
                        last = mm(dst[:, h, :], wgt[:, k, :], rhs(h, k), start=(k == 0), stop=(k == K9 - 1))
                last.then_inc(conv_ready.sem, 1)

            def window(src):
                return lambda h, k: src[:, PAD + 16 * h + k // 3 - 1:PAD + 16 * h + k // 3 + 15,
                                        PAD + k % 3 - 1:PAD + k % 3 - 1 + W]

            def dense(i, base, dst, xTs, GTr, GTt, Gdr, smp):
                for t in range(TILES + 1):
                    if t < TILES:
                        pe.wait_ge(GTr.sem, GTr.at(i, base + t + 1))
                        pe.wait_ge(Gdr.sem, Gdr.at(i, base + t))
                        for q in range(TILES):
                            last = nc.tensor.transpose(psT[:, q // 4, C * (q % 4):C * (q % 4) + C],
                                                       GT[t % 2][:, C * q:C * q + C], ident[:])
                        last.then_inc(GTt.sem, 1)
                    if t:
                        p = t - 1
                        pe.wait_ge(Gdr.sem, Gdr.at(i, base + p + 1))
                        for q in range(TILES):
                            last = mm(dst[:, p // 4, C * (p % 4):C * (p % 4) + C], xTs[:, q, :], Gd[p % 2][:, q, :],
                                      start=(q == 0), stop=(q == TILES - 1))
                        last.then_inc(smp.sem, 1)

            def near0(i, s):
                for n in range(TILES + 1):
                    if n < TILES:
                        o = first_step(0, s) + n
                        pe.wait_ge(n_blk.sem, n_blk.at(i, o))
                        for u in range(2):
                            r0 = 16 * (n % 2) + BR * u
                            b = strip12[s][:, n // 2, r0:r0 + BR, :].rearrange("p r c -> p (r c)")
                            last = nc.tensor.transpose(psT[0:BLK, 1, C * u:C * u + C], b, ident[:])
                        last.then_inc(n_blkp.sem, 1)
                        pe.wait_ge(n_GT.sem, n_GT.at(i, o + 1))
                        pe.wait_ge(n_G.sem, n_G.at(i, o))
                        for u in range(2):
                            last = nc.tensor.transpose(psT[0:BLK, 0, C * u:C * u + C], GT1[n % 2][:, u, :], ident[:])
                        last.then_inc(n_Gp.sem, 1)
                    if n:
                        p = n - 1
                        o = first_step(0, s) + p
                        pe.wait_ge(n_blk.sem, n_blk.at(i, o + 1))
                        pe.wait_ge(n_G.sem, n_G.at(i, o + 1))
                        for u in range(2):
                            last = mm(psO[s][:, p // 4, C * (p % 4):C * (p % 4) + C], xblk[p % 2][:, u, :],
                                      G1[p % 2][:, u, :], start=(u == 0), stop=(u == 1))
                        last.then_inc(n_smp.sem, 1)

            def near(i, s):
                for n in range(STEPS + 1):
                    if n < STEPS:
                        t, ki = n // 3, n % 3
                        o = first_step(1, s) + n
                        pe.wait_ge(n_blk.sem, n_blk.at(i, o))
                        for h in range(2):
                            r0 = 16 * (t % 2) + 8 * h + ki
                            b = strip12[s][:, t // 2, r0:r0 + BR, :].rearrange("p r c -> p (r c)")
                            last = nc.tensor.transpose(psT[0:BLK, 1, C * h:C * h + C], b, ident[:])
                        last.then_inc(n_blkp.sem, 1)
                        pe.wait_ge(n_GT.sem, n_GT.at(i, o + 1))
                        pe.wait_ge(n_G.sem, n_G.at(i, o))
                        for kj in range(3):
                            last = nc.tensor.transpose(psT[0:BLK, 0, C * kj:C * kj + C], GT1[n % 2][:, kj, :], ident[:])
                        last.then_inc(n_Gp.sem, 1)
                    if n:
                        p = n - 1
                        o = first_step(1, s) + p
                        pe.wait_ge(n_blk.sem, n_blk.at(i, o + 1))
                        pe.wait_ge(n_G.sem, n_G.at(i, o + 1))
                        if STEPS * s + p >= 2:
                            pe.wait_ge(n_smp_sb.sem, n_smp_sb.at(i, STEPS * s + p - 1))
                        dst = psO[1][:, p % 2, 0:3 * C].rearrange("p (k c) -> p k c", k=3)
                        for h in range(2):
                            half = slice(64 * h, 64 * h + 64)
                            last = mm(dst[:, :, half], xblk[p % 2][:, h, :], G1[p % 2][:, :, half],
                                      start=True, stop=True)
                        last.then_inc(n_smp.sem, 1)

            def far(i, n):
                pe.wait_ge(far_input.sem, far_input.at(i, n + 1))
                mm(ps[n % 2][:, 2:3], ones, flagf[n % 2][:, 0:1], start=True, stop=True).then_inc(far_count.sem, 1)

            def start_means(j):
                for s in range(2):
                    group_mean(j, s)

            def start_parts(j, s):
                pe.wait_ge(xn_ready.sem, xn_ready.at(j, s + 1))
                if s:
                    pe.wait_ge(parts_ready.sem, parts_ready.at(j, 1))
                offset_parts(s, xn[s], w0off)

            def start_offsets(j):
                for s in range(2):
                    offsets(j, s, 3)

            def start_far(j):
                for s in range(2):
                    far(j, s)

            def one_pass(i, more):
                pe.wait_ge(y_ready.sem, y_ready.at(i, 0))
                for s in range(2):
                    wait_apart(pe, (far_ready, far_ready.at(i, s + 1)))
                    is_far = pe.value_load(flag[s][0:1, 0:1])
                    with pe.If(is_far > 0):
                        pe.wait_ge(strips_ready.sem, strips_ready.at(i, s + 1))
                        image_T(s, xT_product)
                        pe.wait_ge(xT_ready.sem, xT_ready.at(i, s + 1))
                        dense(i, TILES * s, psO[s], xT[s], GT_ready, GTt_ready, Gd_ready, sampled)
                        pe.wait_ge(sampled.sem, sampled.at(i, TILES * (s + 1)))
                        for each in (n_blkp, n_Gp, n_smp):
                            pe.sem_inc(each.sem, TILES)
                    with pe.Else():
                        pe.wait_ge(wide_ready.sem, wide_ready.at(i, s + 1))
                        near0(i, s)
                        pe.wait_ge(n_smp.sem, n_smp.at(i, first_step(0, s) + TILES))
                        pe.sem_inc(xT_product.sem, 1)
                        pe.sem_inc(GTt_ready.sem, TILES)
                        pe.sem_inc(sampled.sem, TILES)
                for s in range(2):
                    pe.wait_ge(img_ready.sem, img_ready.at(i, s + 1))
                    conv(psO[s], w0, window(img[s]), mid=(lambda: group_mean(i, 2)) if s else None)
                pe.wait_ge(pooled_ready.sem, pooled_ready.at(i, 1))
                offset_parts(2, img[0], w1off)
                group_mean(i, 3)
                offsets(i, 2, 27)
                pe.wait_ge(pooled_ready.sem, pooled_ready.at(i, 2))
                offset_parts(3, img[1], w1off)
                far(i, 2)
                offsets(i, 3, 27)
                far(i, 3)
                for s in range(2):
                    wait_apart(pe, (added, added.at(i, 2)), (far_ready, far_ready.at(i, s + 3)))
                    is_far = pe.value_load(flag[s][0:1, 0:1])
                    with pe.If(is_far > 0):
                        pe.wait_ge(g_strips.sem, g_strips.at(i, s + 1))
                        image_T(s, g_xTp)
                        wait_apart(pe, (g_xT, g_xT.at(i, s + 1)))
                        with pe.Fori(0, K9) as k:
                            pe.wait_ge(g_smp_sb.sem, g_smp_sb.at(i, K9 * s) + k)
                            dense(i, K9 * TILES * s + k * TILES, psO[1], xT[s], g_GT, g_GTt, g_Gd, g_smp)
                        pe.wait_ge(g_smp_sb.sem, g_smp_sb.at(i, K9 * (s + 1)))
                        for each in (n_blkp, n_Gp, n_smp):
                            pe.sem_inc(each.sem, STEPS)
                    with pe.Else():
                        pe.wait_ge(wide_ready.sem, wide_ready.at(i, s + 3))
                        near(i, s)
                        pe.wait_ge(n_smp_sb.sem, n_smp_sb.at(i, STEPS * (s + 1)))
                        pe.sem_inc(g_xTp.sem, 1)
                        pe.sem_inc(g_GTt.sem, K9 * TILES)
                        pe.sem_inc(g_smp.sem, K9 * TILES)
                    if s:
                        pe.wait_ge(added.sem, added.at(i, 3))
                    conv(psO[0], w1, lambda h, k: samp[:, k, HALF * h:HALF * h + HALF],
                         mid=(lambda: group_mean(i, 4)) if s else None)
                pe.wait_ge(xn_ready.sem, xn_ready.at(i, 5))
                conv(psO[1], w2, window(xn[0]), mid=lambda: group_mean(i, 5))
                pe.wait_ge(xn_ready.sem, xn_ready.at(i, 6))
                conv(psO[0], w2, window(xn[1]), mid=lambda: group_mean(i, 6))
                group_mean(i, 7)
                pe.wait_ge(xn_ready.sem, xn_ready.at(i, 8))
                pe.wait_ge(added.sem, added.at(i, 6))

                def img_rows(s, h):
                    return xn[s][:, PAD + 16 * h:PAD + 16 * h + 16, PAD:PAD + W]

                def product(n):
                    if n >= 3:
                        pe.wait_ge(l3_act.sem, l3_act.at(i, n - 2))
                    return psO[n % 2]

                d = product(1)
                for s in range(2):
                    for h in range(2):
                        last = mm(d[C2 * s:C2 * s + C2, h, :], win2T[:], img_rows(s, h), start=True, stop=True)
                last.then_inc(l3_product.sem, 1)
                d = product(2)
                for s in range(2):
                    for h in range(2):
                        last = mm(d[32 * s:32 * s + 32, h, :], wu[:, 32 * s:32 * s + 32], img_rows(s, h), start=True, stop=True)
                last.then_inc(l3_product.sem, 1)

                def whole(n, lhsT, rhs):
                    d = product(n)
                    for h in range(2):
                        last = mm(d[:, h, :], lhsT, rhs[:, HALF * h:HALF * h + HALF], start=True, stop=True)
                    last.then_inc(l3_product.sem, 1)

                if more:
                    start_means(i + 1)
                pe.wait_ge(l3_act.sem, l3_act.at(i, 2))
                whole(3, cb2T[:], u3)
                if more:
                    start_parts(i + 1, 0)
                for v in range(2):
                    pe.wait_ge(l3_dw.sem, l3_dw.at(i, v + 1))
                    for t in range(TAPS):
                        whole(4 + TAPS * v + t, (kh_w, kv_w)[v][:, t, :], dwo)
                    if more and v == 0:
                        start_parts(i + 1, 1)
                        start_offsets(i + 1)
                    elif more:
                        start_far(i + 1)
                pe.wait_ge(l3_wss.sem, l3_wss.at(i, 1))
                whole(14, wss[:], xc)
                whole(15, blk64, xc)
                pe.wait_ge(l3_maps.sem, l3_maps.at(i, 2))
                pe.wait_ge(l3_act.sem, l3_act.at(i, 14))
                pe.wait_ge(l3_csum.sem, l3_csum.at(i, 1))
                for s in range(2):
                    for h in range(2):
                        hh = slice(HALF * h, HALF * h + HALF)
                        mm(psO[s][:, h, :], woT[:, s, 0, :], sm[:, hh], start=True, stop=False)
                        last = mm(psO[s][:, h, :], wo2[:, s, :], at[:, hh], start=False, stop=True)
                    last.then_inc(l3_product.sem, 1)

            start_means(0)
            start_parts(0, 0)
            start_parts(0, 1)
            start_offsets(0)
            start_far(0)
            if PASSES > 1:
                with pe.Fori(0, PASSES - 1) as i:
                    one_pass(i, True)
            one_pass(PASSES - 1, False)

        @block.scalar
        def _(act):
            def copy(out, in_):
                return nc.scalar.activation(out, in_, ACT.Copy)

            def dense(i, base, GTt, Gdr, smp):
                for t in range(TILES):
                    act.wait_ge(GTt.sem, GTt.at(i, base + t + 1))
                    if t >= 2:
                        act.wait_ge(smp.sem, smp.at(i, base + t - 1))
                    else:
                        act.wait_ge(smp.sem, smp.at(i, base))
                    copy(Gd[t % 2][:].rearrange("p q c -> p (q c)"),
                         psT[:].rearrange("p b c -> p (b c)")).then_inc(Gdr.sem, 1)

            def wide_windows(whole):
                return bass.AP(whole.tensor, whole.offset, [whole.ap[0], [SW, STRIPS], [PW, PW], [1, BC]])

            def normalise(i, n):
                s = n % 2
                act.wait_ge(affine_ready.sem, affine_ready.at(i, n + 1))
                src = (xin if n < 2 else x)[s]
                nc.scalar.activation(inner(xn[s]), src[:].rearrange("p (r c) -> p r c", c=W), ACT.Identity,
                                     bias=gst[s][:, 20:21], scale=gst[s][:, 19:20]).then_inc(xn_ready.sem, 1)

            def parts(i, n):
                s = n % 2
                act.wait_ge(parts_product.sem, parts_product.at(i, n + 1))
                for b in range(2):
                    last = copy(off_parts[s].rearrange("p (j b r c) -> p j b r c", b=2, j=STRIPS, c=SW)[:, :, b],
                                (psO[s] if n >= 2 else psT)[:, b, :].rearrange("p (r j c) -> p j r c", j=STRIPS, c=SW))
                last.then_inc(parts_ready.sem, 1)

            def start_normalise(j):
                for s in range(2):
                    normalise(j, s)

            def start_parts(j, s):
                act.wait_ge(xn_ready.sem, xn_ready.at(j, s + 1))
                copy(strip12[s][:], wide_windows(xn[s][:])).then_inc(wide_ready.sem, 1)
                parts(j, s)

            def start_masks(j):
                for s in range(2):
                    act.wait_ge(om_ready.sem, om_ready.at(j, s + 1))
                    nc.scalar.activation(mk[s][:, 0:TILES], om0[s][:, 2, :], ACT.Sigmoid).then_inc(mask_ready.sem, 1)

            def one_pass(i, more):
                for s in range(2):
                    wait_apart(act, (far_ready, far_ready.at(i, s + 1)))
                    far = act.value_load(flag[s][0:1, 0:1])
                    with act.If(far > 0):
                        act.wait_ge(xT_product.sem, xT_product.at(i, s + 1))
                        copy(xT[s][:].rearrange("p q c -> p (q c)"), psT[:].rearrange("p b c -> p (b c)"))\
                            .then_inc(xT_ready.sem, 1)
                        dense(i, TILES * s, GTt_ready, Gd_ready, sampled)
                        act.wait_ge(sampled.sem, sampled.at(i, TILES * (s + 1)))
                        act.wait_ge(Gd_ready.sem, Gd_ready.at(i, TILES * (s + 1)))
                        act.sem_inc(n_G.sem, TILES)
                    with act.Else():
                        for n in range(TILES):
                            o = first_step(0, s) + n
                            act.wait_ge(n_Gp.sem, n_Gp.at(i, o + 1))
                            if o >= 2:
                                act.wait_ge(n_smp.sem, n_smp.at(i, o - 1))
                            copy(G1[n % 2][:, 0:2, :].rearrange("p u c -> p (u c)"), psT[0:BLK, 0, 0:2 * C])\
                                .then_inc(n_G.sem, 1)
                        act.wait_ge(n_smp.sem, n_smp.at(i, first_step(0, s) + TILES))
                        act.wait_ge(n_G.sem, n_G.at(i, first_step(0, s) + TILES))
                        act.sem_inc(xT_ready.sem, 1)
                        act.sem_inc(Gd_ready.sem, TILES)
                    for b in range(2):
                        last = copy(tiled(inner(img[s]), b), psO[s][:, b, :].rearrange("p (j r c) -> p j r c", j=2, c=SW))
                    last.then_inc(img_ready.sem, 1)
                for s in range(2):
                    normalise(i, 2 + s)
                for s in range(2):
                    parts(i, 2 + s)
                    act.wait_ge(pooled_ready.sem, pooled_ready.at(i, s + 1))
                    copy(strip12[s][:], wide_windows(img[s][:])).then_inc(wide_ready.sem, 1)
                for s in range(2):
                    act.wait_ge(om_ready.sem, om_ready.at(i, 3 + s))
                    nc.scalar.activation(mk[s][:], om[s][:, 2, :, :].rearrange("p t k -> p (t k)"), ACT.Sigmoid)\
                        .then_inc(mask_ready.sem, 1)
                for s in range(2):
                    wait_apart(act, (far_ready, far_ready.at(i, s + 3)))
                    far = act.value_load(flag[s][0:1, 0:1])
                    with act.If(far > 0):
                        act.wait_ge(g_xTp.sem, g_xTp.at(i, s + 1))
                        copy(xT[s][:].rearrange("p q c -> p (q c)"), psT[:].rearrange("p b c -> p (b c)"))\
                            .then_inc(g_xT.sem, 1)
                        with act.Fori(0, K9) as k:
                            dense(i, K9 * TILES * s + k * TILES, g_GTt, g_Gd, g_smp)
                            act.wait_ge(g_smp.sem, g_smp.at(i, K9 * TILES * s + k * TILES + TILES))
                            tap = samp[:, bass.ds(k, 1), :].rearrange("p k (r c) -> p (k r) c", c=W)
                            for b in range(2):
                                last = copy(tiled(tap, b), psO[1][:, b, :].rearrange("p (j r c) -> p j r c", j=2, c=SW))
                            last.then_inc(g_smp_sb.sem, 1)
                        act.wait_ge(g_smp_sb.sem, g_smp_sb.at(i, K9 * (s + 1)))
                        act.sem_inc(n_G.sem, STEPS)
                        act.sem_inc(n_smp_sb.sem, STEPS)
                    with act.Else():
                        for n in range(STEPS + 1):
                            if n < STEPS:
                                o = first_step(1, s) + n
                                act.wait_ge(n_Gp.sem, n_Gp.at(i, o + 1))
                                if o >= 2:
                                    act.wait_ge(n_smp.sem, n_smp.at(i, o - 1))
                                copy(G1[n % 2][:].rearrange("p k c -> p (k c)"), psT[0:BLK, 0, 0:3 * C])\
                                    .then_inc(n_G.sem, 1)
                            if n:
                                p = n - 1
                                t, ki = p // 3, p % 3
                                act.wait_ge(n_smp.sem, n_smp.at(i, first_step(1, s) + p + 1))
                                r0, c0 = 16 * (t % 2), SW * (t // 2)
                                copy(samp[:, 3 * ki:3 * ki + 3, :].rearrange("p k (r c) -> p k r c", c=W)
                                     [:, :, r0:r0 + 16, c0:c0 + SW],
                                     psO[1][:, p % 2, 0:3 * C].rearrange("p (k r c) -> p k r c", k=3, c=SW))\
                                    .then_inc(n_smp_sb.sem, 1)
                        act.wait_ge(n_smp_sb.sem, n_smp_sb.at(i, STEPS * (s + 1)))
                        act.sem_inc(g_xT.sem, 1)
                        act.sem_inc(g_Gd.sem, K9 * TILES)
                        act.sem_inc(g_smp_sb.sem, K9)
                for n in range(4, 8):
                    normalise(i, n)
                act.wait_ge(l3_product.sem, l3_product.at(i, 1))
                nc.scalar.activation(x2p[:, :, LPAD:LPAD + W], psO[1][:].rearrange("p b (r c) -> p (b r) c", c=W),
                                     ACT.Identity, bias=vec[:, V_BIN2:V_BIN2 + 1]).then_inc(l3_act.sem, 1)
                act.wait_ge(l3_product.sem, l3_product.at(i, 2))
                nc.scalar.activation(u3[0:C2], psO[0][0:C2].rearrange("p b c -> p (b c)"), ACT.Relu,
                                     bias=bu[:]).then_inc(l3_act.sem, 1)
                act.wait_ge(l3_product.sem, l3_product.at(i, 3))
                nc.scalar.activation(xc[:], psO[1][:].rearrange("p b c -> p (b c)"), ACT.Identity,
                                     bias=vec[:, V_BCB2:V_BCB2 + 1]).then_inc(l3_act.sem, 1)
                if more:
                    start_normalise(i + 1)
                    start_parts(i + 1, 0)
                for v in range(2):
                    for t in range(TAPS):
                        n = 4 + TAPS * v + t
                        act.wait_ge(l3_product.sem, l3_product.at(i, n))
                        b = (V_KHB, V_KVB)[v] + t
                        nc.scalar.activation(kern[:, t, :], psO[n % 2][:].rearrange("p b c -> p (b c)"), ACT.Tanh,
                                             bias=vec[:, b:b + 1]).then_inc(l3_act.sem, 1)
                    if more and v == 0:
                        start_parts(i + 1, 1)
                    elif more:
                        start_masks(i + 1)
                act.wait_ge(l3_product.sem, l3_product.at(i, 14))
                nc.scalar.activation(sg, psO[0][:].rearrange("p b c -> p (b c)"), ACT.Sigmoid)\
                    .then_inc(l3_act.sem, 1)
                act.wait_ge(l3_csum.sem, l3_csum.at(i, 1))
                nc.scalar.activation(st3[:, 2:3], st3[:, 1:2], ACT.Sigmoid, scale=1.0 / N).then_inc(l3_csig.sem, 1)

            act.wait_ge(borders_zero, 8)
            start_normalise(0)
            start_parts(0, 0)
            start_parts(0, 1)
            start_masks(0)
            if PASSES > 1:
                with act.Fori(0, PASSES - 1) as i:
                    one_pass(i, True)
            one_pass(PASSES - 1, False)

        @block.vector
        def _(dve):
            v_ = nc.vector
            dve.wait_ge(consts_landed, CONSTS * 16)
            for k in range(K9):
                v_.tensor_scalar(w0[:, k, :], pwT[:], vec[:, V_DW0 + k:V_DW0 + k + 1], None, ALU.mult)
            dve.wait_ge(prep, 2)
            v_.tensor_copy(wu[:], ps[0][:, 0:C2])
            v_.tensor_tensor(bu[:], ps[1][0:C2, 0:1], vec[0:C2, V_BCB1:V_BCB1 + 1], ALU.add)
            dve.wait_ge(w2_landed, 32)
            n2 = K9 * C
            f2 = w2[:].rearrange("p k o -> p (k o)")
            flat = samp[:].rearrange("p a b -> p (a b)")
            r2, sgn, t2, neg = (flat[:, n * n2:(n + 1) * n2] for n in range(4))
            v_.tensor_scalar(sgn, f2, 0.0, None, ALU.is_gt)
            v_.tensor_scalar(neg, f2, 0.0, None, ALU.is_lt)
            v_.tensor_scalar(t2, r2, 0.5, 0.7, ALU.is_gt, ALU.mult).then_inc(prep_dve, 1)
            dve.wait_ge(prep_dve, 1)
            v_.tensor_tensor(sgn, sgn, neg, ALU.subtract)
            v_.tensor_scalar(r2, r2, 0.5, 0.175, ALU.is_lt, ALU.mult).then_inc(prep_dve, 1)
            dve.wait_ge(prep_dve, 2)
            v_.tensor_tensor(t2, t2, r2, ALU.add).then_inc(prep_dve, 1)
            dve.wait_ge(prep_dve, 3)
            v_.tensor_tensor(t2, t2, sgn, ALU.mult).then_inc(prep_dve, 1)
            dve.wait_ge(prep_dve, 4)
            v_.scalar_tensor_tensor(f2, f2, 0.5, t2, ALU.mult, ALU.add).then_inc(weights_ready, 1)
            dve.wait_ge(weights_ready, 1)
            dve.wait_ge(borders_zero, 8)

            def stats(own, n, src):
                g = gst[n % 2]
                for h in range(2):
                    own.step(v_.bn_stats(g[:, 6 * h:6 * h + 6], src[:, HALF * h:HALF * h + HALF]))
                wait_apart(dve, (own.steps, own.steps.at(own.i, own.n)))
                own.step(v_.bn_aggr(g[:, 12:14], g[:, 0:12]))
                own.settle()
                v_.scalar_tensor_tensor(g[:, 13:14], g[:, 12:13], g[:, 12:13], g[:, 13:14], ALU.mult, ALU.add)\
                    .then_inc(stats_ready.sem, 1)

            def affine(own, n):
                g = gst[n % 2]
                dve.wait_ge(group_ready.sem, group_ready.at(own.i, n + 1))
                own.step(v_.tensor_copy(g[:, 14:16], ps[n % 2][:, 0:2]))
                own.settle()
                own.step(v_.scalar_tensor_tensor(g[:, 16:17], g[:, 14:15], g[:, 14:15], g[:, 15:16],
                                                 ALU.mult, ALU.subtract))
                own.settle()
                v_.tensor_scalar(g[:, 17:18], g[:, 16:17], -1.0, EPS, ALU.mult, ALU.add)\
                    .then_inc(var_ready.sem, 1)
                dve.wait_ge(rstd_ready.sem, rstd_ready.at(own.i, n + 1))
                own.step(v_.tensor_scalar(g[:, 19:20], g[:, 18:19], 1.0 / 9 if n // 2 == 1 else 1.0, None, ALU.mult))
                own.settle()
                v_.tensor_scalar(g[:, 20:21], g[:, 14:15], g[:, 19:20], -1.0, ALU.mult, ALU.mult)\
                    .then_inc(affine_ready.sem, 1)

            def hats_dense(s, settle, step, uv, mask, gain):
                h = hat[s]
                step(v_.tensor_tensor(h[:], iota32.unsqueeze(1).broadcast_to((C, 2 * TILES, 32)),
                                      uv.broadcast_to((C, 2 * TILES, 32)), ALU.subtract))
                settle()
                step(v_.scalar_tensor_tensor(h[:], h[:], -1.0, h[:], ALU.mult, ALU.max))
                settle()
                step(v_.tensor_scalar(h[:], h[:], 1.0, 0.0, ALU.subtract, ALU.min))
                settle()
                step(v_.scalar_tensor_tensor(h[:, TILES:], h[:, TILES:], gain, mask.broadcast_to((C, TILES, 32)),
                                             ALU.mult, ALU.mult))
                settle()

            def dense(i_, base, s, GTr, GTt):
                for t in range(TILES):
                    dve.wait_ge(GTt.sem, GTt.at(i_, base + (t - 1 if t >= 2 else 0)))
                    v_.tensor_tensor(GT[t % 2].rearrange("p (j a b) -> p j a b", j=STRIPS, b=SW),
                                     hat[s][:, t, :].unsqueeze(1).unsqueeze(3).broadcast_to((C, STRIPS, H, SW)),
                                     hat[s][:, TILES + t, :].rearrange("p (j b) -> p j b", b=SW).unsqueeze(2)
                                     .broadcast_to((C, STRIPS, H, SW)), ALU.mult).then_inc(GTr.sem, 1)

            def far_flag(own, s, offsets, reach):
                own.step(v_.tensor_reduce(out=flagf[s][:, 1:2], in_=offsets,
                                          op=ALU.max, axis=AX.X, apply_absolute_value=True))
                own.settle()
                v_.tensor_scalar(flagf[s][:, 0:1], flagf[s][:, 1:2], reach, None, ALU.is_gt)\
                    .then_inc(far_input.sem, 1)

            def load_flag(i, n):
                dve.wait_ge(far_count.sem, far_count.at(i, n + 1))
                v_.tensor_copy(flag[n % 2][:], ps[n % 2][:, 2:3]).then_inc(far_ready.sem, 1)

            def block_copy(i, o, b):
                dve.wait_ge(n_blkp.sem, n_blkp.at(i, o + 1))
                if o >= 2:
                    dve.wait_ge(n_smp.sem, n_smp.at(i, o - 1))
                v_.tensor_copy(xblk[b][:].rearrange("p h c -> p (h c)"), psT[0:BLK, 1, 0:2 * C])\
                    .then_inc(n_blk.sem, 1)

            def tile_order(s, src):
                return v_.tensor_copy(q_strips[s][:].rearrange("p (j r c) -> p j r c", j=STRIPS, c=SW),
                                      inner(src).rearrange("p r (j c) -> p j r c", c=SW))

            def start_stats(own):
                for s in range(2):
                    dve.wait_ge(x_landed[s].sem, x_landed[s].at(own.i, 16))
                    stats(own, s, xin[s])

            def start_affine(own):
                for s in range(2):
                    affine(own, s)

            def start_offsets(own):
                for s in range(2):
                    dve.wait_ge(offs_ready.sem, offs_ready.at(own.i, s + 1))
                    v_.tensor_tensor(om0[s][:].rearrange("p g t -> p t g"),
                                     ps[s][:, 4:4 + 3 * TILES].rearrange("p (t g) -> p t g", g=3),
                                     offb[:, 27:30].unsqueeze(1).broadcast_to((C, TILES, 3)), ALU.add)\
                        .then_inc(om_ready.sem, 1)
                    dve.wait_ge(om_ready.sem, om_ready.at(own.i, s + 1))
                    far_flag(own, s, om0[s][:, 0:2, :].rearrange("p g t -> p (g t)"), NEAR0)

            def start_hats(own, s):
                o2 = om0[s][:, 0:2, :].rearrange("p g t -> p (g t)")
                load_flag(own.i, s)
                own.step(v_.tensor_scalar(flagf[s][:, 1:2], ps[s][:, 2:3], 0.5, None, ALU.is_lt))
                own.step(v_.scalar_tensor_tensor(o2, o2, 2.0 / W, tab[:, T_LIN:T_LIN + 2 * TILES], ALU.mult, ALU.add))
                own.settle()
                own.step(v_.tensor_scalar(o2, o2, 1.0, 0.5 * (W - 1), ALU.add, ALU.mult))
                own.settle()
                own.step(v_.scalar_tensor_tensor(o2, tab[:, T_ORG:T_ORG + 2 * TILES], flagf[s][:, 1:2], o2,
                                                 ALU.mult, ALU.add))
                own.settle()
                dve.wait_ge(mask_ready.sem, mask_ready.at(own.i, s + 1))
                hats_dense(s, own.settle, own.step, o2.unsqueeze(2), mk[s][:, 0:TILES].unsqueeze(2), 1.0)

            def one_pass(i, more):
                own = Own(dve, dve_own, i)
                nxt = Own(dve, start_own, i + 1)
                for s in range(2):
                    wait_apart(dve, (far_ready, far_ready.at(i, s + 1)))
                    far = dve.value_load(flag[s][0:1, 0:1])
                    with dve.If(far > 0):
                        dve.wait_ge(xn_ready.sem, xn_ready.at(i, s + 1))
                        tile_order(s, xn[s]).then_inc(strips_ready.sem, 1)
                        dense(i, TILES * s, s, GT_ready, GTt_ready)
                        dve.wait_ge(GTt_ready.sem, GTt_ready.at(i, TILES * (s + 1)))
                        dve.sem_inc(n_GT.sem, TILES)
                        dve.sem_inc(n_blk.sem, TILES)
                    with dve.Else():
                        for n in range(TILES + 1):
                            if n < TILES:
                                o = first_step(0, s) + n
                                if o >= 2:
                                    dve.wait_ge(n_Gp.sem, n_Gp.at(i, o - 1))
                                v_.tensor_tensor(GT1[n % 2][:, 0:2, :].rearrange("p u q -> p (u q)")
                                                 .rearrange("p (a b) -> p a b", b=BC),
                                                 hat[s][:, n, 0:2 * BR].unsqueeze(2).broadcast_to((C, 2 * BR, BC)),
                                                 hat[s][:, TILES + n, 0:BC].unsqueeze(1).broadcast_to((C, 2 * BR, BC)),
                                                 ALU.mult).then_inc(n_GT.sem, 1)
                            if n:
                                block_copy(i, first_step(0, s) + n - 1, (n - 1) % 2)
                        dve.wait_ge(n_blk.sem, n_blk.at(i, first_step(0, s) + TILES))
                        dve.sem_inc(strips_ready.sem, 1)
                        dve.sem_inc(GT_ready.sem, TILES)
                for s in range(2):
                    dve.wait_ge(conv_ready.sem, conv_ready.at(i, s + 1))
                    v_.tensor_tensor(x[s][:], psO[s][:].rearrange("p b c -> p (b c)"), xin[s][:], ALU.add)\
                        .then_inc(added.sem, 1)
                    dve.wait_ge(added.sem, added.at(i, s + 1))
                    stats(own, 2 + s, x[s])
                    affine(own, 2 + s)
                    dve.wait_ge(xn_ready.sem, xn_ready.at(i, 3 + s))
                    a, b, o = xn[s], pool_v, inner(img[s])
                    cols = slice(PAD - 1, PAD + W + 1)
                    own.step(v_.tensor_tensor(b[:], a[:, PAD - 1:PAD - 1 + H, cols], a[:, PAD:PAD + H, cols], ALU.add))
                    own.settle()
                    own.step(v_.tensor_tensor(b[:], b[:], a[:, PAD + 1:PAD + 1 + H, cols], ALU.add))
                    own.settle()
                    own.step(v_.tensor_tensor(o, b[:, :, 0:W], b[:, :, 1:W + 1], ALU.add))
                    own.settle()
                    v_.tensor_tensor(o, o, b[:, :, 2:W + 2], ALU.add).then_inc(pooled_ready.sem, 1)
                for s in range(2):
                    dve.wait_ge(offs_ready.sem, offs_ready.at(i, 3 + s))
                    v_.tensor_tensor(om[s][:].rearrange("p g t k -> p t g k"),
                                     ps[s][:, 4:4 + 27 * TILES].rearrange("p (t g k) -> p t g k", g=3, k=K9),
                                     offb[:, 0:27].rearrange("p (g k) -> p g k", k=K9).unsqueeze(1)
                                     .broadcast_to((C, TILES, 3, K9)), ALU.add).then_inc(om_ready.sem, 1)
                    dve.wait_ge(om_ready.sem, om_ready.at(i, 3 + s))
                    far_flag(own, s, om[s][:, 0:2].rearrange("p g t k -> p (g t k)"), NEAR)
                    load_flag(i, 2 + s)
                for s in range(2):
                    wait_apart(dve, (far_ready, far_ready.at(i, s + 3)), (mask_ready, mask_ready.at(i, 3 + s)))
                    far = dve.value_load(flag[s][0:1, 0:1])
                    with dve.If(far > 0):
                        count = [0]
                        tap = [None]

                        def gstep(ins):
                            ins.then_inc(g_own.sem, 1)
                            count[0] += 1

                        def gsettle():
                            v = g_own.at(i, G_OWN * s + count[0])
                            dve.wait_ge(g_own.sem, v if tap[0] is None else v + tap[0] * 4)

                        tile_order(s, img[s]).then_inc(g_strips.sem, 1)
                        o2 = om[s][:, 0:2].rearrange("p g t k -> p (g t k)")
                        gstep(v_.tensor_tensor(o2, o2, tab[:, T_POS:T_POS + 2 * TILES * K9], ALU.add))
                        wait_apart(dve, (g_own, g_own.at(i, G_OWN * s + count[0])))
                        with dve.Fori(0, K9) as k:
                            tap[0] = k
                            dve.wait_ge(g_GTt.sem, g_GTt.at(i, K9 * TILES * s + k * TILES))
                            uv = om[s][:, 0:2].rearrange("p g t k -> p (g t) k")[:, :, bass.ds(k, 1)]
                            m = mk[s][:].rearrange("p (t k) -> p t k", k=K9)[:, :, bass.ds(k, 1)]
                            hats_dense(s, gsettle, gstep, uv, m, 2.0)
                            dense(i, K9 * TILES * s + k * TILES, s, g_GT, g_GTt)
                        assert count[0] == 5
                        dve.wait_ge(g_GTt.sem, g_GTt.at(i, K9 * TILES * (s + 1)))
                        dve.sem_inc(n_own.sem, N_OWN)
                        dve.sem_inc(n_GT.sem, STEPS)
                        dve.sem_inc(n_blk.sem, STEPS)
                    with dve.Else():
                        cnt = [0]

                        def nstep(ins):
                            ins.then_inc(n_own.sem, 1)
                            cnt[0] += 1

                        def nsettle():
                            dve.wait_ge(n_own.sem, n_own.at(i, N_OWN * s + cnt[0]))

                        TK = TILES * K9
                        dyx = om[s][:].rearrange("p g t k -> p g (t k)")
                        nstep(v_.tensor_tensor(hfy[s][:], tab[:, T_EY:T_EY + BR].unsqueeze(1).broadcast_to((C, TK, BR)),
                                               dyx[:, 0, :].unsqueeze(2).broadcast_to((C, TK, BR)), ALU.subtract))
                        nstep(v_.tensor_tensor(
                            hfx[s][:].rearrange("p (t k) b -> p t k b", k=K9),
                            tab[:, T_EX:T_EX + K9 * BC].rearrange("p (k b) -> p k b", b=BC).unsqueeze(1)
                            .broadcast_to((C, TILES, K9, BC)),
                            om[s][:, 1].unsqueeze(3).broadcast_to((C, TILES, K9, BC)), ALU.subtract))
                        nsettle()
                        for hf in (hfy[s], hfx[s]):
                            nstep(v_.scalar_tensor_tensor(hf[:], hf[:], -1.0, hf[:], ALU.mult, ALU.max))
                        nsettle()
                        for hf in (hfy[s], hfx[s]):
                            nstep(v_.tensor_scalar(hf[:], hf[:], 1.0, 0.0, ALU.subtract, ALU.min))
                        nsettle()
                        nstep(v_.scalar_tensor_tensor(hfx[s][:], hfx[s][:], 2.0,
                                                      mk[s][:].unsqueeze(2).broadcast_to((C, TK, BC)),
                                                      ALU.mult, ALU.mult))
                        nsettle()
                        assert cnt[0] == N_OWN
                        hy = hfy[s][:].rearrange("p (t k) a -> p t k a", k=K9)
                        hx = hfx[s][:].rearrange("p (t k) b -> p t k b", k=K9)
                        for n in range(STEPS + 1):
                            if n < STEPS:
                                t, ki = n // 3, n % 3
                                o = first_step(1, s) + n
                                if o >= 2:
                                    dve.wait_ge(n_Gp.sem, n_Gp.at(i, o - 1))
                                three = slice(3 * ki, 3 * ki + 3)
                                v_.tensor_tensor(GT1[n % 2][:].rearrange("p k (a b) -> p k a b", b=BC),
                                                 hy[:, t, three, :].unsqueeze(3).broadcast_to((C, 3, BR, BC)),
                                                 hx[:, t, three, :].unsqueeze(2).broadcast_to((C, 3, BR, BC)),
                                                 ALU.mult).then_inc(n_GT.sem, 1)
                            if n:
                                block_copy(i, first_step(1, s) + n - 1, (n - 1) % 2)
                        dve.wait_ge(n_blk.sem, n_blk.at(i, first_step(1, s) + STEPS))
                        dve.sem_inc(g_strips.sem, 1)
                        dve.sem_inc(g_own.sem, G_OWN)
                        dve.sem_inc(g_GT.sem, K9 * TILES)
                for s in range(2):
                    dve.wait_ge(conv_ready.sem, conv_ready.at(i, 3 + s))
                    v_.scalar_tensor_tensor(x[s][:], psO[0][:].rearrange("p b c -> p (b c)"),
                                            vec[:, V_B1:V_B1 + 1], x[s][:], ALU.add, ALU.add).then_inc(added.sem, 1)
                    dve.wait_ge(added.sem, added.at(i, 3 + s))
                    stats(own, 4 + s, x[s])
                    affine(own, 4 + s)
                for s in range(2):
                    dve.wait_ge(conv_ready.sem, conv_ready.at(i, 5 + s))
                    v_.scalar_tensor_tensor(x[s][:], psO[1 - s][:].rearrange("p b c -> p (b c)"),
                                            vec[:, V_B2:V_B2 + 1], x[s][:], ALU.add, ALU.add).then_inc(added.sem, 1)
                    dve.wait_ge(added.sem, added.at(i, 5 + s))
                    stats(own, 6 + s, x[s])
                    affine(own, 6 + s)
                if more:
                    start_stats(nxt)
                img3 = lambda t: t[:, :].rearrange("p (r c) -> p r c", c=W)
                for v in range(2):
                    src, rows, cols = ((x2p, H, LW), (ahp, H + 2 * LPAD, W))[v]

                    def shifted(t, d, v=v):
                        return t[:, :, d:d + W] if v == 0 else t[:, d:d + H, :]

                    if v == 0:
                        dve.wait_ge(l3_act.sem, l3_act.at(i, 1))
                    else:
                        dve.wait_ge(l3_product.sem, l3_product.at(i, 3 + TAPS))
                    w_at = (V_DWH, V_DWV)[v]
                    b_at = (V_DWHB, V_DWVB)[v]
                    own.step(v_.tensor_scalar(img3(dwo), shifted(src, 0), vec[:, w_at:w_at + 1],
                                              vec[:, b_at:b_at + 1], ALU.mult, ALU.add))
                    for d in range(1, 7):
                        own.settle()
                        ins = v_.scalar_tensor_tensor(img3(dwo), shifted(src, d), vec[:, w_at + d:w_at + d + 1],
                                                      img3(dwo), ALU.mult, ALU.add)
                        if d < 6:
                            own.step(ins)
                        else:
                            ins.then_inc(l3_dw.sem, 1)
                        if more and v == 0 and d == 2:
                            start_affine(nxt)
                        if more and v == 1 and d == 6:
                            start_offsets(nxt)
                    if v == 0:
                        pair = psum2[:, 0:H * (LW - 1)].rearrange("p (r c) -> p r c", c=LW - 1)
                        own.step(v_.tensor_tensor(pair, src[:, :, 0:LW - 1], src[:, :, 1:LW], ALU.add))
                        taps = [pair[:, :, 0:W], shifted(src, 2), shifted(src, 3), shifted(src, 4), pair[:, :, 5:5 + W]]
                    else:
                        pair = psum2[:, 0:(rows - 1) * W].rearrange("p (r c) -> p r c", c=W)
                        own.step(v_.tensor_tensor(pair, src[:, 0:rows - 1, :], src[:, 1:rows, :], ALU.add))
                        taps = [pair[:, 0:H, :], shifted(src, 2), shifted(src, 3), shifted(src, 4), pair[:, 5:5 + H, :]]
                    out = ahp[:, LPAD:LPAD + H, :] if v == 0 else img3(at)
                    own.settle()
                    for t in range(TAPS):
                        dve.wait_ge(l3_act.sem, l3_act.at(i, 4 + TAPS * v + t))
                        kt = kern[:, t, :].rearrange("p (r c) -> p r c", c=W)
                        dst = out if t == 0 else img3(tmp3)
                        own.step(v_.scalar_tensor_tensor(dst, taps[t], 0.5 if t in (0, 4) else 1.0, kt,
                                                         ALU.mult, ALU.mult))
                        own.settle()
                        if t:
                            if t == 4 and v == 1:
                                own.step(v_.scalar_tensor_tensor(out, out, 1.0, img3(tmp3), ALU.mult, ALU.add,
                                                                 accum_out=st3[:, 0:1]))
                            else:
                                own.step(v_.tensor_tensor(out, out, img3(tmp3), ALU.add))
                            own.settle()
                v_.tensor_scalar(wss[:], blk64, st3[:, 0:1], 1.0 / N, ALU.mult, ALU.mult).then_inc(l3_wss.sem, 1)
                if more:
                    start_hats(nxt, 0)
                dve.wait_ge(l3_product.sem, l3_product.at(i, 15))
                v_.scalar_tensor_tensor(tmp3, at[:], 1.0, psO[1][:].rearrange("p b c -> p (b c)"),
                                        ALU.mult, ALU.mult, accum_out=st3[:, 1:2]).then_inc(l3_csum.sem, 1)
                dve.wait_ge(l3_act.sem, l3_act.at(i, 14))
                v_.tensor_tensor(sm, sg, xc[:], ALU.mult).then_inc(l3_maps.sem, 1)
                dve.wait_ge(l3_csig.sem, l3_csig.at(i, 1))
                v_.tensor_scalar(wo2, woT[:, :, 1, :], st3[:, 2:3], None, ALU.mult).then_inc(l3_maps.sem, 1)
                if more:
                    start_hats(nxt, 1)
                for s in range(2):
                    dve.wait_ge(l3_product.sem, l3_product.at(i, 16 + s))
                    dve.wait_ge(yout_free.sem, yout_free.at(i, 0))
                    v_.scalar_tensor_tensor(yout[s][:], psO[s][:].rearrange("p b c -> p (b c)"),
                                            vec[:, V_BOUT:V_BOUT + 1], x[s][:], ALU.add, ALU.add)\
                        .then_inc(y_ready.sem, 1)
                assert own.n == DVE_STEPS and nxt.n == (START_STEPS if more else 0), (own.n, nxt.n)

            first = Own(dve, start_own, 0)
            start_stats(first)
            start_affine(first)
            start_offsets(first)
            for s in range(2):
                start_hats(first, s)
            assert first.n == START_STEPS, first.n
            if PASSES > 1:
                with dve.Fori(0, PASSES - 1) as i:
                    one_pass(i, True)
            one_pass(PASSES - 1, False)


def tables():
    import numpy as np

    tab = np.zeros((C, TAB_N), np.float32)
    p = np.arange(C)
    row, col = p // SW, p % SW
    t = np.arange(TILES)
    y = 16 * (t % 2)[None, :] + row[:, None]
    x = SW * (t // 2)[None, :] + col[:, None]
    k = np.arange(K9)
    tab[:, T_IOTA:T_IOTA + 32] = np.arange(32)
    tab[:, T_GAVG:T_GAVG + C] = (p[:, None] // GROUP == p[None, :] // GROUP) / GROUP
    tab[:, T_ONES:T_ONES + C] = 1
    tab[:, T_BLK:T_BLK + C] = (p[:, None] // C2 == p[None, :] // C2) / C2
    line = np.linspace(-1, 1, W, dtype=np.float32)
    tab[:, T_LIN:T_LIN + 2 * TILES] = np.concatenate([line[y], line[x]], 1)
    pos = np.stack([y[:, :, None] + k // 3 - 1, x[:, :, None] + k % 3 - 1], 1)
    tab[:, T_POS:T_POS + 2 * TILES * K9] = pos.reshape(C, -1)
    tab[:, T_EY:T_EY + BR] = np.arange(BR)[None, :] - (row % 8)[:, None] - 1
    ex = np.arange(BC)[None, None, :] - col[:, None, None] - (k % 3)[None, :, None] - 1
    tab[:, T_EX:T_EX + K9 * BC] = ex.reshape(C, -1)
    tab[:, T_SEL:T_SEL + 32] = p[:, None] % 32 == np.arange(32)
    origin = np.concatenate([16 * (t % 2) - PAD, SW * (t // 2) - PAD])
    tab[:, T_ORG:T_ORG + 2 * TILES] = -origin[None, :]
    return tab


def layout(a):
    import numpy as np

    wide = lambda w: np.concatenate([w, np.zeros((32 - len(w),) + w.shape[1:], w.dtype)])
    both = lambda v: np.concatenate([v, v])
    taps = lambda w: np.ascontiguousarray(w.transpose(1, 2, 3, 0).reshape(w.shape[1], K9, w.shape[0]))

    def diagonal(w):
        z = np.zeros((2, w.shape[0], 2, w.shape[1]), np.float32)
        z[0, :, 0] = w
        z[1, :, 1] = w
        return z.reshape(2 * w.shape[0], 2 * w.shape[1])

    def output_weights(w):
        z = np.zeros((2, C2, 2, 2, C), np.float32)
        for s in range(2):
            for m in range(2):
                z[s, :, s, m] = w[C2 * m:C2 * m + C2]
        return z.reshape(C, 2, 2, C)

    def strip(w, b):
        heads = np.arange(C2) // (C2 // 8)
        ws = np.stack([diagonal(w[heads * TAPS + t].T) for t in range(TAPS)], 1)
        return np.ascontiguousarray(ws), np.stack([both(b[heads * TAPS + t]) for t in range(TAPS)], 1)

    kh, khb = strip(a["L3_conv_hk_pw_w"], a["L3_conv_hk_pw_b"])
    kv, kvb = strip(a["L3_conv_vk_pw_w"], a["L3_conv_vk_pw_b"])
    bin_ = a["L3_conv_proj_in_b"]
    cb1 = a["L3_conv_cb_b1"]
    vec = np.zeros((C, V_N), np.float32)
    vec[:, V_B1] = a["L1_conv_b"]
    vec[:, V_B2] = a["L2_conv_bias"]
    vec[:, V_BIN1] = both(bin_[:C2])
    vec[:, V_BIN2] = both(bin_[C2:])
    vec[:, V_BCB1] = both(both(cb1))
    vec[:, V_BCB2] = both(a["L3_conv_cb_b2"])
    vec[:, V_BOUT] = a["L3_conv_proj_out_b"]
    vec[:, V_DWHB] = both(a["L3_conv_hk_dw_b"])
    vec[:, V_DWVB] = both(a["L3_conv_vk_dw_b"])
    vec[:, V_DWH:V_DWH + 7] = both(a["L3_conv_hk_dw_w"].reshape(C2, 7))
    vec[:, V_DWV:V_DWV + 7] = both(a["L3_conv_vk_dw_w"].reshape(C2, 7))
    vec[:, V_KHB:V_KHB + TAPS] = khb
    vec[:, V_KVB:V_KVB + TAPS] = kvb
    vec[:, V_DW0:V_DW0 + K9] = a["L0_conv_w_dw"].reshape(C, K9)

    off = np.arange(2 * K9).reshape(K9, 2).T.reshape(-1)
    w1off = np.concatenate([a["L1_conv_off_w"][off], a["L1_conv_mod_w"]])
    b1off = np.concatenate([a["L1_conv_off_b"][off], a["L1_conv_mod_b"], a["L0_conv_b_off"]])
    x = a["x"]
    wo = a["L3_conv_proj_out_w"].T
    return {
        "x": x.reshape(x.shape[0], C, N),
        "ident": np.eye(C, dtype=np.float32),
        "tab": tables(),
        "vec": vec,
        "offb": np.ascontiguousarray(np.broadcast_to(b1off, (C, 30))),
        "w0off": taps(wide(a["L0_conv_w_off"])),
        "pwT": a["L0_conv_w_pw"].reshape(C, C).T,
        "w1off": taps(wide(w1off)),
        "w1": taps(a["L1_conv_w"]),
        "w2": taps(a["L2_conv_weight"]),
        "r2": taps(a["L2_conv_r_matrix"]).reshape(C, K9 * C),
        "win": a["L3_conv_proj_in_w"][:C2],
        "win2T": a["L3_conv_proj_in_w"][C2:].T,
        "cb1T": both(a["L3_conv_cb_w1"]).T,
        "cb2T": np.concatenate([diagonal(a["L3_conv_cb_w2"].T), np.zeros((C2, C), np.float32)]),
        "kh": kh,
        "kv": kv,
        "woT": output_weights(wo),
    }


def kernel(**inputs):
    import numpy as np
    import concourse.bacc as bacc
    from concourse.bass_utils import run_bass_kernel_spmd

    arrays = {k: np.ascontiguousarray(v) for k, v in layout({k: np.asarray(v) for k, v in inputs.items()}).items()}
    nc = bacc.Bacc("TRN2", target_bir_lowering=False, num_devices=1)
    args = [nc.dram_tensor(f"in_{k}", v.shape, mybir.dt.from_np(v.dtype), kind="ExternalInput").ap()
            for k, v in arrays.items()]
    out = nc.dram_tensor("out", arrays["x"].shape, F32, kind="ExternalOutput").ap()
    conv_preact_kernel(nc, *args, out)
    r = run_bass_kernel_spmd(nc, [{f"in_{k}": v for k, v in arrays.items()}], core_ids=[0])
    return r.results[0]["out"].reshape(inputs["x"].shape)
```

```python
from contextlib import ExitStack

import concourse.bass as bass
from concourse import mybir

F32 = mybir.dt.float32
I32 = mybir.dt.int32
ALU = mybir.AluOpType
ACT = mybir.ActivationFunctionType
AX = mybir.AxisListType

C = 128
H = W = 32
N = H * W
HALF = 512
PAD = 2
PW = W + 2 * PAD
TILES = 8
STRIPS = 4
SW = W // STRIPS
K9 = 9
GROUP = 4
EPS = 1e-5
BR, BC = 10, 12
BLK = BR * BC
C2 = 64
TAPS = 5
LPAD = 3
LW = W + 2 * LPAD

V_B1, V_B2, V_BIN1, V_BIN2, V_BCB1, V_BCB2, V_BOUT, V_DWHB, V_DWVB = range(9)
V_DWH, V_DWV = 9, 16
V_KHB, V_KVB = 23, 28
V_DW0 = 33
V_N = 42

T_IOTA = 0
T_GAVG = T_IOTA + 32
T_ONES = T_GAVG + C
T_BLK = T_ONES + C
T_LIN = T_BLK + C
T_POS = T_LIN + 2 * TILES
T_EY = T_POS + 2 * TILES * K9
T_EX = T_EY + BR
T_SEL = T_EX + K9 * BC
T_ORG = T_SEL + 32
TAB_N = T_ORG + 2 * TILES
NEAR0, NEAR = 2.0, 1.0
EARLY, LATE = 6, 9
DVE_STEPS = 109
START_STEPS = 30


class Signal:

    def __init__(self, sem, per_pass, start=1):
        self.sem, self.per_pass, self.start = sem, per_pass, start

    def at(self, i, n):
        assert self.start or n
        return i * self.per_pass + n + self.start


class Own:

    def __init__(self, eng, steps, i):
        self.eng, self.steps, self.i, self.n = eng, steps, i, 0

    def finished(self, n):
        self.eng.wait_ge(self.steps.sem, self.steps.at(self.i, n))

    def step(self, ins):
        ins.then_inc(self.steps.sem, 1)
        self.n += 1

    def settle(self):
        self.eng.wait_ge(self.steps.sem, self.steps.at(self.i, self.n))


def conv_preact_kernel(nc, x_d, ident_d, tab_d, vec_d, offb_d, w0off_d, w0dw_pw_d, w1off_d, w1_d, w2_d, r2_d,
                       win_d, win2T_d, cb1T_d, cb2T_d, kh_d, kv_d, woT_d, out_d):
    PASSES = x_d.shape[0] // 2
    with ExitStack() as ctx:
        def sb(name, shape, dt=F32):
            return ctx.enter_context(nc.sbuf_tensor(name, shape, dt))

        def sem(name):
            return ctx.enter_context(nc.semaphore(name))

        signals = []

        def signal(name, per_pass):
            signals.append(Signal(sem(name), per_pass))
            return signals[-1]

        ident = sb("ident", [C, C])
        tab = sb("tab", [C, TAB_N])
        vec = sb("vec", [C, V_N])
        offb = sb("offb", [C, 30])
        w0off = sb("w0off", [C, K9, 32])
        pwT = sb("pwT", [C, C])
        w0 = sb("w0", [C, K9, C])
        w1off = sb("w1off", [C, K9, 32])
        w1 = sb("w1", [C, K9, C])
        w2 = sb("w2", [C, K9, C])
        win = sb("win", [C2, C])
        win2T = sb("win2T", [C, C2])
        cb1T = sb("cb1T", [C2, C2])
        cb2T = sb("cb2T", [C, C])
        kh_w = sb("kh_w", [C, TAPS, C])
        kv_w = sb("kv_w", [C, TAPS, C])
        woT = sb("woT", [C, 2, 2, C])
        wu = sb("wu", [C, C2])
        bu = sb("bu", [C2, 1])

        xin = [sb(f"xin{s}", [C, N]) for s in range(2)]
        x = [sb(f"x{s}", [C, N]) for s in range(2)]
        yout = [sb(f"yout{s}", [C, N]) for s in range(2)]
        xn = [sb(f"xn{s}", [C, PW, PW]) for s in range(2)]
        img = [sb(f"img{s}", [C, PW, PW]) for s in range(2)]
        gst = [sb(f"gst{s}", [C, 21]) for s in range(2)]
        gst0 = [sb(f"gst0{s}", [C, 21]) for s in range(2)]
        om = [sb(f"om{s}", [C, 3, TILES, K9]) for s in range(2)]
        om0 = [sb(f"om0{s}", [C, 3, TILES]) for s in range(2)]
        mk = [sb(f"mk{s}", [C, TILES * K9]) for s in range(2)]
        xT = [sb(f"xT{s}", [C, TILES, C]) for s in range(2)]
        hat = [sb(f"hat{s}", [C, 2 * TILES, 32]) for s in range(2)]
        hfy = [sb(f"hfy{s}", [C, TILES * K9, BR]) for s in range(2)]
        hfx = [sb(f"hfx{s}", [C, TILES * K9, BC]) for s in range(2)]
        pool_v = sb("pool_v", [C, H, W + 2])
        neg_half = sb("neg_half", [C, 1])
        GTs = sb("GTs", [C, 2, N])
        GT = [GTs[:, b, :] for b in range(2)]
        Gd = [sb(f"Gd{b}", [C, TILES, C]) for b in range(2)]
        GT1 = [sb(f"GT1{b}", [C, 3, BLK]) for b in range(2)]
        G1 = [sb(f"G1{b}", [BLK, 3, C]) for b in range(2)]
        xblk = [sb(f"xblk{b}", [BLK, 2, C]) for b in range(2)]
        samp = sb("samp", [C, K9, N])
        off_parts = [Gd[s][:].rearrange("p q c -> p (q c)") for s in range(2)]
        q_strips = [sb(f"q_strips{s}", [C, N]) for s in range(2)]
        strip12 = [sb(f"strip12{s}", [C, STRIPS, PW, BC]) for s in range(2)]
        flag = [sb(f"flag{s}", [C, 1], I32) for s in range(2)]
        flagf = [sb(f"flagf{s}", [C, 2]) for s in range(2)]
        x2p = sb("x2p", [C, H, LW])
        ahp = sb("ahp", [C, H + 2 * LPAD, W])
        kern, dwo, tmp3, sg, sm = samp[:, 0:TAPS, :], *(samp[:, TAPS + n, :] for n in range(4))
        psum2 = GTs[:].rearrange("p b q -> p (b q)")
        u3 = sb("u3", [C, N])
        xc = sb("xc", [C, N])
        xm = q_strips[1]
        at = sb("at", [C, N])
        wss = xT[0][:, 2, :]
        wo2 = xT[0][:, 0:2, :]
        st3 = sb("st3", [C, 5])

        ps = [ctx.enter_context(nc.psum_tensor(f"ps{b}", [C, HALF], F32)) for b in range(2)]
        psO = [ctx.enter_context(nc.psum_tensor(f"psO{b}", [C, 2, HALF], F32)) for b in range(2)]
        psT = ctx.enter_context(nc.psum_tensor("psT", [C, 2, HALF], F32))

        iota32 = tab[:, T_IOTA:T_IOTA + 32]
        gavg = tab[:, T_GAVG:T_GAVG + C]
        ones = tab[:, T_ONES:T_ONES + C]
        blk64 = tab[:, T_BLK:T_BLK + C]

        passed = {eng: sem(f"passed_{name}") for eng, name in ((nc.tensor, "pe"), (nc.scalar, "act"), (nc.vector, "dve"))}
        early_landed = sem("early_landed")
        late_landed = sem("late_landed")
        borders_zero = sem("borders_zero")
        prep = sem("prep")
        prep_dve = sem("prep_dve")
        weights_ready = sem("weights_ready")
        w2_landed = sem("w2_landed")
        x_landed = [Signal(sem(f"x_landed{s}"), 16, 0) for s in range(2)]
        y_ready = signal("y_ready", 2)
        yout_free = signal("yout_free", 2)
        y_stored = [Signal(sem(f"y_stored{s}"), 16, 0) for s in range(2)]
        stats_ready = signal("stats_ready", 8)
        group_ready = signal("group_ready", 8)
        var_ready = signal("var_ready", 8)
        rstd_ready = signal("rstd_ready", 8)
        affine_ready = signal("affine_ready", 8)
        xn_ready = signal("xn_ready", 8)
        pooled_ready = signal("pooled_ready", 2)
        strips_ready = signal("strips_ready", 2)
        parts_product = signal("parts_product", 4)
        parts_ready = signal("parts_ready", 4)
        wide_ready = signal("wide_ready", 4)
        xT_product = signal("xT_product", 2)
        xT_ready = signal("xT_ready", 2)
        offs_ready = signal("offs_ready", 4)
        om_ready = signal("om_ready", 4)
        mask_ready = signal("mask_ready", 4)
        GT_ready = signal("GT_ready", 2 * TILES)
        GTt_ready = signal("GTt_ready", 2 * TILES)
        Gd_ready = signal("Gd_ready", 2 * TILES)
        sampled = signal("sampled", 2 * TILES)
        img_ready = signal("img_ready", 2)
        conv_ready = signal("conv_ready", 6)
        added = signal("added", 6)
        far_count = signal("far_count", 4)
        far_input = signal("far_input", 4)
        far_ready = signal("far_ready", 4)
        G_OWN = 1 + K9 * 4
        g_strips = signal("g_strips", 2)
        g_xTp = signal("g_xTp", 2)
        g_xT = signal("g_xT", 2)
        g_own = signal("g_own", 2 * G_OWN)
        g_GT = signal("g_GT", 2 * K9 * TILES)
        g_GTt = signal("g_GTt", 2 * K9 * TILES)
        g_Gd = signal("g_Gd", 2 * K9 * TILES)
        g_smp = signal("g_smp", 2 * K9 * TILES)
        g_smp_sb = signal("g_smp_sb", 2 * K9)
        STEPS = TILES * 3
        POOL_AT = (6, 10, 14, 18)
        N_OWN = 7
        n_own = signal("n_own", 2 * N_OWN)
        n_GT = signal("n_GT", 2 * (TILES + STEPS))
        n_blkp = signal("n_blkp", 2 * (TILES + STEPS))
        n_Gp = signal("n_Gp", 2 * (TILES + STEPS))
        n_blk = signal("n_blk", 2 * (TILES + STEPS))
        n_G = signal("n_G", 2 * (TILES + STEPS))
        n_smp = signal("n_smp", 2 * (TILES + STEPS))
        n_smp_sb = signal("n_smp_sb", 2 * STEPS)

        def first_step(layer, s):
            return (2 * TILES + STEPS * s) if layer else TILES * s

        P_X2, P_U, P_XC = 1, 3, 5
        P_MEAN = 7
        P_KERN = 9
        P_GATE = P_KERN + 4 * TAPS
        P_OUT = P_GATE + 2
        l3_product = signal("l3_product", P_OUT + 1)
        l3_act = signal("l3_act", P_GATE + 1)
        l3_dw = signal("l3_dw", 4)
        l3_wss = signal("l3_wss", 1)
        l3_csum = signal("l3_csum", 1)
        l3_csig = signal("l3_csig", 1)
        l3_maps = signal("l3_maps", 2)
        dve_own = signal("dve_own", DVE_STEPS)
        start_own = signal("start_own", START_STEPS)

        def inner(t):
            return t[:, PAD:PAD + H, PAD:PAD + W]

        def norm(n):
            return (gst0 if n < 2 else gst)[n % 2]

        def block0_norm(s, first):
            return s if first else s - 2

        def block3_norm(s, more):
            return (8 if more else 6) + s

        def bank(m):
            return psO[(m - 1) // 2 % 2][:, (m - 1) % 2, :]

        def tiled(t, b):
            return t[:, :, 16 * b:16 * b + 16].rearrange("p r (j c) -> p j r c", c=SW)

        def wait_apart(eng, *waits):
            for signal, value in waits:
                eng.wait_ge(signal.sem, value)
            eng.sem_inc(passed[eng], 1)

        block = ctx.enter_context(nc.Block())

        @block.sync
        def _(sp):
            for s in range(2):
                sp.dma_start(xin[s][:], x_d[s, :, :]).then_inc(x_landed[s].sem, 16)
            for dst, src in ((tab, tab_d), (vec, vec_d), (w0off, w0off_d), (offb, offb_d), (pwT, w0dw_pw_d),
                             (ident, ident_d)):
                sp.dma_start(dst[:], src).then_inc(early_landed, 16)
            sp.dma_start(w2[:], w2_d).then_inc(w2_landed, 16)
            sp.dma_start(samp[:, 0:2, :].rearrange("p a b -> p (a b)")[:, 0:K9 * C], r2_d).then_inc(w2_landed, 16)
            for dst, src in ((w1off, w1off_d), (win, win_d), (win2T, win2T_d), (cb1T, cb1T_d), (cb2T, cb2T_d), (w1, w1_d),
                             (kh_w, kh_d), (kv_w, kv_d), (woT, woT_d)):
                sp.dma_start(dst[:], src).then_inc(late_landed, 16)

            def store(i, s):
                sp.wait_ge(y_ready.sem, y_ready.at(i, s + 1))
                sp.dma_start(out_d[2 * i + s, :, :], yout[s][:]).then_inc(y_stored[s].sem, 16)

            if PASSES > 1:
                with sp.Fori(0, PASSES - 1) as i:
                    for s in range(2):
                        sp.wait_ge(added.sem, added.at(i, s + 1))
                        sp.dma_start(xin[s][:], x_d[2 * i + 2 + s, :, :]).then_inc(x_landed[s].sem, 16)
                    for s in range(2):
                        store(i, s)
                    for s in range(2):
                        sp.wait_ge(y_stored[s].sem, y_stored[s].at(i, 16))
                        sp.sem_inc(yout_free.sem, 1)
            for s in range(2):
                store(PASSES - 1, s)
            for s in range(2):
                sp.wait_ge(y_stored[s].sem, y_stored[s].at(PASSES - 1, 16))

        @block.gpsimd
        def _(pool):
            for each in signals:
                pool.sem_inc(each.sem, each.start)
            for t in (xn[0], xn[1], img[0], img[1], x2p, ahp, u3):
                nc.gpsimd.memset(t[:], 0.0).then_inc(borders_zero, 1)
            nc.gpsimd.memset(neg_half[:], -0.5).then_inc(borders_zero, 1)
            pool.wait_ge(borders_zero, 8)

            def rsqrt(i, n):
                g = norm(n)
                pool.wait_ge(var_ready.sem, var_ready.at(i, n + 1))
                nc.gpsimd.tensor_tensor(out=g[:, 18:19], in0=g[:, 17:18], in1=neg_half[:],
                                        op=ALU.pow).then_inc(rstd_ready.sem, 1)

            def one_pass(i, more):
                for n in range(2, 6):
                    rsqrt(i, n)
                if more:
                    for s in range(2):
                        rsqrt(i + 1, block0_norm(s, False))
                for s in range(2):
                    rsqrt(i, block3_norm(s, more))

            for s in range(2):
                rsqrt(0, block0_norm(s, True))
            if PASSES > 1:
                with pool.Fori(0, PASSES - 1) as i:
                    one_pass(i, True)
            one_pass(PASSES - 1, False)

        @block.tensor
        def _(pe):
            mm = nc.tensor.matmul
            pe.wait_ge(early_landed, EARLY * 16)

            def group_mean(i, n):
                pe.wait_ge(stats_ready.sem, stats_ready.at(i, n + 1))
                g = norm(n)
                mm(ps[n % 2][:, 0:2], gavg, g[:, 12:14], start=True, stop=True).then_inc(group_ready.sem, 1)

            def offset_parts(n, src, w):
                dst = psO[n % 2] if n >= 2 else psT
                for h in range(2):
                    for k in range(K9):
                        g = (K9 * h + k) % 4
                        last = mm(dst[32 * g:32 * g + 32, h, :], w[:, k, :], window(src)(h, k),
                                  start=(k < 4), stop=(k >= K9 - 4), skip_group_check=True)
                last.then_inc(parts_product.sem, 1)

            def offsets(i, n, m):
                s = n % 2
                pe.wait_ge(parts_ready.sem, parts_ready.at(i, n + 1))
                for t in range(TILES):
                    last = mm(ps[s][:, 4 + m * t:4 + m * t + m], off_parts[s][:, C * t:C * t + C],
                              tab[:, T_SEL:T_SEL + m], start=True, stop=True)
                last.then_inc(offs_ready.sem, 1)

            def image_T(s, finished):
                for q in range(TILES):
                    last = nc.tensor.transpose(psT[:, q // 4, C * (q % 4):C * (q % 4) + C],
                                               q_strips[s][:, C * q:C * q + C], ident[:])
                last.then_inc(finished.sem, 1)

            def conv(dst, wgt, rhs, between={}):
                for h in range(2):
                    for k in range(K9):
                        if (h, k) in between:
                            between[h, k]()
                        last = mm(dst[:, h, :], wgt[:, k, :], rhs(h, k), start=(k == 0), stop=(k == K9 - 1))
                last.then_inc(conv_ready.sem, 1)

            def window(src):
                return lambda h, k: src[:, PAD + 16 * h + k // 3 - 1:PAD + 16 * h + k // 3 + 15,
                                        PAD + k % 3 - 1:PAD + k % 3 - 1 + W]

            def dense(i, base, dst, xTs, GTr, GTt, Gdr, smp):
                for t in range(TILES + 1):
                    if t < TILES:
                        pe.wait_ge(GTr.sem, GTr.at(i, base + t + 1))
                        pe.wait_ge(Gdr.sem, Gdr.at(i, base + t))
                        for q in range(TILES):
                            last = nc.tensor.transpose(psT[:, q // 4, C * (q % 4):C * (q % 4) + C],
                                                       GT[t % 2][:, C * q:C * q + C], ident[:])
                        last.then_inc(GTt.sem, 1)
                    if t:
                        p = t - 1
                        pe.wait_ge(Gdr.sem, Gdr.at(i, base + p + 1))
                        for q in range(TILES):
                            last = mm(dst[:, p // 4, C * (p % 4):C * (p % 4) + C], xTs[:, q, :], Gd[p % 2][:, q, :],
                                      start=(q == 0), stop=(q == TILES - 1))
                        last.then_inc(smp.sem, 1)

            def near0(i, s):
                for n in range(TILES + 1):
                    if n < TILES:
                        o = first_step(0, s) + n
                        pe.wait_ge(n_blk.sem, n_blk.at(i, o))
                        for u in range(2):
                            r0 = 16 * (n % 2) + BR * u
                            b = strip12[s][:, n // 2, r0:r0 + BR, :].rearrange("p r c -> p (r c)")
                            last = nc.tensor.transpose(psT[0:BLK, 1, C * u:C * u + C], b, ident[:])
                        last.then_inc(n_blkp.sem, 1)
                        pe.wait_ge(n_GT.sem, n_GT.at(i, o + 1))
                        pe.wait_ge(n_G.sem, n_G.at(i, o))
                        for u in range(2):
                            last = nc.tensor.transpose(psT[0:BLK, 0, C * u:C * u + C], GT1[n % 2][:, u, :], ident[:])
                        last.then_inc(n_Gp.sem, 1)
                    if n:
                        p = n - 1
                        o = first_step(0, s) + p
                        pe.wait_ge(n_blk.sem, n_blk.at(i, o + 1))
                        pe.wait_ge(n_G.sem, n_G.at(i, o + 1))
                        for u in range(2):
                            last = mm(psO[s][:, p // 4, C * (p % 4):C * (p % 4) + C], xblk[p % 2][:, u, :],
                                      G1[p % 2][:, u, :], start=(u == 0), stop=(u == 1))
                        last.then_inc(n_smp.sem, 1)

            def near(i, s):
                for n in range(STEPS + 1):
                    if n < STEPS:
                        t, ki = n // 3, n % 3
                        o = first_step(1, s) + n
                        pe.wait_ge(n_blk.sem, n_blk.at(i, o))
                        for h in range(2):
                            r0 = 16 * (t % 2) + 8 * h + ki
                            b = strip12[s][:, t // 2, r0:r0 + BR, :].rearrange("p r c -> p (r c)")
                            last = nc.tensor.transpose(psT[0:BLK, 1, C * h:C * h + C], b, ident[:])
                        last.then_inc(n_blkp.sem, 1)
                        pe.wait_ge(n_GT.sem, n_GT.at(i, o + 1))
                        pe.wait_ge(n_G.sem, n_G.at(i, o))
                        for kj in range(3):
                            last = nc.tensor.transpose(psT[0:BLK, 0, C * kj:C * kj + C], GT1[n % 2][:, kj, :], ident[:])
                        last.then_inc(n_Gp.sem, 1)
                    if n:
                        p = n - 1
                        o = first_step(1, s) + p
                        pe.wait_ge(n_blk.sem, n_blk.at(i, o + 1))
                        pe.wait_ge(n_G.sem, n_G.at(i, o + 1))
                        if STEPS * s + p >= 2:
                            pe.wait_ge(n_smp_sb.sem, n_smp_sb.at(i, STEPS * s + p - 1))
                        dst = psO[1][:, p % 2, 0:3 * C].rearrange("p (k c) -> p k c", k=3)
                        for h in range(2):
                            half = slice(64 * h, 64 * h + 64)
                            last = mm(dst[:, :, half], xblk[p % 2][:, h, :], G1[p % 2][:, :, half],
                                      start=True, stop=True)
                        last.then_inc(n_smp.sem, 1)

            def far(i, n):
                pe.wait_ge(far_input.sem, far_input.at(i, n + 1))
                mm(ps[n % 2][:, 2:3], ones, flagf[n % 2][:, 0:1], start=True, stop=True).then_inc(far_count.sem, 1)

            def start_means(j, first):
                for s in range(2):
                    group_mean(j, block0_norm(s, first))

            def start_parts(j, s):
                pe.wait_ge(xn_ready.sem, xn_ready.at(j, s + 1))
                if s:
                    pe.wait_ge(parts_ready.sem, parts_ready.at(j, 1))
                offset_parts(s, xn[s], w0off)

            def start_offsets(j):
                for s in range(2):
                    offsets(j, s, 3)

            def start_far(j):
                for s in range(2):
                    far(j, s)

            def one_pass(i, more):
                pe.wait_ge(y_ready.sem, y_ready.at(i, 0))
                for s in range(2):
                    wait_apart(pe, (far_ready, far_ready.at(i, s + 1)))
                    is_far = pe.value_load(flag[s][0:1, 0:1])
                    with pe.If(is_far > 0):
                        pe.wait_ge(strips_ready.sem, strips_ready.at(i, s + 1))
                        image_T(s, xT_product)
                        pe.wait_ge(xT_ready.sem, xT_ready.at(i, s + 1))
                        dense(i, TILES * s, psO[s], xT[s], GT_ready, GTt_ready, Gd_ready, sampled)
                        pe.wait_ge(sampled.sem, sampled.at(i, TILES * (s + 1)))
                        for each in (n_blkp, n_Gp, n_smp):
                            pe.sem_inc(each.sem, TILES)
                    with pe.Else():
                        pe.wait_ge(wide_ready.sem, wide_ready.at(i, s + 1))
                        near0(i, s)
                        pe.wait_ge(n_smp.sem, n_smp.at(i, first_step(0, s) + TILES))
                        pe.sem_inc(xT_product.sem, 1)
                        pe.sem_inc(GTt_ready.sem, TILES)
                        pe.sem_inc(sampled.sem, TILES)
                for s in range(2):
                    pe.wait_ge(img_ready.sem, img_ready.at(i, s + 1))
                    conv(psO[s], w0, window(img[s]), {(0, 6): lambda: group_mean(i, 2)} if s else {})
                pe.wait_ge(pooled_ready.sem, pooled_ready.at(i, 1))
                offset_parts(2, img[0], w1off)
                group_mean(i, 3)
                offsets(i, 2, 27)
                far(i, 2)
                for s in range(2):
                    wait_apart(pe, (added, added.at(i, 2)), (far_ready, far_ready.at(i, s + 3)))
                    is_far = pe.value_load(flag[s][0:1, 0:1])
                    with pe.If(is_far > 0):
                        pe.wait_ge(g_strips.sem, g_strips.at(i, s + 1))
                        image_T(s, g_xTp)
                        wait_apart(pe, (g_xT, g_xT.at(i, s + 1)))
                        with pe.Fori(0, K9) as k:
                            pe.wait_ge(g_smp_sb.sem, g_smp_sb.at(i, K9 * s) + k)
                            dense(i, K9 * TILES * s + k * TILES, psO[1], xT[s], g_GT, g_GTt, g_Gd, g_smp)
                        pe.wait_ge(g_smp_sb.sem, g_smp_sb.at(i, K9 * (s + 1)))
                        for each in (n_blkp, n_Gp, n_smp):
                            pe.sem_inc(each.sem, STEPS)
                    with pe.Else():
                        pe.wait_ge(wide_ready.sem, wide_ready.at(i, s + 3))
                        near(i, s)
                        pe.wait_ge(n_smp_sb.sem, n_smp_sb.at(i, STEPS * (s + 1)))
                        pe.sem_inc(g_xTp.sem, 1)
                        pe.sem_inc(g_GTt.sem, K9 * TILES)
                        pe.sem_inc(g_smp.sem, K9 * TILES)

                    def samples(h, k):
                        return samp[:, k, HALF * h:HALF * h + HALF]

                    if s == 0:
                        pe.wait_ge(pooled_ready.sem, pooled_ready.at(i, 2))
                        offset_parts(3, img[1], w1off)
                        conv(psO[0], w1, samples, {(0, 4): lambda: offsets(i, 3, 27), (1, 0): lambda: far(i, 3)})
                    else:
                        pe.wait_ge(added.sem, added.at(i, 3))
                        conv(psO[0], w1, samples, {(0, 4): lambda: group_mean(i, 4)})
                pe.wait_ge(xn_ready.sem, xn_ready.at(i, 5))
                conv(psO[1], w2, window(xn[0]), {(0, 6): lambda: group_mean(i, 5),
                                                 **({(1, 4): lambda: start_means(i + 1, False)} if more else {})})
                pe.wait_ge(xn_ready.sem, xn_ready.at(i, 6))
                conv(psO[0], w2, window(xn[1]), {(0, 6): lambda: group_mean(i, block3_norm(0, more))})
                group_mean(i, block3_norm(1, more))
                pe.wait_ge(xn_ready.sem, xn_ready.at(i, 8))
                pe.wait_ge(added.sem, added.at(i, 6))

                def img_rows(s, h):
                    return xn[s][:, PAD + 16 * h:PAD + 16 * h + 16, PAD:PAD + W]

                def product(m):
                    if m > 4:
                        pe.wait_ge(l3_act.sem, l3_act.at(i, m - 4))
                    return bank(m)

                for h in range(2):
                    d = product(P_X2 + h)
                    for s in range(2):
                        last = mm(d[C2 * s:C2 * s + C2, :], win2T[:], img_rows(s, h), start=True, stop=True)
                    last.then_inc(l3_product.sem, 1)
                for h in range(2):
                    d = product(P_U + h)
                    for s in range(2):
                        last = mm(d[32 * s:32 * s + 32, :], wu[:, 32 * s:32 * s + 32], img_rows(s, h), start=True, stop=True)
                    last.then_inc(l3_product.sem, 1)

                def half(m, h, lhsT, rhs):
                    mm(product(m), lhsT, rhs[:, HALF * h:HALF * h + HALF], start=True, stop=True)\
                        .then_inc(l3_product.sem, 1)

                for h in range(2):
                    pe.wait_ge(l3_act.sem, l3_act.at(i, P_U + h))
                    half(P_XC + h, h, cb2T[:], u3)
                for h in range(2):
                    pe.wait_ge(l3_act.sem, l3_act.at(i, P_XC + h))
                    half(P_MEAN + h, h, blk64, xc)
                for v in range(2):
                    for h in range(2):
                        pe.wait_ge(l3_dw.sem, l3_dw.at(i, 2 * v + h + 1))
                        for t in range(TAPS):
                            half(P_KERN + TAPS * (2 * v + h) + t, h, (kh_w, kv_w)[v][:, t, :], dwo)
                        if more and v == 0:
                            start_parts(i + 1, h)
                            if h:
                                start_offsets(i + 1)
                if more:
                    start_far(i + 1)
                pe.wait_ge(l3_wss.sem, l3_wss.at(i, 1))
                for h in range(2):
                    half(P_GATE + h, h, wss, xc)
                pe.wait_ge(l3_maps.sem, l3_maps.at(i, 2))
                pe.wait_ge(l3_act.sem, l3_act.at(i, P_GATE + 1))
                for s in range(2):
                    for h in range(2):
                        hh = slice(HALF * h, HALF * h + HALF)
                        mm(psO[s][:, h, :], woT[:, s, 0, :], sm[:, hh], start=True, stop=False)
                        last = mm(psO[s][:, h, :], wo2[:, s, :], at[:, hh], start=False, stop=True)
                    last.then_inc(l3_product.sem, 1)

            start_means(0, True)
            start_parts(0, 0)
            start_parts(0, 1)
            start_offsets(0)
            start_far(0)
            pe.wait_ge(late_landed, LATE * 16)
            mm(psT[:, 0, 0:C2], win[:], cb1T[:], start=True, stop=True).then_inc(prep, 1)
            mm(psT[0:C2, 1, 0:1], cb1T[:], vec[0:C2, V_BIN1:V_BIN1 + 1], start=True, stop=True).then_inc(prep, 1)
            pe.wait_ge(weights_ready, 2)
            pe.wait_ge(borders_zero, 8)
            if PASSES > 1:
                with pe.Fori(0, PASSES - 1) as i:
                    one_pass(i, True)
            one_pass(PASSES - 1, False)

        @block.scalar
        def _(act):
            def copy(out, in_):
                return nc.scalar.activation(out, in_, ACT.Copy)

            def dense(i, base, GTt, Gdr, smp):
                for t in range(TILES):
                    act.wait_ge(GTt.sem, GTt.at(i, base + t + 1))
                    if t >= 2:
                        act.wait_ge(smp.sem, smp.at(i, base + t - 1))
                    else:
                        act.wait_ge(smp.sem, smp.at(i, base))
                    copy(Gd[t % 2][:].rearrange("p q c -> p (q c)"),
                         psT[:].rearrange("p b c -> p (b c)")).then_inc(Gdr.sem, 1)

            def wide_windows(whole):
                return bass.AP(whole.tensor, whole.offset, [whole.ap[0], [SW, STRIPS], [PW, PW], [1, BC]])

            def normalise(i, n):
                s = n % 2
                g = norm(n)
                act.wait_ge(affine_ready.sem, affine_ready.at(i, n + 1))
                src = (xin if n < 2 else x)[s]
                nc.scalar.activation(inner(xn[s]), src[:].rearrange("p (r c) -> p r c", c=W), ACT.Identity,
                                     bias=g[:, 20:21], scale=g[:, 19:20]).then_inc(xn_ready.sem, 1)

            def parts(i, n):
                s = n % 2
                act.wait_ge(parts_product.sem, parts_product.at(i, n + 1))
                for b in range(2):
                    last = copy(off_parts[s].rearrange("p (j b r c) -> p j b r c", b=2, j=STRIPS, c=SW)[:, :, b],
                                (psO[s] if n >= 2 else psT)[:, b, :].rearrange("p (r j c) -> p j r c", j=STRIPS, c=SW))
                last.then_inc(parts_ready.sem, 1)

            def start_normalise(j, first):
                for s in range(2):
                    normalise(j, block0_norm(s, first))

            def start_parts(j, s):
                act.wait_ge(xn_ready.sem, xn_ready.at(j, s + 1))
                copy(strip12[s][:], wide_windows(xn[s][:])).then_inc(wide_ready.sem, 1)
                parts(j, s)

            def start_masks(j):
                for s in range(2):
                    act.wait_ge(om_ready.sem, om_ready.at(j, s + 1))
                    nc.scalar.activation(mk[s][:, 0:TILES], om0[s][:, 2, :], ACT.Sigmoid).then_inc(mask_ready.sem, 1)

            def one_pass(i, more):
                for s in range(2):
                    wait_apart(act, (far_ready, far_ready.at(i, s + 1)))
                    far = act.value_load(flag[s][0:1, 0:1])
                    with act.If(far > 0):
                        act.wait_ge(xT_product.sem, xT_product.at(i, s + 1))
                        copy(xT[s][:].rearrange("p q c -> p (q c)"), psT[:].rearrange("p b c -> p (b c)"))\
                            .then_inc(xT_ready.sem, 1)
                        dense(i, TILES * s, GTt_ready, Gd_ready, sampled)
                        act.wait_ge(sampled.sem, sampled.at(i, TILES * (s + 1)))
                        act.wait_ge(Gd_ready.sem, Gd_ready.at(i, TILES * (s + 1)))
                        act.sem_inc(n_G.sem, TILES)
                    with act.Else():
                        for n in range(TILES):
                            o = first_step(0, s) + n
                            act.wait_ge(n_Gp.sem, n_Gp.at(i, o + 1))
                            if o >= 2:
                                act.wait_ge(n_smp.sem, n_smp.at(i, o - 1))
                            copy(G1[n % 2][:, 0:2, :].rearrange("p u c -> p (u c)"), psT[0:BLK, 0, 0:2 * C])\
                                .then_inc(n_G.sem, 1)
                        act.wait_ge(n_smp.sem, n_smp.at(i, first_step(0, s) + TILES))
                        act.wait_ge(n_G.sem, n_G.at(i, first_step(0, s) + TILES))
                        act.sem_inc(xT_ready.sem, 1)
                        act.sem_inc(Gd_ready.sem, TILES)
                    for b in range(2):
                        last = copy(tiled(inner(img[s]), b), psO[s][:, b, :].rearrange("p (j r c) -> p j r c", j=2, c=SW))
                    last.then_inc(img_ready.sem, 1)
                normalise(i, 2)
                for s in range(2):
                    parts(i, 2 + s)
                    act.wait_ge(pooled_ready.sem, pooled_ready.at(i, s + 1))
                    copy(strip12[s][:], wide_windows(img[s][:])).then_inc(wide_ready.sem, 1)
                    if s == 0:
                        normalise(i, 3)
                    act.wait_ge(om_ready.sem, om_ready.at(i, 3 + s))
                    nc.scalar.activation(mk[s][:], om[s][:, 2, :, :].rearrange("p t k -> p (t k)"), ACT.Sigmoid)\
                        .then_inc(mask_ready.sem, 1)
                    wait_apart(act, (far_ready, far_ready.at(i, s + 3)))
                    far = act.value_load(flag[s][0:1, 0:1])
                    with act.If(far > 0):
                        act.wait_ge(g_xTp.sem, g_xTp.at(i, s + 1))
                        copy(xT[s][:].rearrange("p q c -> p (q c)"), psT[:].rearrange("p b c -> p (b c)"))\
                            .then_inc(g_xT.sem, 1)
                        with act.Fori(0, K9) as k:
                            dense(i, K9 * TILES * s + k * TILES, g_GTt, g_Gd, g_smp)
                            act.wait_ge(g_smp.sem, g_smp.at(i, K9 * TILES * s + k * TILES + TILES))
                            tap = samp[:, bass.ds(k, 1), :].rearrange("p k (r c) -> p (k r) c", c=W)
                            for b in range(2):
                                last = copy(tiled(tap, b), psO[1][:, b, :].rearrange("p (j r c) -> p j r c", j=2, c=SW))
                            last.then_inc(g_smp_sb.sem, 1)
                        act.wait_ge(g_smp_sb.sem, g_smp_sb.at(i, K9 * (s + 1)))
                        act.sem_inc(n_G.sem, STEPS)
                        act.sem_inc(n_smp_sb.sem, STEPS)
                    with act.Else():
                        for n in range(STEPS + 1):
                            if n < STEPS:
                                o = first_step(1, s) + n
                                act.wait_ge(n_Gp.sem, n_Gp.at(i, o + 1))
                                if o >= 2:
                                    act.wait_ge(n_smp.sem, n_smp.at(i, o - 1))
                                copy(G1[n % 2][:].rearrange("p k c -> p (k c)"), psT[0:BLK, 0, 0:3 * C])\
                                    .then_inc(n_G.sem, 1)
                            if n:
                                p = n - 1
                                t, ki = p // 3, p % 3
                                act.wait_ge(n_smp.sem, n_smp.at(i, first_step(1, s) + p + 1))
                                r0, c0 = 16 * (t % 2), SW * (t // 2)
                                copy(samp[:, 3 * ki:3 * ki + 3, :].rearrange("p k (r c) -> p k r c", c=W)
                                     [:, :, r0:r0 + 16, c0:c0 + SW],
                                     psO[1][:, p % 2, 0:3 * C].rearrange("p (k r c) -> p k r c", k=3, c=SW))\
                                    .then_inc(n_smp_sb.sem, 1)
                        act.wait_ge(n_smp_sb.sem, n_smp_sb.at(i, STEPS * (s + 1)))
                        act.sem_inc(g_xT.sem, 1)
                        act.sem_inc(g_Gd.sem, K9 * TILES)
                        act.sem_inc(g_smp_sb.sem, K9)
                for n in (4, 5, block3_norm(0, more), block3_norm(1, more)):
                    normalise(i, n)
                for h in range(2):
                    act.wait_ge(l3_product.sem, l3_product.at(i, P_X2 + h))
                    nc.scalar.activation(x2p[:, 16 * h:16 * h + 16, LPAD:LPAD + W],
                                         bank(P_X2 + h).rearrange("p (r c) -> p r c", c=W),
                                         ACT.Identity, bias=vec[:, V_BIN2:V_BIN2 + 1]).then_inc(l3_act.sem, 1)
                for h in range(2):
                    act.wait_ge(l3_product.sem, l3_product.at(i, P_U + h))
                    nc.scalar.activation(u3[0:C2, HALF * h:HALF * h + HALF], bank(P_U + h)[0:C2], ACT.Relu,
                                         bias=bu[:]).then_inc(l3_act.sem, 1)
                for h in range(2):
                    act.wait_ge(l3_product.sem, l3_product.at(i, P_XC + h))
                    nc.scalar.activation(xc[:, HALF * h:HALF * h + HALF], bank(P_XC + h), ACT.Identity,
                                         bias=vec[:, V_BCB2:V_BCB2 + 1]).then_inc(l3_act.sem, 1)
                for h in range(2):
                    act.wait_ge(l3_product.sem, l3_product.at(i, P_MEAN + h))
                    copy(xm[:, HALF * h:HALF * h + HALF], bank(P_MEAN + h)).then_inc(l3_act.sem, 1)
                if more:
                    start_normalise(i + 1, False)
                for v in range(2):
                    for h in range(2):
                        for t in range(TAPS):
                            m = P_KERN + TAPS * (2 * v + h) + t
                            act.wait_ge(l3_product.sem, l3_product.at(i, m))
                            b = (V_KHB, V_KVB)[v] + t
                            nc.scalar.activation(kern[:, t, HALF * h:HALF * h + HALF], bank(m), ACT.Tanh,
                                                 bias=vec[:, b:b + 1]).then_inc(l3_act.sem, 1)
                        if more and v == 0:
                            start_parts(i + 1, h)
                if more:
                    start_masks(i + 1)
                for h in range(2):
                    act.wait_ge(l3_product.sem, l3_product.at(i, P_GATE + h))
                    nc.scalar.activation(sg[:, HALF * h:HALF * h + HALF], bank(P_GATE + h), ACT.Sigmoid)\
                        .then_inc(l3_act.sem, 1)
                act.wait_ge(l3_csum.sem, l3_csum.at(i, 1))
                nc.scalar.activation(st3[:, 2:3], st3[:, 1:2], ACT.Sigmoid, scale=1.0 / N).then_inc(l3_csig.sem, 1)

            act.wait_ge(borders_zero, 8)
            start_normalise(0, True)
            start_parts(0, 0)
            start_parts(0, 1)
            start_masks(0)
            if PASSES > 1:
                with act.Fori(0, PASSES - 1) as i:
                    one_pass(i, True)
            one_pass(PASSES - 1, False)

        @block.vector
        def _(dve):
            v_ = nc.vector
            dve.wait_ge(early_landed, EARLY * 16)

            def weights():
                for k in range(K9):
                    v_.tensor_scalar(w0[:, k, :], pwT[:], vec[:, V_DW0 + k:V_DW0 + k + 1], None, ALU.mult)
                dve.wait_ge(w2_landed, 32)
                n2 = K9 * C
                f2 = w2[:].rearrange("p k o -> p (k o)")
                flat = samp[:].rearrange("p a b -> p (a b)")
                r2, sgn, t2, neg = (flat[:, n * n2:(n + 1) * n2] for n in range(4))
                v_.tensor_scalar(sgn, f2, 0.0, None, ALU.is_gt)
                v_.tensor_scalar(neg, f2, 0.0, None, ALU.is_lt)
                v_.tensor_scalar(t2, r2, 0.5, 0.7, ALU.is_gt, ALU.mult).then_inc(prep_dve, 1)
                dve.wait_ge(prep_dve, 1)
                v_.tensor_tensor(sgn, sgn, neg, ALU.subtract)
                v_.tensor_scalar(r2, r2, 0.5, 0.175, ALU.is_lt, ALU.mult).then_inc(prep_dve, 1)
                dve.wait_ge(prep_dve, 2)
                v_.tensor_tensor(t2, t2, r2, ALU.add).then_inc(prep_dve, 1)
                dve.wait_ge(prep_dve, 3)
                v_.tensor_tensor(t2, t2, sgn, ALU.mult).then_inc(prep_dve, 1)
                dve.wait_ge(prep_dve, 4)
                v_.scalar_tensor_tensor(f2, f2, 0.5, t2, ALU.mult, ALU.add).then_inc(weights_ready, 1)

            def stats(own, n, src):
                g = norm(n)
                for h in range(2):
                    own.step(v_.bn_stats(g[:, 6 * h:6 * h + 6], src[:, HALF * h:HALF * h + HALF]))
                wait_apart(dve, (own.steps, own.steps.at(own.i, own.n)))
                own.step(v_.bn_aggr(g[:, 12:14], g[:, 0:12]))
                own.settle()
                v_.scalar_tensor_tensor(g[:, 13:14], g[:, 12:13], g[:, 12:13], g[:, 13:14], ALU.mult, ALU.add)\
                    .then_inc(stats_ready.sem, 1)

            def affine(own, n):
                g = norm(n)
                dve.wait_ge(group_ready.sem, group_ready.at(own.i, n + 1))
                own.step(v_.tensor_copy(g[:, 14:16], ps[n % 2][:, 0:2]))
                own.settle()
                own.step(v_.scalar_tensor_tensor(g[:, 16:17], g[:, 14:15], g[:, 14:15], g[:, 15:16],
                                                 ALU.mult, ALU.subtract))
                own.settle()
                v_.tensor_scalar(g[:, 17:18], g[:, 16:17], -1.0, EPS, ALU.mult, ALU.add)\
                    .then_inc(var_ready.sem, 1)
                dve.wait_ge(rstd_ready.sem, rstd_ready.at(own.i, n + 1))
                own.step(v_.tensor_scalar(g[:, 19:20], g[:, 18:19], 1.0 / 9 if n // 2 == 1 else 1.0, None, ALU.mult))
                own.settle()
                v_.tensor_scalar(g[:, 20:21], g[:, 14:15], g[:, 19:20], -1.0, ALU.mult, ALU.mult)\
                    .then_inc(affine_ready.sem, 1)

            def hats_dense(s, settle, step, uv, mask, gain):
                h = hat[s]
                step(v_.tensor_tensor(h[:], iota32.unsqueeze(1).broadcast_to((C, 2 * TILES, 32)),
                                      uv.broadcast_to((C, 2 * TILES, 32)), ALU.subtract))
                settle()
                step(v_.scalar_tensor_tensor(h[:], h[:], -1.0, h[:], ALU.mult, ALU.max))
                settle()
                step(v_.tensor_scalar(h[:], h[:], 1.0, 0.0, ALU.subtract, ALU.min))
                settle()
                step(v_.scalar_tensor_tensor(h[:, TILES:], h[:, TILES:], gain, mask.broadcast_to((C, TILES, 32)),
                                             ALU.mult, ALU.mult))
                settle()

            def dense(i_, base, s, GTr, GTt):
                for t in range(TILES):
                    dve.wait_ge(GTt.sem, GTt.at(i_, base + (t - 1 if t >= 2 else 0)))
                    v_.tensor_tensor(GT[t % 2].rearrange("p (j a b) -> p j a b", j=STRIPS, b=SW),
                                     hat[s][:, t, :].unsqueeze(1).unsqueeze(3).broadcast_to((C, STRIPS, H, SW)),
                                     hat[s][:, TILES + t, :].rearrange("p (j b) -> p j b", b=SW).unsqueeze(2)
                                     .broadcast_to((C, STRIPS, H, SW)), ALU.mult).then_inc(GTr.sem, 1)

            def far_flag(own, s, offsets, reach):
                own.step(v_.tensor_reduce(out=flagf[s][:, 1:2], in_=offsets,
                                          op=ALU.max, axis=AX.X, apply_absolute_value=True))
                own.settle()
                v_.tensor_scalar(flagf[s][:, 0:1], flagf[s][:, 1:2], reach, None, ALU.is_gt)\
                    .then_inc(far_input.sem, 1)

            def load_flag(i, n):
                dve.wait_ge(far_count.sem, far_count.at(i, n + 1))
                v_.tensor_copy(flag[n % 2][:], ps[n % 2][:, 2:3]).then_inc(far_ready.sem, 1)

            def block_copy(i, o, b):
                dve.wait_ge(n_blkp.sem, n_blkp.at(i, o + 1))
                if o >= 2:
                    dve.wait_ge(n_smp.sem, n_smp.at(i, o - 1))
                v_.tensor_copy(xblk[b][:].rearrange("p h c -> p (h c)"), psT[0:BLK, 1, 0:2 * C])\
                    .then_inc(n_blk.sem, 1)

            def tile_order(s, src):
                return v_.tensor_copy(q_strips[s][:].rearrange("p (j r c) -> p j r c", j=STRIPS, c=SW),
                                      inner(src).rearrange("p r (j c) -> p j r c", c=SW))

            def start_stats(own, first):
                for s in range(2):
                    dve.wait_ge(x_landed[s].sem, x_landed[s].at(own.i, 16))
                    stats(own, block0_norm(s, first), xin[s])

            def start_affine(own, first):
                for s in range(2):
                    affine(own, block0_norm(s, first))

            def start_offsets(own):
                for s in range(2):
                    dve.wait_ge(offs_ready.sem, offs_ready.at(own.i, s + 1))
                    v_.tensor_tensor(om0[s][:].rearrange("p g t -> p t g"),
                                     ps[s][:, 4:4 + 3 * TILES].rearrange("p (t g) -> p t g", g=3),
                                     offb[:, 27:30].unsqueeze(1).broadcast_to((C, TILES, 3)), ALU.add)\
                        .then_inc(om_ready.sem, 1)
                    dve.wait_ge(om_ready.sem, om_ready.at(own.i, s + 1))
                    far_flag(own, s, om0[s][:, 0:2, :].rearrange("p g t -> p (g t)"), NEAR0)

            def start_hats(own, s):
                o2 = om0[s][:, 0:2, :].rearrange("p g t -> p (g t)")
                load_flag(own.i, s)
                own.step(v_.tensor_scalar(flagf[s][:, 1:2], ps[s][:, 2:3], 0.5, None, ALU.is_lt))
                own.step(v_.scalar_tensor_tensor(o2, o2, 2.0 / W, tab[:, T_LIN:T_LIN + 2 * TILES], ALU.mult, ALU.add))
                own.settle()
                own.step(v_.tensor_scalar(o2, o2, 1.0, 0.5 * (W - 1), ALU.add, ALU.mult))
                own.settle()
                own.step(v_.scalar_tensor_tensor(o2, tab[:, T_ORG:T_ORG + 2 * TILES], flagf[s][:, 1:2], o2,
                                                 ALU.mult, ALU.add))
                own.settle()
                dve.wait_ge(mask_ready.sem, mask_ready.at(own.i, s + 1))
                hats_dense(s, own.settle, own.step, o2.unsqueeze(2), mk[s][:, 0:TILES].unsqueeze(2), 1.0)

            def one_pass(i, more):
                own = Own(dve, dve_own, i)
                nxt = Own(dve, start_own, i + 1)

                def pool3(s, part):
                    if part == 0:
                        dve.wait_ge(xn_ready.sem, xn_ready.at(i, 3 + s))
                    else:
                        own.settle()
                    a, b, o = xn[s], pool_v, inner(img[s])
                    cols = slice(PAD - 1, PAD + W + 1)
                    if part == 0:
                        own.step(v_.tensor_tensor(b[:], a[:, PAD - 1:PAD - 1 + H, cols], a[:, PAD:PAD + H, cols], ALU.add))
                    elif part == 1:
                        own.step(v_.tensor_tensor(b[:], b[:], a[:, PAD + 1:PAD + 1 + H, cols], ALU.add))
                    elif part == 2:
                        own.step(v_.tensor_tensor(o, b[:, :, 0:W], b[:, :, 1:W + 1], ALU.add))
                    else:
                        v_.tensor_tensor(o, o, b[:, :, 2:W + 2], ALU.add).then_inc(pooled_ready.sem, 1)

                for s in range(2):
                    wait_apart(dve, (far_ready, far_ready.at(i, s + 1)))
                    far = dve.value_load(flag[s][0:1, 0:1])
                    with dve.If(far > 0):
                        dve.wait_ge(xn_ready.sem, xn_ready.at(i, s + 1))
                        tile_order(s, xn[s]).then_inc(strips_ready.sem, 1)
                        dense(i, TILES * s, s, GT_ready, GTt_ready)
                        dve.wait_ge(GTt_ready.sem, GTt_ready.at(i, TILES * (s + 1)))
                        dve.sem_inc(n_GT.sem, TILES)
                        dve.sem_inc(n_blk.sem, TILES)
                    with dve.Else():
                        for n in range(TILES + 1):
                            if n < TILES:
                                o = first_step(0, s) + n
                                if o >= 2:
                                    dve.wait_ge(n_Gp.sem, n_Gp.at(i, o - 1))
                                v_.tensor_tensor(GT1[n % 2][:, 0:2, :].rearrange("p u q -> p (u q)")
                                                 .rearrange("p (a b) -> p a b", b=BC),
                                                 hat[s][:, n, 0:2 * BR].unsqueeze(2).broadcast_to((C, 2 * BR, BC)),
                                                 hat[s][:, TILES + n, 0:BC].unsqueeze(1).broadcast_to((C, 2 * BR, BC)),
                                                 ALU.mult).then_inc(n_GT.sem, 1)
                            if n:
                                block_copy(i, first_step(0, s) + n - 1, (n - 1) % 2)
                        dve.wait_ge(n_blk.sem, n_blk.at(i, first_step(0, s) + TILES))
                        dve.sem_inc(strips_ready.sem, 1)
                        dve.sem_inc(GT_ready.sem, TILES)
                for s in range(2):
                    dve.wait_ge(conv_ready.sem, conv_ready.at(i, s + 1))
                    v_.tensor_tensor(x[s][:], psO[s][:].rearrange("p b c -> p (b c)"), xin[s][:], ALU.add)\
                        .then_inc(added.sem, 1)
                    dve.wait_ge(added.sem, added.at(i, s + 1))
                    stats(own, 2 + s, x[s])
                    affine(own, 2 + s)
                    if s == 0:
                        for part in range(4):
                            pool3(0, part)
                for s in range(2):
                    dve.wait_ge(offs_ready.sem, offs_ready.at(i, 3 + s))
                    v_.tensor_tensor(om[s][:].rearrange("p g t k -> p t g k"),
                                     ps[s][:, 4:4 + 27 * TILES].rearrange("p (t g k) -> p t g k", g=3, k=K9),
                                     offb[:, 0:27].rearrange("p (g k) -> p g k", k=K9).unsqueeze(1)
                                     .broadcast_to((C, TILES, 3, K9)), ALU.add).then_inc(om_ready.sem, 1)
                    dve.wait_ge(om_ready.sem, om_ready.at(i, 3 + s))
                    far_flag(own, s, om[s][:, 0:2].rearrange("p g t k -> p (g t k)"), NEAR)
                    load_flag(i, 2 + s)
                    own_before = own.n
                    wait_apart(dve, (far_ready, far_ready.at(i, s + 3)), (mask_ready, mask_ready.at(i, 3 + s)))
                    far = dve.value_load(flag[s][0:1, 0:1])
                    with dve.If(far > 0):
                        count = [0]
                        tap = [None]

                        def gstep(ins):
                            ins.then_inc(g_own.sem, 1)
                            count[0] += 1

                        def gsettle():
                            v = g_own.at(i, G_OWN * s + count[0])
                            dve.wait_ge(g_own.sem, v if tap[0] is None else v + tap[0] * 4)

                        if s == 0:
                            for part in range(4):
                                pool3(1, part)
                        tile_order(s, img[s]).then_inc(g_strips.sem, 1)
                        o2 = om[s][:, 0:2].rearrange("p g t k -> p (g t k)")
                        gstep(v_.tensor_tensor(o2, o2, tab[:, T_POS:T_POS + 2 * TILES * K9], ALU.add))
                        wait_apart(dve, (g_own, g_own.at(i, G_OWN * s + count[0])))
                        with dve.Fori(0, K9) as k:
                            tap[0] = k
                            dve.wait_ge(g_GTt.sem, g_GTt.at(i, K9 * TILES * s + k * TILES))
                            uv = om[s][:, 0:2].rearrange("p g t k -> p (g t) k")[:, :, bass.ds(k, 1)]
                            m = mk[s][:].rearrange("p (t k) -> p t k", k=K9)[:, :, bass.ds(k, 1)]
                            hats_dense(s, gsettle, gstep, uv, m, 2.0)
                            dense(i, K9 * TILES * s + k * TILES, s, g_GT, g_GTt)
                        assert count[0] == 5
                        dve.wait_ge(g_GTt.sem, g_GTt.at(i, K9 * TILES * (s + 1)))
                        dve.sem_inc(n_own.sem, N_OWN)
                        dve.sem_inc(n_GT.sem, STEPS)
                        dve.sem_inc(n_blk.sem, STEPS)
                    own.n = own_before
                    with dve.Else():
                        cnt = [0]

                        def nstep(ins):
                            ins.then_inc(n_own.sem, 1)
                            cnt[0] += 1

                        def nsettle():
                            dve.wait_ge(n_own.sem, n_own.at(i, N_OWN * s + cnt[0]))

                        TK = TILES * K9
                        dyx = om[s][:].rearrange("p g t k -> p g (t k)")
                        nstep(v_.tensor_tensor(hfy[s][:], tab[:, T_EY:T_EY + BR].unsqueeze(1).broadcast_to((C, TK, BR)),
                                               dyx[:, 0, :].unsqueeze(2).broadcast_to((C, TK, BR)), ALU.subtract))
                        nstep(v_.tensor_tensor(
                            hfx[s][:].rearrange("p (t k) b -> p t k b", k=K9),
                            tab[:, T_EX:T_EX + K9 * BC].rearrange("p (k b) -> p k b", b=BC).unsqueeze(1)
                            .broadcast_to((C, TILES, K9, BC)),
                            om[s][:, 1].unsqueeze(3).broadcast_to((C, TILES, K9, BC)), ALU.subtract))
                        nsettle()
                        for hf in (hfy[s], hfx[s]):
                            nstep(v_.scalar_tensor_tensor(hf[:], hf[:], -1.0, hf[:], ALU.mult, ALU.max))
                        nsettle()
                        for hf in (hfy[s], hfx[s]):
                            nstep(v_.tensor_scalar(hf[:], hf[:], 1.0, 0.0, ALU.subtract, ALU.min))
                        nsettle()
                        nstep(v_.scalar_tensor_tensor(hfx[s][:], hfx[s][:], 2.0,
                                                      mk[s][:].unsqueeze(2).broadcast_to((C, TK, BC)),
                                                      ALU.mult, ALU.mult))
                        nsettle()
                        assert cnt[0] == N_OWN
                        hy = hfy[s][:].rearrange("p (t k) a -> p t k a", k=K9)
                        hx = hfx[s][:].rearrange("p (t k) b -> p t k b", k=K9)
                        for n in range(STEPS + 1):
                            if n < STEPS:
                                t, ki = n // 3, n % 3
                                o = first_step(1, s) + n
                                if o >= 2:
                                    dve.wait_ge(n_Gp.sem, n_Gp.at(i, o - 1))
                                three = slice(3 * ki, 3 * ki + 3)
                                v_.tensor_tensor(GT1[n % 2][:].rearrange("p k (a b) -> p k a b", b=BC),
                                                 hy[:, t, three, :].unsqueeze(3).broadcast_to((C, 3, BR, BC)),
                                                 hx[:, t, three, :].unsqueeze(2).broadcast_to((C, 3, BR, BC)),
                                                 ALU.mult).then_inc(n_GT.sem, 1)
                            if n:
                                block_copy(i, first_step(1, s) + n - 1, (n - 1) % 2)
                            if s == 0 and n in POOL_AT:
                                pool3(1, POOL_AT.index(n))
                        dve.wait_ge(n_blk.sem, n_blk.at(i, first_step(1, s) + STEPS))
                        dve.sem_inc(g_strips.sem, 1)
                        dve.sem_inc(g_own.sem, G_OWN)
                        dve.sem_inc(g_GT.sem, K9 * TILES)
                for s in range(2):
                    dve.wait_ge(conv_ready.sem, conv_ready.at(i, 3 + s))
                    v_.scalar_tensor_tensor(x[s][:], psO[0][:].rearrange("p b c -> p (b c)"),
                                            vec[:, V_B1:V_B1 + 1], x[s][:], ALU.add, ALU.add).then_inc(added.sem, 1)
                    dve.wait_ge(added.sem, added.at(i, 3 + s))
                    stats(own, 4 + s, x[s])
                    affine(own, 4 + s)
                if more:
                    start_stats(nxt, False)
                    start_affine(nxt, False)
                for s in range(2):
                    dve.wait_ge(conv_ready.sem, conv_ready.at(i, 5 + s))
                    v_.scalar_tensor_tensor(x[s][:], psO[1 - s][:].rearrange("p b c -> p (b c)"),
                                            vec[:, V_B2:V_B2 + 1], x[s][:], ALU.add, ALU.add).then_inc(added.sem, 1)
                    dve.wait_ge(added.sem, added.at(i, 5 + s))
                    stats(own, block3_norm(s, more), x[s])
                    affine(own, block3_norm(s, more))
                def rows3(t, h):
                    return t[:, HALF * h:HALF * h + HALF].rearrange("p (r c) -> p r c", c=W)

                for v in range(2):
                    src = (x2p, ahp)[v]
                    w_at = (V_DWH, V_DWV)[v]
                    b_at = (V_DWHB, V_DWVB)[v]

                    def shifted(t, d, h, v=v):
                        return t[:, 16 * h:16 * h + 16, d:d + W] if v == 0 else t[:, 16 * h + d:16 * h + d + 16, :]

                    done = [own.n, own.n]
                    for h, d in [(h, n - 3 * h) for n in range(10) for h in range(2) if 0 <= n - 3 * h < 7]:
                        if d == 0 and v == 0:
                            dve.wait_ge(l3_act.sem, l3_act.at(i, P_X2 + h))
                        elif d == 0:
                            dve.wait_ge(l3_product.sem, l3_product.at(i, P_KERN + TAPS * (h + 1) - 1))
                        if d == 0:
                            own.step(v_.tensor_scalar(rows3(dwo, h), shifted(src, 0, h), vec[:, w_at:w_at + 1],
                                                      vec[:, b_at:b_at + 1], ALU.mult, ALU.add))
                            done[h] = own.n
                            continue
                        own.finished(done[h])
                        ins = v_.scalar_tensor_tensor(rows3(dwo, h), shifted(src, d, h), vec[:, w_at + d:w_at + d + 1],
                                                      rows3(dwo, h), ALU.mult, ALU.add)
                        if d < 6:
                            own.step(ins)
                            done[h] = own.n
                        else:
                            ins.then_inc(l3_dw.sem, 1)
                    if more and v == 1:
                        start_offsets(nxt)
                    for h in range(2):
                        if v == 0:
                            pair = psum2[:, 0:16 * (LW - 1)].rearrange("p (r c) -> p r c", c=LW - 1)
                            rows = src[:, 16 * h:16 * h + 16, :]
                            own.step(v_.tensor_tensor(pair, rows[:, :, 0:LW - 1], rows[:, :, 1:LW], ALU.add))
                            outer = pair[:, :, 0:W], pair[:, :, 5:5 + W]
                            out = ahp[:, LPAD + 16 * h:LPAD + 16 * h + 16, :]
                        else:
                            pair = psum2[:, 0:21 * W].rearrange("p (r c) -> p r c", c=W)
                            own.step(v_.tensor_tensor(pair, src[:, 16 * h:16 * h + 21, :],
                                                      src[:, 16 * h + 1:16 * h + 22, :], ALU.add))
                            outer = pair[:, 0:16, :], pair[:, 5:21, :]
                            out = rows3(at, h)
                        taps = [outer[0]] + [shifted(src, d, h) for d in (2, 3, 4)] + [outer[1]]
                        terms = [out, rows3(tmp3, 0), rows3(tmp3, 1), rows3(sm, 0), rows3(sm, 1)]
                        done = {}

                        def term(t):
                            if t in (0, 4):
                                own.finished(pair_done)
                            dve.wait_ge(l3_act.sem, l3_act.at(i, P_KERN + TAPS * (2 * v + h) + t))
                            own.step(v_.scalar_tensor_tensor(terms[t], taps[t], 0.5 if t in (0, 4) else 1.0,
                                                             rows3(kern[:, t, :], h), ALU.mult, ALU.mult))
                            done[t] = own.n

                        def add(t):
                            own.finished(max(done["sum"] if t > 1 else done[0], done[t]))
                            if t == 4 and v == 1:
                                own.step(v_.scalar_tensor_tensor(out, out, 1.0, terms[t], ALU.mult, ALU.add,
                                                                 accum_out=st3[:, 3 * h:3 * h + 1]))
                            else:
                                own.step(v_.tensor_tensor(out, out, terms[t], ALU.add))
                            done["sum"] = own.n

                        pair_done = own.n
                        for what, t in ((term, 1), (term, 0), (term, 2), (add, 1), (term, 3), (add, 2), (term, 4),
                                        (add, 3), (add, 4)):
                            what(t)
                        own.settle()
                own.step(v_.tensor_tensor(st3[:, 4:5], st3[:, 0:1], st3[:, 3:4], ALU.add))
                own.settle()
                v_.tensor_scalar(wss, blk64, st3[:, 4:5], 1.0 / N, ALU.mult, ALU.mult).then_inc(l3_wss.sem, 1)
                dve.wait_ge(l3_act.sem, l3_act.at(i, P_MEAN + 1))
                v_.scalar_tensor_tensor(tmp3, at[:], 1.0, xm[:], ALU.mult, ALU.mult, accum_out=st3[:, 1:2])\
                    .then_inc(l3_csum.sem, 1)
                if more:
                    start_hats(nxt, 0)
                dve.wait_ge(l3_act.sem, l3_act.at(i, P_GATE + 1))
                v_.tensor_tensor(sm, sg, xc[:], ALU.mult).then_inc(l3_maps.sem, 1)
                dve.wait_ge(l3_csig.sem, l3_csig.at(i, 1))
                v_.tensor_scalar(wo2, woT[:, :, 1, :], st3[:, 2:3], None, ALU.mult).then_inc(l3_maps.sem, 1)
                if more:
                    start_hats(nxt, 1)
                for s in range(2):
                    dve.wait_ge(l3_product.sem, l3_product.at(i, P_OUT + s))
                    dve.wait_ge(yout_free.sem, yout_free.at(i, 0))
                    v_.scalar_tensor_tensor(yout[s][:], psO[s][:].rearrange("p b c -> p (b c)"),
                                            vec[:, V_BOUT:V_BOUT + 1], x[s][:], ALU.add, ALU.add)\
                        .then_inc(y_ready.sem, 1)
                assert own.n == DVE_STEPS and nxt.n == (START_STEPS if more else 0), (own.n, nxt.n)

            first = Own(dve, start_own, 0)
            start_stats(first, True)
            start_affine(first, True)
            weights()
            start_offsets(first)
            for s in range(2):
                start_hats(first, s)
            dve.wait_ge(prep, 2)
            v_.tensor_copy(wu[:], psT[:, 0, 0:C2])
            v_.tensor_tensor(bu[:], psT[0:C2, 1, 0:1], vec[0:C2, V_BCB1:V_BCB1 + 1], ALU.add).then_inc(weights_ready, 1)
            dve.wait_ge(weights_ready, 2)
            dve.wait_ge(borders_zero, 8)
            assert first.n == START_STEPS, first.n
            if PASSES > 1:
                with dve.Fori(0, PASSES - 1) as i:
                    one_pass(i, True)
            one_pass(PASSES - 1, False)


def tables():
    import numpy as np

    tab = np.zeros((C, TAB_N), np.float32)
    p = np.arange(C)
    row, col = p // SW, p % SW
    t = np.arange(TILES)
    y = 16 * (t % 2)[None, :] + row[:, None]
    x = SW * (t // 2)[None, :] + col[:, None]
    k = np.arange(K9)
    tab[:, T_IOTA:T_IOTA + 32] = np.arange(32)
    tab[:, T_GAVG:T_GAVG + C] = (p[:, None] // GROUP == p[None, :] // GROUP) / GROUP
    tab[:, T_ONES:T_ONES + C] = 1
    tab[:, T_BLK:T_BLK + C] = (p[:, None] // C2 == p[None, :] // C2) / C2
    line = np.linspace(-1, 1, W, dtype=np.float32)
    tab[:, T_LIN:T_LIN + 2 * TILES] = np.concatenate([line[y], line[x]], 1)
    pos = np.stack([y[:, :, None] + k // 3 - 1, x[:, :, None] + k % 3 - 1], 1)
    tab[:, T_POS:T_POS + 2 * TILES * K9] = pos.reshape(C, -1)
    tab[:, T_EY:T_EY + BR] = np.arange(BR)[None, :] - (row % 8)[:, None] - 1
    ex = np.arange(BC)[None, None, :] - col[:, None, None] - (k % 3)[None, :, None] - 1
    tab[:, T_EX:T_EX + K9 * BC] = ex.reshape(C, -1)
    tab[:, T_SEL:T_SEL + 32] = p[:, None] % 32 == np.arange(32)
    origin = np.concatenate([16 * (t % 2) - PAD, SW * (t // 2) - PAD])
    tab[:, T_ORG:T_ORG + 2 * TILES] = -origin[None, :]
    return tab


def layout(a):
    import numpy as np

    wide = lambda w: np.concatenate([w, np.zeros((32 - len(w),) + w.shape[1:], w.dtype)])
    both = lambda v: np.concatenate([v, v])
    taps = lambda w: np.ascontiguousarray(w.transpose(1, 2, 3, 0).reshape(w.shape[1], K9, w.shape[0]))

    def diagonal(w):
        z = np.zeros((2, w.shape[0], 2, w.shape[1]), np.float32)
        z[0, :, 0] = w
        z[1, :, 1] = w
        return z.reshape(2 * w.shape[0], 2 * w.shape[1])

    def output_weights(w):
        z = np.zeros((2, C2, 2, 2, C), np.float32)
        for s in range(2):
            for m in range(2):
                z[s, :, s, m] = w[C2 * m:C2 * m + C2]
        return z.reshape(C, 2, 2, C)

    def strip(w, b):
        heads = np.arange(C2) // (C2 // 8)
        ws = np.stack([diagonal(w[heads * TAPS + t].T) for t in range(TAPS)], 1)
        return np.ascontiguousarray(ws), np.stack([both(b[heads * TAPS + t]) for t in range(TAPS)], 1)

    kh, khb = strip(a["L3_conv_hk_pw_w"], a["L3_conv_hk_pw_b"])
    kv, kvb = strip(a["L3_conv_vk_pw_w"], a["L3_conv_vk_pw_b"])
    bin_ = a["L3_conv_proj_in_b"]
    cb1 = a["L3_conv_cb_b1"]
    vec = np.zeros((C, V_N), np.float32)
    vec[:, V_B1] = a["L1_conv_b"]
    vec[:, V_B2] = a["L2_conv_bias"]
    vec[:, V_BIN1] = both(bin_[:C2])
    vec[:, V_BIN2] = both(bin_[C2:])
    vec[:, V_BCB1] = both(both(cb1))
    vec[:, V_BCB2] = both(a["L3_conv_cb_b2"])
    vec[:, V_BOUT] = a["L3_conv_proj_out_b"]
    vec[:, V_DWHB] = both(a["L3_conv_hk_dw_b"])
    vec[:, V_DWVB] = both(a["L3_conv_vk_dw_b"])
    vec[:, V_DWH:V_DWH + 7] = both(a["L3_conv_hk_dw_w"].reshape(C2, 7))
    vec[:, V_DWV:V_DWV + 7] = both(a["L3_conv_vk_dw_w"].reshape(C2, 7))
    vec[:, V_KHB:V_KHB + TAPS] = khb
    vec[:, V_KVB:V_KVB + TAPS] = kvb
    vec[:, V_DW0:V_DW0 + K9] = a["L0_conv_w_dw"].reshape(C, K9)

    off = np.arange(2 * K9).reshape(K9, 2).T.reshape(-1)
    w1off = np.concatenate([a["L1_conv_off_w"][off], a["L1_conv_mod_w"]])
    b1off = np.concatenate([a["L1_conv_off_b"][off], a["L1_conv_mod_b"], a["L0_conv_b_off"]])
    x = a["x"]
    wo = a["L3_conv_proj_out_w"].T
    return {
        "x": x.reshape(x.shape[0], C, N),
        "ident": np.eye(C, dtype=np.float32),
        "tab": tables(),
        "vec": vec,
        "offb": np.ascontiguousarray(np.broadcast_to(b1off, (C, 30))),
        "w0off": taps(wide(a["L0_conv_w_off"])),
        "pwT": a["L0_conv_w_pw"].reshape(C, C).T,
        "w1off": taps(wide(w1off)),
        "w1": taps(a["L1_conv_w"]),
        "w2": taps(a["L2_conv_weight"]),
        "r2": taps(a["L2_conv_r_matrix"]).reshape(C, K9 * C),
        "win": a["L3_conv_proj_in_w"][:C2],
        "win2T": a["L3_conv_proj_in_w"][C2:].T,
        "cb1T": both(a["L3_conv_cb_w1"]).T,
        "cb2T": np.concatenate([diagonal(a["L3_conv_cb_w2"].T), np.zeros((C2, C), np.float32)]),
        "kh": kh,
        "kv": kv,
        "woT": output_weights(wo),
    }


def kernel(**inputs):
    import numpy as np
    import concourse.bacc as bacc
    from concourse.bass_utils import run_bass_kernel_spmd

    arrays = {k: np.ascontiguousarray(v) for k, v in layout({k: np.asarray(v) for k, v in inputs.items()}).items()}
    nc = bacc.Bacc("TRN2", target_bir_lowering=False, num_devices=1)
    args = [nc.dram_tensor(f"in_{k}", v.shape, mybir.dt.from_np(v.dtype), kind="ExternalInput").ap()
            for k, v in arrays.items()]
    out = nc.dram_tensor("out", arrays["x"].shape, F32, kind="ExternalOutput").ap()
    conv_preact_kernel(nc, *args, out)
    r = run_bass_kernel_spmd(nc, [{f"in_{k}": v for k, v in arrays.items()}], core_ids=[0])
    return r.results[0]["out"].reshape(inputs["x"].shape)
```
